# Optimizing a Trainium2 kernel written in Bass

```python
import numpy as np
import jax
import jax.numpy as jnp

def _softmax(x, axis=-1):
    return jax.nn.softmax(x, axis=axis)

def _gelu(x):
    return jax.nn.gelu(x, approximate=True)

def _silu(x):
    return jax.nn.silu(x)

def _sigmoid(x):
    return jax.nn.sigmoid(x)

def _layernorm(x, axis=-1, eps=1e-05):
    m = jnp.mean(x, axis=axis, keepdims=True)
    v = jnp.var(x, axis=axis, keepdims=True)
    return (x - m) / jnp.sqrt(v + eps)

def _scatter_add(tgt, idx, src, axis=0):
    return tgt.at[idx].add(src)

def _segment_sum(src, seg, n):
    return jax.ops.segment_sum(src, seg, n)
kernel_name = 'mk_vit_tower_postln_d1_tok_img1024_r4_1daa1b'

def setup_inputs(seed: int=0):
    np.random.seed(seed)
    _w = jnp.asarray

    def _rec_inputs():
        import jax
        import jax.numpy as jnp
        _rk = jax.random.key(seed)
        x = -0.00150118 + 0.499729 * jax.random.normal(jax.random.fold_in(_rk, 1), (32, 256, 64, 2), jnp.float32)
        return x
    x = _rec_inputs()

    def _L0_tok_setup():
        import jax, jax.numpy as jnp
        import numpy as np
        import math
        H = 256
        N = 64
        CH = 1
        SEQ_L = 256
        key = jax.random.key(seed)
        k1, k2, k3, k4 = jax.random.split(key, 4)
        log_dt = jax.random.uniform(k1, (H,), dtype=jnp.float32, minval=math.log(0.001), maxval=math.log(0.1))
        inv_A_real = jnp.log(0.5 * jnp.ones((H, N), jnp.float32)) + 0.1 * jax.random.normal(k2, (H, N), dtype=jnp.float32)
        A_imag = jnp.broadcast_to(math.pi * jnp.arange(N, dtype=jnp.float32), (H, N)).copy()
        B_ri = jax.random.normal(k3, (H, N, 2), dtype=jnp.float32) * 0.5
        C_ri = jax.random.normal(k4, (CH, H, N, 2), dtype=jnp.float32) * 0.5
        return {'log_dt': log_dt, 'inv_A_real': inv_A_real, 'A_imag': A_imag, 'B_ri': B_ri, 'C_ri': C_ri, 'L': SEQ_L}
    _L0_tok_all = _L0_tok_setup()
    _L0_tok_in = {k: v for k, v in _L0_tok_all.items() if k in ('log_dt', 'inv_A_real', 'A_imag', 'B_ri')}
    del _L0_tok_all

    def _L0_attn_setup():
        import jax, jax.numpy as jnp
        import numpy as np
        LN_EPS = 1e-05
        WKV_EPS = 1e-08
        NEG_INF = -1e+38

        def _layernorm(x, g, b):
            m = jnp.mean(x, axis=-1, keepdims=True)
            v = jnp.mean(jnp.square(x - m), axis=-1, keepdims=True)
            return (x - m) * jax.lax.rsqrt(v + LN_EPS) * g + b

        def _wkv(w, u, k, v):
            B, T, C = k.shape
            aa0 = jnp.zeros((B, C), k.dtype)
            bb0 = jnp.full((B, C), NEG_INF, k.dtype)

            def step(carry, kv_t):
                aa, bb = carry
                kk, vv = kv_t
                ww = u + kk
                p = jnp.maximum(bb, ww)
                e1 = jnp.exp(bb - p)
                e2 = jnp.exp(ww - p)
                y_t = (e1 * aa + e2 * vv) / (e1 + e2 + WKV_EPS)
                ww = w + bb
                p = jnp.maximum(ww, kk)
                e1 = jnp.exp(ww - p)
                e2 = jnp.exp(kk - p)
                aa = e1 * aa + e2 * vv
                bb = p + jnp.log(e1 + e2 + WKV_EPS)
                return ((aa, bb), y_t)
            (aa, bb), ys = jax.lax.scan(step, (aa0, bb0), (jnp.swapaxes(k, 0, 1), jnp.swapaxes(v, 0, 1)))
            y = jnp.swapaxes(ys, 0, 1)
            new_state = jnp.stack([aa, bb], axis=-1)
            return (y, new_state)

        def _reference_tuple_inner(x, time_decay, time_first, W_tm, g1, b1, tmk, tmv, tmr, W_cm, W_cp, g2, b2, cmk, cmr):
            x_prev = jnp.concatenate([x[:, :1], x[:, :-1]], axis=1)
            kvr = _layernorm(x, g1, b1) @ W_tm
            k, v, r = jnp.split(kvr, 3, axis=-1)
            k = k * tmk + x_prev * (1.0 - tmk)
            v = v * tmv + x_prev * (1.0 - tmv)
            r = jax.nn.sigmoid(r * tmr + x_prev * (1.0 - tmr))
            y, new_state = _wkv(time_decay, time_first, k, v)
            x = x + r * y
            xp = jnp.concatenate([x[:, -1:], x[:, :-1]], axis=1)
            xn = _layernorm(x, g2, b2)
            kk = xn @ W_cm
            cmk4 = jnp.tile(cmk, (1, 1, 4))
            xp4 = jnp.tile(xp, (1, 1, 4))
            kk = kk * cmk4 + xp4 * (1.0 - cmk4)
            rr = jax.nn.sigmoid(xn * cmr + xp * (1.0 - cmr))
            vv = jnp.square(jax.nn.relu(kk)) @ W_cp
            x = x + rr * vv
            return (x, new_state)
        key = jax.random.key(seed)
        ks = jax.random.split(key, 12)
        B, T, C = (8, 512, 256)
        scale = 0.02
        return {'x': jax.random.normal(ks[0], (B, T, C), jnp.float32), 'time_decay': jax.random.uniform(ks[1], (C,), jnp.float32, -1.0, 1.0), 'time_first': jax.random.uniform(ks[2], (C,), jnp.float32, -1.0, 1.0), 'W_tm': jax.random.normal(ks[3], (C, 3 * C), jnp.float32) * scale, 'g1': jnp.ones((C,), jnp.float32), 'b1': jnp.zeros((C,), jnp.float32), 'tmk': jax.random.uniform(ks[4], (1, 1, C), jnp.float32), 'tmv': jax.random.uniform(ks[5], (1, 1, C), jnp.float32), 'tmr': jax.random.uniform(ks[6], (1, 1, C), jnp.float32), 'W_cm': jax.random.normal(ks[7], (C, 4 * C), jnp.float32) * scale, 'W_cp': jax.random.normal(ks[8], (4 * C, C), jnp.float32) * scale, 'g2': jnp.ones((C,), jnp.float32), 'b2': jnp.zeros((C,), jnp.float32), 'cmk': jax.random.uniform(ks[9], (1, 1, C), jnp.float32), 'cmr': jax.random.uniform(ks[10], (1, 1, C), jnp.float32)}
    _L0_attn_all = _L0_attn_setup()
    _L0_attn_in = {k: v for k, v in _L0_attn_all.items() if k in ('time_decay', 'time_first', 'W_tm', 'g1', 'b1', 'tmk', 'tmv', 'tmr', 'W_cm', 'W_cp', 'g2', 'b2', 'cmk', 'cmr')}
    del _L0_attn_all

    def _L0_ffn_setup():
        import jax, jax.numpy as jnp
        import numpy as np
        D_IN, D_HID = (256, 1024)

        def _ternary(key, shape):
            return jax.random.randint(key, shape, -1, 2).astype(jnp.float32)

        def _tlin(x, w, s):
            return jnp.einsum('bsi,oi->bso', x, w) * s
        key = jax.random.key(seed)
        ks = jax.random.split(key, 12)
        inv = lambda fan: 1.0 / np.sqrt(fan).astype(np.float32)
        return {'x': jax.random.normal(ks[0], (4, 512, D_IN), dtype=jnp.float32), 'w1_w': _ternary(ks[1], (D_HID, D_IN)), 'w1_s': jax.random.uniform(ks[2], (D_HID,), dtype=jnp.float32) * inv(D_IN), 'w2_w': _ternary(ks[3], (D_HID, D_IN)), 'w2_s': jax.random.uniform(ks[4], (D_HID,), dtype=jnp.float32) * inv(D_IN), 'h1_w': _ternary(ks[5], (D_HID, D_HID)), 'h1_s': jax.random.uniform(ks[6], (D_HID,), dtype=jnp.float32) * inv(D_HID), 'h2_w': _ternary(ks[7], (D_HID, D_HID)), 'h2_s': jax.random.uniform(ks[8], (D_HID,), dtype=jnp.float32) * inv(D_HID), 'w3_w': _ternary(ks[9], (D_IN, D_HID)), 'w3_s': jax.random.uniform(ks[10], (D_IN,), dtype=jnp.float32) * inv(D_HID)}
    _L0_ffn_all = _L0_ffn_setup()
    _L0_ffn_in = {k: v for k, v in _L0_ffn_all.items() if k in ('w1_w', 'w1_s', 'w2_w', 'w2_s', 'h1_w', 'h1_s', 'h2_w', 'h2_s', 'w3_w', 'w3_s')}
    del _L0_ffn_all
    return {'x': x, 'L0_tok_log_dt': _L0_tok_in['log_dt'], 'L0_tok_inv_A_real': _L0_tok_in['inv_A_real'], 'L0_tok_A_imag': _L0_tok_in['A_imag'], 'L0_tok_B_ri': _L0_tok_in['B_ri'], 'L0_attn_time_decay': _L0_attn_in['time_decay'], 'L0_attn_time_first': _L0_attn_in['time_first'], 'L0_attn_W_tm': _L0_attn_in['W_tm'], 'L0_attn_g1': _L0_attn_in['g1'], 'L0_attn_b1': _L0_attn_in['b1'], 'L0_attn_tmk': _L0_attn_in['tmk'], 'L0_attn_tmv': _L0_attn_in['tmv'], 'L0_attn_tmr': _L0_attn_in['tmr'], 'L0_attn_W_cm': _L0_attn_in['W_cm'], 'L0_attn_W_cp': _L0_attn_in['W_cp'], 'L0_attn_g2': _L0_attn_in['g2'], 'L0_attn_b2': _L0_attn_in['b2'], 'L0_attn_cmk': _L0_attn_in['cmk'], 'L0_attn_cmr': _L0_attn_in['cmr'], 'L0_ffn_w1_w': _L0_ffn_in['w1_w'], 'L0_ffn_w1_s': _L0_ffn_in['w1_s'], 'L0_ffn_w2_w': _L0_ffn_in['w2_w'], 'L0_ffn_w2_s': _L0_ffn_in['w2_s'], 'L0_ffn_h1_w': _L0_ffn_in['h1_w'], 'L0_ffn_h1_s': _L0_ffn_in['h1_s'], 'L0_ffn_h2_w': _L0_ffn_in['h2_w'], 'L0_ffn_h2_s': _L0_ffn_in['h2_s'], 'L0_ffn_w3_w': _L0_ffn_in['w3_w'], 'L0_ffn_w3_s': _L0_ffn_in['w3_s']}

def reference(x, L0_tok_log_dt, L0_tok_inv_A_real, L0_tok_A_imag, L0_tok_B_ri, L0_attn_time_decay, L0_attn_time_first, L0_attn_W_tm, L0_attn_g1, L0_attn_b1, L0_attn_tmk, L0_attn_tmv, L0_attn_tmr, L0_attn_W_cm, L0_attn_W_cp, L0_attn_g2, L0_attn_b2, L0_attn_cmk, L0_attn_cmr, L0_ffn_w1_w, L0_ffn_w1_s, L0_ffn_w2_w, L0_ffn_w2_s, L0_ffn_h1_w, L0_ffn_h1_s, L0_ffn_h2_w, L0_ffn_h2_s, L0_ffn_w3_w, L0_ffn_w3_s):
    import jax
    import jax.numpy as jnp

    def _L0_tok_ref(log_dt, inv_A_real, A_imag, B_ri, C_ri, L):
        import jax, jax.numpy as jnp
        import numpy as np
        import math
        H = 256
        N = 64
        CH = 1
        SEQ_L = 256
        dt = jnp.exp(log_dt)
        A = -jnp.exp(inv_A_real) + 1j * A_imag
        B = B_ri[..., 0] + 1j * B_ri[..., 1]
        C = C_ri[..., 0] + 1j * C_ri[..., 1]
        dtA = A * dt[:, None]
        dA = (1.0 + dtA / 2) / (1.0 - dtA / 2)
        C_term = C * B[None]
        log_dA = jnp.log(dA)
        V = jnp.exp(log_dA[:, :, None] * jnp.arange(L))
        K = 2.0 * jnp.einsum('chn,hnl->chl', C_term, V).real
        return K.astype(jnp.float32)

    def _L0_attn_ref(x, time_decay, time_first, W_tm, g1, b1, tmk, tmv, tmr, W_cm, W_cp, g2, b2, cmk, cmr):
        import jax, jax.numpy as jnp
        import numpy as np
        LN_EPS = 1e-05
        WKV_EPS = 1e-08
        NEG_INF = -1e+38

        def _layernorm(x, g, b):
            m = jnp.mean(x, axis=-1, keepdims=True)
            v = jnp.mean(jnp.square(x - m), axis=-1, keepdims=True)
            return (x - m) * jax.lax.rsqrt(v + LN_EPS) * g + b

        def _wkv(w, u, k, v):
            B, T, C = k.shape
            aa0 = jnp.zeros((B, C), k.dtype)
            bb0 = jnp.full((B, C), NEG_INF, k.dtype)

            def step(carry, kv_t):
                aa, bb = carry
                kk, vv = kv_t
                ww = u + kk
                p = jnp.maximum(bb, ww)
                e1 = jnp.exp(bb - p)
                e2 = jnp.exp(ww - p)
                y_t = (e1 * aa + e2 * vv) / (e1 + e2 + WKV_EPS)
                ww = w + bb
                p = jnp.maximum(ww, kk)
                e1 = jnp.exp(ww - p)
                e2 = jnp.exp(kk - p)
                aa = e1 * aa + e2 * vv
                bb = p + jnp.log(e1 + e2 + WKV_EPS)
                return ((aa, bb), y_t)
            (aa, bb), ys = jax.lax.scan(step, (aa0, bb0), (jnp.swapaxes(k, 0, 1), jnp.swapaxes(v, 0, 1)))
            y = jnp.swapaxes(ys, 0, 1)
            new_state = jnp.stack([aa, bb], axis=-1)
            return (y, new_state)

        def _reference_tuple_inner(x, time_decay, time_first, W_tm, g1, b1, tmk, tmv, tmr, W_cm, W_cp, g2, b2, cmk, cmr):
            x_prev = jnp.concatenate([x[:, :1], x[:, :-1]], axis=1)
            kvr = _layernorm(x, g1, b1) @ W_tm
            k, v, r = jnp.split(kvr, 3, axis=-1)
            k = k * tmk + x_prev * (1.0 - tmk)
            v = v * tmv + x_prev * (1.0 - tmv)
            r = jax.nn.sigmoid(r * tmr + x_prev * (1.0 - tmr))
            y, new_state = _wkv(time_decay, time_first, k, v)
            x = x + r * y
            xp = jnp.concatenate([x[:, -1:], x[:, :-1]], axis=1)
            xn = _layernorm(x, g2, b2)
            kk = xn @ W_cm
            cmk4 = jnp.tile(cmk, (1, 1, 4))
            xp4 = jnp.tile(xp, (1, 1, 4))
            kk = kk * cmk4 + xp4 * (1.0 - cmk4)
            rr = jax.nn.sigmoid(xn * cmr + xp * (1.0 - cmr))
            vv = jnp.square(jax.nn.relu(kk)) @ W_cp
            x = x + rr * vv
            return (x, new_state)
        return _reference_tuple_inner(x, time_decay, time_first, W_tm, g1, b1, tmk, tmv, tmr, W_cm, W_cp, g2, b2, cmk, cmr)[0]

    def _L0_ffn_ref(x, w1_w, w1_s, w2_w, w2_s, h1_w, h1_s, h2_w, h2_s, w3_w, w3_s):
        import jax, jax.numpy as jnp
        import numpy as np
        D_IN, D_HID = (256, 1024)

        def _ternary(key, shape):
            return jax.random.randint(key, shape, -1, 2).astype(jnp.float32)

        def _tlin(x, w, s):
            return jnp.einsum('bsi,oi->bso', x, w) * s
        h = jax.nn.silu(_tlin(x, w1_w, w1_s)) * _tlin(x, w2_w, w2_s)
        h = jax.nn.gelu(_tlin(h, h1_w, h1_s), approximate=False)
        h = jax.nn.gelu(_tlin(h, h2_w, h2_s), approximate=False)
        return _tlin(h, w3_w, w3_s)
    h = _L0_tok_ref(L0_tok_log_dt, L0_tok_inv_A_real, L0_tok_A_imag, L0_tok_B_ri, x, 256)
    h = _layernorm(h + _L0_attn_ref(h, L0_attn_time_decay, L0_attn_time_first, L0_attn_W_tm, L0_attn_g1, L0_attn_b1, L0_attn_tmk, L0_attn_tmv, L0_attn_tmr, L0_attn_W_cm, L0_attn_W_cp, L0_attn_g2, L0_attn_b2, L0_attn_cmk, L0_attn_cmr), axis=-1)
    h = _layernorm(h + _L0_ffn_ref(h, L0_ffn_w1_w, L0_ffn_w1_s, L0_ffn_w2_w, L0_ffn_w2_s, L0_ffn_h1_w, L0_ffn_h1_s, L0_ffn_h2_w, L0_ffn_h2_s, L0_ffn_w3_w, L0_ffn_w3_s), axis=-1)
    return h

_drawn_inputs = setup_inputs


def setup_inputs(seed=0):
    import zlib

    import numpy as np

    out = dict(_drawn_inputs(seed))
    spreads = {'L0_attn_g1': (1.0, 0.2),
     'L0_attn_b1': (0.0, 0.8),
     'L0_attn_g2': (1.0, 0.6),
     'L0_attn_b2': (0.0, 0.545)}
    factors = {'L0_attn_W_cm': 4.143,
     'L0_ffn_w1_w': 8.0,
     'L0_ffn_w1_s': 8.0,
     'L0_ffn_w2_w': 8.0,
     'L0_ffn_w2_s': 8.0,
     'L0_ffn_h1_w': 8.0,
     'L0_ffn_h1_s': 8.0,
     'L0_ffn_h2_w': 8.0,
     'L0_ffn_h2_s': 8.0,
     'L0_ffn_w3_w': 8.0,
     'L0_ffn_w3_s': 8.0}
    for name, (base, spread) in spreads.items():
        noise = np.random.default_rng([zlib.crc32(name.encode()), seed]).standard_normal(out[name].shape)
        drawn = base * np.exp(spread * noise) if base else spread * noise
        out[name] = jnp.asarray(drawn.astype(out[name].dtype))
    for name, factor in factors.items():
        out[name] = (out[name] * factor).astype(out[name].dtype)
    return out
```

```python
from contextlib import ExitStack

import concourse.bass as bass
from concourse import mybir

F32 = mybir.dt.float32
I32 = mybir.dt.int32
ALU = mybir.AluOpType
ACT = mybir.ActivationFunctionType

P = 128
NB = 32
T = 256
C = 256
NS = 64
F = 1024
NT = 8
CH = T // NT
TOK = NB * NT
CT = C // P
FT = F // P
LN = CT * NB
W9 = NT + 1
QP = T // 2
QC = NT // 2
QG = 32
HX = QC * 2 * 16
R16 = 16
LN_EPS = 1e-5
WKV_EPS = 1e-8
NEG_INF = -1e38

COLS = {}
for _name, _n in (("w", CT), ("u", CT), ("tmk", CT), ("tmv", CT), ("tmr", CT), ("g1", CT), ("b1", CT),
                  ("g2", CT), ("b2", CT), ("cmk", CT), ("cmr", CT), ("s1", FT), ("s2", FT), ("sh1", FT),
                  ("sh2", FT), ("s3", CT)):
    COLS[_name] = (sum(n for _, n in COLS.values()), _n)
NCOL = sum(n for _, n in COLS.values())


class Line:

    def __init__(self, sem, steps):
        self.sem, self.steps, self.at = sem, steps, 0

    def step(self, name):
        assert self.steps[self.at] == name, (self.steps[self.at], name)
        self.at = (self.at + 1) % len(self.steps)
        return self.sem, 1

    def value(self, name, n):
        return len(self.steps) * n + self.steps.index(name) + 1


def after(eng, line, name, n):
    if not (isinstance(n, int) and n < 0):
        eng.wait_ge(line.sem, line.value(name, n))


def build(nc, c_in, log_dt, a_re, a_im, b_ri, par, w_tm, w_cm, w_cp, w1, w2, h1, h2, w3, out, tpq):
    ctx = ExitStack()
    with ctx:
        def sb(name, shape, dt=F32, stack=ctx):
            return stack.enter_context(nc.sbuf_tensor(name, shape, dt))

        def sem(name):
            return ctx.enter_context(nc.semaphore(name))

        W_tm = sb("W_tm", [P, CT, 3 * C])
        W_cm = sb("W_cm", [P, CT, F])
        W_cp = sb("W_cp", [P, FT, C])
        W_1 = sb("W_1", [P, CT, F])
        W_2 = sb("W_2", [P, CT, F])
        W_h1 = sb("W_h1", [P, FT, F])
        W_h2 = sb("W_h2", [P, FT, F])
        W_3 = sb("W_3", [P, FT, C])
        prm = sb("prm", [P, NCOL])
        onem = sb("onem", [P, 5 * CT])
        negu = sb("negu", [P, CT])
        mean_w = sb("mean_w", [P, P])
        eps_c = sb("eps_c", [P, 2])
        wdec = sb("wdec", [P, LN, W9])
        bmode = sb("bmode", [P, QP, 2])
        x1_first = sb("x1_first", [P, LN])

        cin = sb("cin", [P, 2, QC, 2, NB])
        pq = sb("pq", [P, 2, 2, QC, 2, R16])
        cbt = sb("cbt", [P, 2, QC, 2, NB])
        bd = sb("bd", [P, QC, 2, 2 * NB])
        Vr = sb("Vr", [P, 2, C])
        Vi = sb("Vi", [P, 2, C])
        Vt = sb("Vt", [P, 2, C])
        xn = sb("xn", [P, CT, TOK])
        xw = sb("xw", [P, 2, LN, W9])
        x1w = sb("x1w", [P, 2, LN, W9])
        xn2 = sb("xn2", [P, CT, TOK])
        x2 = sb("x2", [P, CT, TOK])
        rr = sb("rr", [P, CT, TOK])
        xpc = sb("xpc", [P, CT, TOK])
        kk = sb("kk", [P, 2, 2, TOK])
        hres = sb("hres", [P, 2, CT, TOK])
        ha = sb("ha", [P, FT, TOK])
        hb = sb("hb", [P, FT, TOK])
        sil = sb("sil", [P, 2, TOK])
        sq4 = sb("sq4", [P, CT, TOK])
        hs4 = sb("hs4", [P, TOK])
        rs4 = sb("rs4", [P, TOK])

        setup = ExitStack()
        EX = sb("EX", [P, 2, QP], stack=setup)
        EN = sb("EN", [P, 2, QP], stack=setup)
        EQ = sb("EQ", [P, 2, QP], stack=setup)
        EI = sb("EI", [P, 2, QP], I32, stack=setup)
        aim = sb("aim", [P, QP], stack=setup)
        Z = sb("Z", [P, 2, QP, 2, 4], stack=setup)
        zt = sb("zt", [P, 2, 2 * QG, 8], stack=setup)
        tg = sb("tg", [P, 2, QG, 2, R16], stack=setup)
        setup.close()
        kw = sb("kw", [P, LN, W9])
        vw = sb("vw", [P, LN, W9])
        rw = sb("rw", [P, LN, W9])
        mw = sb("mw", [P, LN, W9])
        sw = sb("sw", [P, LN, W9])
        aw = sb("aw", [P, LN, W9])
        e1 = sb("e1", [P, 2, LN, W9])
        e2 = sb("e2", [P, 2, LN, W9])
        t3 = sb("t3", [P, LN, W9])

        bank = [ctx.enter_context(nc.psum_tensor(f"bank{i}", [P, 512], F32)) for i in range(8)]
        S_ST, S_CP, S_A, S_CM = 4, 5, 6, 7

        def col(name, k=0):
            at = COLS[name][0] + k
            return prm[:, at:at + 1]

        def one_minus(name, k):
            at = CT * ("tmk", "tmv", "tmr", "cmk", "cmr").index(name) + k
            return onem[:, at:at + 1]

        def cur(w):
            return w[..., 1:W9]

        def prv(w):
            return w[..., 0:NT]

        def half(w, h):
            return w[:, h * NB:(h + 1) * NB, :]

        def win(flat):
            return flat.rearrange("p c (b t) -> p (c b) t", t=NT)

        def win1(flat):
            return flat.rearrange("p (b t) -> p b t", t=NT)

        def both(ap):
            return ap.unsqueeze(1).broadcast_to([P, CT, TOK])

        lnA = t3[:].rearrange("p l t -> p (l t)")
        hs1, rs1 = lnA[:, 0:TOK], lnA[:, TOK:2 * TOK]
        sq1 = e2[:, 1].rearrange("p l t -> p (l t)")[:, 0:CT * TOK].rearrange("p (c n) -> p c n", c=CT)
        sqB = kk[:, 0]
        hsB, rsB = kk[:, 1, 0], kk[:, 1, 1]

        ld_w = sem("ld_w")
        ld_tm = sem("ld_tm")
        ld_cm = sem("ld_cm")
        ld_ff = sem("ld_ff")
        ld_a = [sem("ld_a0"), sem("ld_a1")]
        put_t = sem("put_t")
        put_o = [sem("put_o0"), sem("put_o1")]
        su_vec = sem("su_vec")
        su_pool = sem("su_pool")
        su_act = sem("su_act")
        su_pe = sem("su_pe")

        a_pool = Line(sem("a_pool"), ["cb_re", "cb_im", "bd0", "bd1", "bd2", "bd3", "sum", "sum_sq"])
        a_pe = Line(sem("a_pe"), ["tok0", "tok1", "mean", "var", "kvr0", "kvr1", "kvr2"])
        a_act = Line(sem("a_act"), ["x_slot", "x", "sq", "lnv", "rstd", "kp0", "kp1", "vp0", "vp1", "rp0", "rp1",
                                    "d1", "d2", "lns", "ef1", "ef2", "lnd", "rden", "sig"])
        a_vec = Line(sem("a_vec"), [f"{s}{g}" for g in range(2) for s in ("vr", "vt", "vs", "vi", "vu", "vw")]
                     + ["xc", "xn", "xg0", "xg1", "k0", "k1", "v0", "v1", "r0", "r1",
                        "mc", "m", "d10", "d11", "d2", "sc", "s", "bb", "dl0", "dl1", "gm0", "gm1",
                        "mn", "mx", "ev", "ac", "aa", "den", "n1", "n2", "n3", "y", "ry", "x1", "x1s"])
        b_pool = Line(sem("b_pool"), ["sum", "sum_sq", "xx", "sum3", "sum_sq3"])
        b_pe = Line(sem("b_pe"), ["mean", "var", "cm0", "cm1", "cp0", "cm2", "cp1", "cm3", "cp2", "cp3",
                                  "mean3", "var3"])
        b_act = Line(sem("b_act"), ["sq", "lnv", "rstd", "kp0", "kp1", "rp0", "rp1", "rr", "sq3", "lnv3", "rstd3"])
        b_vec = Line(sem("b_vec"), ["xc", "xn", "xg0", "xg1", "r0", "r1"]
                     + [s for i in range(4) for s in (f"k{2*i}", f"k{2*i+1}", f"q{i}")]
                     + ["rv", "x2", "xc3", "h"])
        c_pool = Line(sem("c_pool"), ["sum", "sum_sq"])
        c_pe = Line(sem("c_pe"), [f"w{m}" for m in range(8)] + [f"h1{i}" for i in range(4)]
                    + [f"h2{i}" for i in range(4)] + ["y", "mean", "var"])
        c_act = Line(sem("c_act"), [f"s{m}" for m in range(8)] + [f"g1{m}" for m in range(8)]
                     + [f"g2{m}" for m in range(8)] + ["sq", "lnv", "rstd"])
        c_vec = Line(sem("c_vec"), [f"h{m}" for m in range(8)] + ["y0", "y1", "xc", "o"])

        block = ctx.enter_context(nc.Block())


        def iterations(eng, stages):
            for n in range(4):
                stages(n, n % 2)
            with eng.Fori(4, CH - 1, 2) as n:
                stages(n, 0)
                stages(n + 1, 1)
            stages(CH, 0)
            stages(CH + 1, 1)

        def has(stage, n):
            lag = "ABC".index(stage)
            return not isinstance(n, int) or 0 <= n - lag < CH

        def chunk(dram, n):
            return dram[bass.ds(n, 1)].rearrange("o p x -> (o p) x")


        @block.sync
        def _(eng):
            eng.dma_start(prm[:], par).then_inc(ld_w, 16)
            eng.dma_start(EX[0:NS, 0, :], log_dt[0:1, :].broadcast_to([NS, QP])).then_inc(ld_w, 16)
            eng.dma_start(EX[NS:P, 0, :], log_dt[1:2, :].broadcast_to([NS, QP])).then_inc(ld_w, 16)
            eng.dma_start(EX[:, 1, :], a_re).then_inc(ld_w, 16)
            eng.dma_start(aim[:], a_im).then_inc(ld_w, 16)
            eng.dma_start(bmode[:], b_ri).then_inc(ld_w, 16)
            eng.dma_start(cin[:, 1].rearrange("p q r b -> p (q r b)"), c_in[CH - 1]).then_inc(ld_a[1], 16)
            eng.dma_start(W_tm[:], w_tm).then_inc(ld_tm, 16)
            for i, g in enumerate((3, 0, 1, 2)):
                eng.wait_ge(su_vec, TG_DONE[i])
                for ri in range(2):
                    eng.dma_start(tpq[8 * g:8 * g + 8, :, ri * HX:(ri + 1) * HX].rearrange("n p x -> p n x"),
                                  tg[:, ri].rearrange("p (n q) s r -> p n (q s r)", n=8)).then_inc(put_t, 16)
            eng.wait_ge(put_t, 128)

            def load_a(n, p):
                if not (isinstance(n, int) and n < 2):
                    after(eng, a_pool, "cb_im", n - 2)
                    after(eng, a_vec, "vw1", n - 2)
                eng.dma_start(cin[:, p].rearrange("p q r b -> p (q r b)"), chunk(c_in, n)).then_inc(ld_a[p], 16)
                eng.dma_start(pq[:, p].rearrange("p r q s l -> p (r q s l)"), chunk(tpq, n)).then_inc(ld_a[p], 16)

            def stages(n, p):
                if has("A", n):
                    load_a(n, p)
                if has("C", n):
                    after(eng, c_vec, "o", n - 2)
                    eng.dma_start(chunk(out, n - 2), hres[:, p].rearrange("p c n -> p (c n)")).then_inc(put_o[p], 16)

            eng.wait_ge(su_vec, V0_DONE)
            eng.wait_ge(su_pool, CB0_DONE)
            iterations(eng, stages)
            for p in range(2):
                eng.wait_ge(put_o[p], 8 * CH)

        @block.gpsimd
        def _(eng):
            k = 0

            def did(ins):
                nonlocal k
                k += 1
                ins.then_inc(su_pool, 1)

            did(eng.memset(mean_w[:], 1.0 / C))
            did(eng.memset(eps_c[:, 0:1], LN_EPS))
            did(eng.memset(eps_c[:, 1:2], WKV_EPS))
            did(eng.memset(bd[:], 0.0))
            eng.wait_ge(su_vec, BM_DONE)
            eng.wait_ge(ld_a[1], 16)
            q = QP - 1
            qc = QC - 1
            did(eng.tensor_tensor(cbt[:, 0, 0], cin[:, 1, qc], bmode[:, q, 0:1].unsqueeze(2).broadcast_to([P, 2, NB]), ALU.mult))
            did(eng.tensor_tensor(cbt[:, 1, 0], cin[:, 1, qc], bmode[:, q, 1:2].unsqueeze(2).broadcast_to([P, 2, NB]), ALU.mult))
            assert k == CB0_DONE
            eng.wait_ge(su_pool, k)
            s = slice(NS, P)
            did(eng.tensor_tensor(bd[s, 0, 0, NB:], cbt[s, 0, 0, 0], cbt[s, 1, 0, 1], ALU.add))
            did(eng.tensor_tensor(bd[s, 0, 1, NB:], cbt[s, 1, 0, 0], cbt[s, 0, 0, 1], ALU.subtract))
            assert k == BD0_DONE

            def stage_a(n, p):
                bre = bmode[:, bass.ds(QC * n, QC), 0:1]
                bim = bmode[:, bass.ds(QC * n, QC), 1:2]
                eng.wait_ge(ld_a[p], ld_value(n, p))
                if isinstance(n, int) and n == 0:
                    eng.wait_ge(su_pool, BD0_DONE)
                after(eng, a_pool, "bd3", n - 1)
                eng.tensor_tensor(cbt[:, 0], cin[:, p], bre.unsqueeze(3).broadcast_to([P, QC, 2, NB]),
                                  ALU.mult).then_inc(*a_pool.step("cb_re"))
                eng.tensor_tensor(cbt[:, 1], cin[:, p], bim.unsqueeze(3).broadcast_to([P, QC, 2, NB]),
                                  ALU.mult).then_inc(*a_pool.step("cb_im"))
                after(eng, a_pool, "cb_im", n)
                after(eng, a_pe, "tok1", n - 1)
                if isinstance(n, int) and n == 0:
                    eng.wait_ge(su_pe, 1)
                for t in range(2):
                    s = slice(t * NS, (t + 1) * NS)
                    eng.tensor_tensor(bd[s, :, 0, t * NB:(t + 1) * NB], cbt[s, 0, :, 0], cbt[s, 1, :, 1],
                                      ALU.add).then_inc(*a_pool.step(f"bd{2 * t}"))
                    eng.tensor_tensor(bd[s, :, 1, t * NB:(t + 1) * NB], cbt[s, 1, :, 0], cbt[s, 0, :, 1],
                                      ALU.subtract).then_inc(*a_pool.step(f"bd{2 * t + 1}"))

            def stage_a_x(n, p):
                after(eng, a_act, "x", n)
                after(eng, a_vec, "y", n - 1)
                eng.tensor_tensor(win1(hs1), cur(half(xw[:, p], 0)), cur(half(xw[:, p], 1)),
                                  ALU.add).then_inc(*a_pool.step("sum"))

            def stage_a_sq(n, p):
                after(eng, a_act, "sq", n)
                after(eng, a_pe, "mean", n)
                eng.tensor_tensor(hs1, sq1[:, 0], sq1[:, 1], ALU.add).then_inc(*a_pool.step("sum_sq"))

            def stage_b1(n, p):
                after(eng, a_vec, "x1s", n)
                if isinstance(n, int) and n == CH - 1:
                    eng.wait_ge(su_vec, X1_FIXED)
                after(eng, b_vec, "h", n - 1)
                eng.tensor_tensor(win1(hsB), cur(half(x1w[:, p], 0)), cur(half(x1w[:, p], 1)),
                                  ALU.add).then_inc(*b_pool.step("sum"))
                after(eng, b_act, "sq", n)
                after(eng, b_pe, "mean", n)
                eng.tensor_tensor(hsB, sqB[:, 0], sqB[:, 1], ALU.add).then_inc(*b_pool.step("sum_sq"))
                eng.tensor_tensor(win(x2[:]), cur(xw[:, p]), cur(x1w[:, p]), ALU.add).then_inc(*b_pool.step("xx"))

            def stage_b3(n, p):
                after(eng, b_vec, "x2", n)
                after(eng, b_pe, "cp3", n)
                eng.tensor_tensor(hsB, x2[:, 0], x2[:, 1], ALU.add).then_inc(*b_pool.step("sum3"))
                after(eng, b_act, "sq3", n)
                after(eng, b_pe, "mean3", n)
                eng.tensor_tensor(hsB, sqB[:, 0], sqB[:, 1], ALU.add).then_inc(*b_pool.step("sum_sq3"))

            def stage_c(n, p):
                after(eng, c_vec, "y1", n)
                after(eng, c_pe, "var", n - 1)
                eng.tensor_tensor(hs4[:], hres[:, p, 0], hres[:, p, 1], ALU.add).then_inc(*c_pool.step("sum"))
                after(eng, c_act, "sq", n)
                after(eng, c_pe, "mean", n)
                eng.tensor_tensor(hs4[:], sq4[:, 0], sq4[:, 1], ALU.add).then_inc(*c_pool.step("sum_sq"))

            def stages(n, p):
                if has("A", n):
                    stage_a(n, p)
                    stage_a_x(n, p)
                    stage_a_sq(n, p)
                if has("B", n):
                    stage_b1(n - 1, 1 - p)
                if has("C", n):
                    stage_c(n - 2, p)
                if has("B", n):
                    stage_b3(n - 1, 1 - p)

            iterations(eng, stages)

        @block.scalar
        def _(eng):
            eng.dma_start(W_cm[:], w_cm).then_inc(ld_cm, 16)
            eng.dma_start(W_cp[:], w_cp).then_inc(ld_cm, 16)
            eng.dma_start(W_1[:], w1).then_inc(ld_ff, 16)
            eng.dma_start(W_2[:], w2).then_inc(ld_ff, 16)
            eng.dma_start(W_h1[:], h1).then_inc(ld_ff, 16)
            eng.dma_start(W_h2[:], h2).then_inc(ld_ff, 16)
            eng.dma_start(W_3[:], w3).then_inc(ld_ff, 16)
            k = 0

            def did(ins):
                nonlocal k
                k += 1
                ins.then_inc(su_act, 1)

            xw0 = xw[:, 1, :, NT]
            eng.wait_ge(su_pe, 1)
            did(eng.activation(xw0.rearrange("p (c b) -> p c b", c=CT),
                               bank[S_A][:, 0:2 * 2 * NB].rearrange("p (c t b) -> p c t b", c=2, t=2)[:, :, 1, :], ACT.Copy))
            assert k == X0_DONE
            eng.wait_ge(su_vec, XC0_DONE)
            did(eng.activation(sq1[:, :, 0:NB], xn[:, :, 0:NB], ACT.Square))
            assert k == SQ0_DONE
            eng.wait_ge(su_pe, 3)
            eng.wait_ge(su_pool, BD0_DONE)
            did(eng.activation(rs1[:, 0:NB], bank[S_ST][:, TOK:TOK + NB], ACT.Ln, bias=eps_c[:, 0:1]))
            eng.wait_ge(su_act, k)
            did(eng.activation(rs1[:, 0:NB], rs1[:, 0:NB], ACT.Exp, scale=-0.5))
            assert k == RS0_DONE
            eng.wait_ge(su_vec, R0_DONE)
            did(eng.activation(rw[:, :, NT], rw[:, :, NT], ACT.Sigmoid))
            assert k == SG0_DONE

            def a_norm(n, p):
                after(eng, a_act, "rp1", n - 1)
                if isinstance(n, int) and n == 0:
                    eng.wait_ge(su_act, X0_DONE)
                eng.activation(xw[:, p, :, 0], xw[:, 1 - p, :, NT], ACT.Copy).then_inc(*a_act.step("x_slot"))
                after(eng, a_pe, "tok1", n)
                after(eng, b_pool, "xx", n - 2)
                src = bank[S_A][:].rearrange("p (c t b) -> p c t b", c=CT, b=NB)
                dst = cur(xw[:, p]).rearrange("p (c b) t -> p c t b", c=CT)
                eng.activation(dst, src, ACT.Copy).then_inc(*a_act.step("x"))
                after(eng, a_vec, "xc", n)
                eng.activation(sq1, xn[:], ACT.Square).then_inc(*a_act.step("sq"))

            def a_rstd(n, p):
                after(eng, a_pe, "var", n)
                eng.activation(rs1, bank[S_ST][:, TOK:2 * TOK], ACT.Ln, bias=eps_c[:, 0:1]).then_inc(*a_act.step("lnv"))
                after(eng, a_act, "lnv", n)
                eng.activation(rs1, rs1, ACT.Exp, scale=-0.5).then_inc(*a_act.step("rstd"))
                after(eng, a_act, "x", n)
                after(eng, a_vec, "ry", n - 1)
                if isinstance(n, int) and n == 0:
                    eng.wait_ge(su_vec, A0_DONE)
                for name, w, tm in (("kp", kw, "tmk"), ("vp", vw, "tmv"), ("rp", rw, "tmr")):
                    for h in range(CT):
                        eng.activation(cur(half(w[:], h)), prv(half(xw[:, p], h)), ACT.Copy,
                                       scale=one_minus(tm, h)).then_inc(*a_act.step(f"{name}{h}"))

            def a_exp(n, p):
                after(eng, a_vec, "d11", n)
                eng.activation(cur(e1[:, 0]), cur(e1[:, 0]), ACT.Exp).then_inc(*a_act.step("d1"))
                after(eng, a_vec, "d2", n)
                eng.activation(cur(e2[:, 0]), cur(e2[:, 0]), ACT.Exp).then_inc(*a_act.step("d2"))
                after(eng, a_vec, "s", n)
                eng.activation(t3[:], sw[:], ACT.Ln, bias=eps_c[:, 1:2]).then_inc(*a_act.step("lns"))
                after(eng, a_vec, "mx", n)
                eng.activation(cur(e1[:]), cur(e1[:]), ACT.Exp).then_inc(*a_act.step("ef1"))
                eng.activation(cur(e2[:]), cur(e2[:]), ACT.Exp, scale=-1.0).then_inc(*a_act.step("ef2"))
                after(eng, a_vec, "den", n)
                eng.activation(cur(t3[:]), cur(t3[:]), ACT.Ln).then_inc(*a_act.step("lnd"))
                after(eng, a_act, "lnd", n)
                eng.activation(cur(t3[:]), cur(t3[:]), ACT.Exp, scale=-1.0).then_inc(*a_act.step("rden"))

            def a_sig(n, p):
                after(eng, a_vec, "r1", n)
                eng.activation(cur(rw[:]), cur(rw[:]), ACT.Sigmoid).then_inc(*a_act.step("sig"))

            def b_norm(n, p):
                after(eng, b_vec, "xc", n)
                eng.activation(sqB, xn2[:], ACT.Square).then_inc(*b_act.step("sq"))
                after(eng, b_pe, "var", n)
                eng.activation(rsB, bank[S_ST][:, TOK:2 * TOK], ACT.Ln, bias=eps_c[:, 0:1]).then_inc(*b_act.step("lnv"))
                after(eng, b_act, "lnv", n)
                eng.activation(rsB, rsB, ACT.Exp, scale=-0.5).then_inc(*b_act.step("rstd"))

            def b_mix(n, p):
                after(eng, b_vec, "x2", n - 1)
                for h in range(CT):
                    eng.activation(win1(xpc[:, h]), prv(half(x1w[:, p], h)), ACT.Copy,
                                   scale=one_minus("cmk", h)).then_inc(*b_act.step(f"kp{h}"))
                for h in range(CT):
                    eng.activation(win1(rr[:, h]), prv(half(x1w[:, p], h)), ACT.Copy,
                                   scale=one_minus("cmr", h)).then_inc(*b_act.step(f"rp{h}"))

            def b_sig(n, p):
                after(eng, b_vec, "r1", n)
                eng.activation(rr[:], rr[:], ACT.Sigmoid).then_inc(*b_act.step("rr"))

            def b_norm3(n, p):
                after(eng, b_vec, "xc3", n)
                eng.activation(sqB, x2[:], ACT.Square).then_inc(*b_act.step("sq3"))
                after(eng, b_pe, "var3", n)
                eng.activation(rsB, bank[S_ST][:, TOK:2 * TOK], ACT.Ln, bias=eps_c[:, 0:1]).then_inc(*b_act.step("lnv3"))
                after(eng, b_act, "lnv3", n)
                eng.activation(rsB, rsB, ACT.Exp, scale=-0.5).then_inc(*b_act.step("rstd3"))

            def c_silu(n, p):
                for m in range(FT):
                    after(eng, c_pe, f"w{m}", n)
                    if m >= 2:
                        after(eng, c_vec, f"h{m - 2}", n)
                    else:
                        after(eng, c_vec, f"h{m + 6}", n - 1)
                    eng.activation(sil[:, m % 2], bank[m % 4][:, 0:TOK], ACT.Silu,
                                   scale=col("s1", m)).then_inc(*c_act.step(f"s{m}"))

            def c_gelu(n, p, layer):
                dst, src, sc = (hb, "h1", "sh1") if layer == 1 else (ha, "h2", "sh2")
                if layer == 1:
                    after(eng, c_pe, "h23", n - 1)
                else:
                    after(eng, c_pe, "h13", n)
                for m in range(FT):
                    if m % 2 == 0:
                        after(eng, c_pe, f"{src}{m // 2}", n)
                    eng.activation(dst[:, m], bank[m // 2][:, (m % 2) * TOK:(m % 2 + 1) * TOK], ACT.Gelu,
                                   scale=col(sc, m)).then_inc(*c_act.step(f"g{layer}{m}"))

            def c_norm(n, p):
                after(eng, c_vec, "xc", n)
                eng.activation(sq4[:], hres[:, p], ACT.Square).then_inc(*c_act.step("sq"))
                after(eng, c_pe, "var", n)
                eng.activation(rs4[:], bank[S_ST][:, TOK:2 * TOK], ACT.Ln, bias=eps_c[:, 0:1]).then_inc(*c_act.step("lnv"))
                after(eng, c_act, "lnv", n)
                eng.activation(rs4[:], rs4[:], ACT.Exp, scale=-0.5).then_inc(*c_act.step("rstd"))

            def stages(n, p):
                A, B, Cc = has("A", n), has("B", n), has("C", n)
                if Cc:
                    c_silu(n - 2, p)
                if A:
                    a_norm(n, p)
                    a_rstd(n, p)
                if Cc:
                    c_gelu(n - 2, p, 1)
                if A:
                    a_exp(n, p)
                    a_sig(n, p)
                if B:
                    b_norm(n - 1, 1 - p)
                    b_mix(n - 1, 1 - p)
                if B:
                    b_sig(n - 1, 1 - p)
                if Cc:
                    c_gelu(n - 2, p, 2)
                    c_norm(n - 2, p)
                if B:
                    b_norm3(n - 1, 1 - p)

            iterations(eng, stages)

        @block.vector
        def _(eng):
            k = 0

            def did(ins, then=None):
                nonlocal k
                k += 1
                ins.then_inc(su_vec, 1)
                eng.wait_ge(su_vec, k)

            eng.wait_ge(ld_w, 96)
            did(eng.tensor_scalar(bmode[:, :, 0], bmode[:, :, 0], 2.0, None, ALU.mult))
            did(eng.tensor_scalar(bmode[:, :, 1], bmode[:, :, 1], -2.0, None, ALU.mult))
            assert k == BM_DONE, k
            for i, name in enumerate(("tmk", "tmv", "tmr", "cmk", "cmr")):
                a = COLS[name][0]
                did(eng.tensor_scalar(onem[:, CT * i:CT * i + CT], prm[:, a:a + CT], -1.0, 1.0, ALU.mult, ALU.add))
            a = COLS["u"][0]
            did(eng.tensor_scalar(negu[:], prm[:, a:a + CT], -1.0, None, ALU.mult))
            magic = 12582912.0
            did(eng.tensor_scalar(EN[:], EX[:], 1.4426950408889634, magic, ALU.mult, ALU.add))
            did(eng.tensor_scalar(EN[:], EN[:], magic, None, ALU.subtract))
            did(eng.tensor_scalar(EN[:], EN[:], -126.0, 127.0, ALU.max, ALU.min))
            did(eng.scalar_tensor_tensor(EX[:], EN[:], -0.693359375, EX[:], ALU.mult, ALU.add))
            did(eng.scalar_tensor_tensor(EX[:], EN[:], 2.12194440054690583e-4, EX[:], ALU.mult, ALU.add))
            did(eng.tensor_scalar(EN[:], EN[:], 127.0, None, ALU.add))
            did(eng.tensor_copy(EI[:], EN[:]))
            did(eng.tensor_scalar(EI[:], EI[:], 23, None, ALU.logical_shift_left))
            did(eng.tensor_scalar(EQ[:], EX[:], 1.0 / 5040, None, ALU.mult))
            for c in (720, 120, 24, 6, 2, 1):
                did(eng.scalar_tensor_tensor(EQ[:], EQ[:], 1.0 / c, EX[:], ALU.add, ALU.mult))
            did(eng.scalar_tensor_tensor(EX[:], EQ[:], 1.0, EI[:].bitcast(F32), ALU.add, ALU.mult))
            dt, a, b = EX[:, 0], EX[:, 1], aim[:]
            did(eng.scalar_tensor_tensor(a, a, -0.5, dt, ALU.mult, ALU.mult))
            did(eng.scalar_tensor_tensor(b, b, 0.5, dt, ALU.mult, ALU.mult))
            b2, den, num = EQ[:, 0], EQ[:, 1], EN[:, 0]
            did(eng.tensor_tensor(b2, b, b, ALU.mult))
            did(eng.tensor_scalar(EN[:, 1], a, -1.0, 1.0, ALU.mult, ALU.add))
            did(eng.tensor_tensor(den, EN[:, 1], EN[:, 1], ALU.mult))
            did(eng.tensor_tensor(den, den, b2, ALU.add))
            did(eng.scalar_tensor_tensor(num, a, 1.0, EN[:, 1], ALU.add, ALU.mult))
            did(eng.tensor_tensor(num, num, b2, ALU.subtract))
            did(eng.reciprocal(EN[:, 1], den))
            did(eng.tensor_tensor(Z[:, 0, :, 0, 0], num, EN[:, 1], ALU.mult))
            did(eng.scalar_tensor_tensor(Z[:, 1, :, 0, 0], b, 2.0, EN[:, 1], ALU.mult, ALU.mult))
            for j in range(7):
                r0, i0 = Z[:, 0, :, j // 4, j % 4], Z[:, 1, :, j // 4, j % 4]
                r1, i1 = Z[:, 0, :, (j + 1) // 4, (j + 1) % 4], Z[:, 1, :, (j + 1) // 4, (j + 1) % 4]
                did(eng.tensor_tensor(r1, r0, r0, ALU.mult))
                did(eng.tensor_tensor(num, i0, i0, ALU.mult))
                did(eng.tensor_tensor(r1, r1, num, ALU.subtract))
                did(eng.scalar_tensor_tensor(i1, r0, 2.0, i0, ALU.mult, ALU.mult))
            for i, g in enumerate((3, 0, 1, 2)):
                if i:
                    eng.wait_ge(put_t, 32 * i)
                t = tg[:].rearrange("p r q s l -> p r (q s) l")
                zg = Z[:, :, g * QG:(g + 1) * QG].rearrange("p r q s j -> p r (q s) j")
                did(eng.memset(t[:, 0, :, 0], 1.0))
                did(eng.memset(t[:, 1, :, 0], 0.0))
                did(eng.tensor_copy(t[:, :, :, 1], zg[:, :, :, 0]))
                for j in range(1, 4):
                    n = 1 << j
                    re, im = t[:, 0, :, 0:n], t[:, 1, :, 0:n]
                    zr = zg[:, 0, :, j:j + 1].broadcast_to([P, 2 * QG, n])
                    zi = zg[:, 1, :, j:j + 1].broadcast_to([P, 2 * QG, n])
                    did(eng.tensor_tensor(t[:, 0, :, n:2 * n], re, zr, ALU.mult))
                    did(eng.tensor_tensor(zt[:, 0, :, 0:n], im, zi, ALU.mult))
                    did(eng.tensor_tensor(t[:, 0, :, n:2 * n], t[:, 0, :, n:2 * n], zt[:, 0, :, 0:n], ALU.subtract))
                    did(eng.tensor_tensor(t[:, 1, :, n:2 * n], re, zi, ALU.mult))
                    did(eng.tensor_tensor(zt[:, 1, :, 0:n], im, zr, ALU.mult))
                    did(eng.tensor_tensor(t[:, 1, :, n:2 * n], t[:, 1, :, n:2 * n], zt[:, 1, :, 0:n], ALU.add))
                assert k == TG_DONE[i], (i, k)
                if i == 0:
                    did(eng.tensor_copy(pq[:, 1, :, QC - 1], tg[:, :, QG - 1]))
            eng.wait_ge(put_t, 128)
            did(eng.memset(wdec[:, :, 0], NEG_INF))
            for h in range(CT):
                did(eng.tensor_copy(half(wdec[:], h)[:, :, 1:W9].rearrange("p b t -> p b t"),
                                    col("w", h).unsqueeze(2).broadcast_to([P, NB, NT])))
            for w in (e1, e2, kw, vw, rw, mw, sw, aw, t3):
                did(eng.memset(w[:], 0.0))

            def powers(step, p, q0, nq, dst_r, dst_i, tmp):
                def pw(ri, s):
                    v = pq[:, p, ri, q0:q0 + nq, s]
                    v = v.unsqueeze(3) if s else v.unsqueeze(2)
                    return v.broadcast_to([P, nq, R16, R16])
                def o(x):
                    return x[:, 0:nq].rearrange("p q (a b) -> p q a b", b=R16)
                step(lambda: eng.tensor_tensor(o(dst_r), pw(0, 1), pw(0, 0), ALU.mult), "vr")
                step(lambda: eng.tensor_tensor(o(tmp), pw(1, 1), pw(1, 0), ALU.mult), "vt")
                step(lambda: eng.tensor_tensor(dst_r[:, 0:nq], dst_r[:, 0:nq], tmp[:, 0:nq], ALU.subtract), "vs")
                step(lambda: eng.tensor_tensor(o(dst_i), pw(0, 1), pw(1, 0), ALU.mult), "vi")
                step(lambda: eng.tensor_tensor(o(tmp), pw(1, 1), pw(0, 0), ALU.mult), "vu")
                step(lambda: eng.tensor_tensor(dst_i[:, 0:nq], dst_i[:, 0:nq], tmp[:, 0:nq], ALU.add), "vw")

            powers(lambda f, _: did(f()), 1, QC - 1, 1, Vr, Vi, Vt)
            assert k == V0_DONE, k
            x0 = xw[:, 1, :, NT].rearrange("p (c b) -> p c b", c=CT)
            eng.wait_ge(su_act, X0_DONE)
            did(eng.tensor_tensor(hs1[:, 0:NB], x0[:, 0], x0[:, 1], ALU.add))
            assert k == HS0_DONE, k
            eng.wait_ge(su_pe, 2)
            n0 = xn[:, :, 0:NB]
            did(eng.tensor_tensor(n0, x0, bank[S_ST][:, 0:NB].unsqueeze(1).broadcast_to([P, CT, NB]), ALU.subtract))
            assert k == XC0_DONE, k
            eng.wait_ge(su_act, SQ0_DONE)
            did(eng.tensor_tensor(hs1[:, 0:NB], sq1[:, 0, 0:NB], sq1[:, 1, 0:NB], ALU.add))
            assert k == HQ0_DONE, k
            eng.wait_ge(su_act, RS0_DONE)
            did(eng.tensor_tensor(n0, n0, rs1[:, 0:NB].unsqueeze(1).broadcast_to([P, CT, NB]), ALU.mult))
            for h in range(CT):
                did(eng.tensor_scalar(n0[:, h], n0[:, h], col("g1", h), col("b1", h), ALU.mult, ALU.add))
            assert k == XN0_DONE, k
            eng.wait_ge(su_pe, 4)
            for j, (w, tm) in enumerate(((mw, "tmk"), (aw, "tmv"), (rw, "tmr"))):
                for h in range(CT):
                    dst = half(w[:], h)[:, :, NT]
                    did(eng.tensor_scalar(dst, x0[:, h], one_minus(tm, h), None, ALU.mult))
                    at = (2 * j + h) * NB
                    did(eng.scalar_tensor_tensor(dst, bank[S_A][:, at:at + NB], col(tm, h), dst, ALU.mult, ALU.add))
            assert k == R0_DONE, k
            did(eng.memset(sw[:, :, NT], 1.0))
            eng.wait_ge(su_act, SG0_DONE)
            did(eng.scalar_tensor_tensor(x1_first[:], aw[:, :, NT], 1.0 / (1.0 + WKV_EPS), rw[:, :, NT], ALU.mult, ALU.mult))
            did(eng.tensor_tensor(x1_first[:], x1_first[:], xw[:, 1, :, NT], ALU.add))
            did(eng.tensor_copy(x1w[:, 1, :, NT], x1_first[:]))
            assert k == A0_DONE, k

            def a_powers(n, p):
                eng.wait_ge(ld_a[p], ld_value(n, p))
                for g in range(2):
                    if g:
                        after(eng, a_pe, "tok0", n)
                    else:
                        after(eng, a_pe, "tok1", n - 1)
                        if isinstance(n, int) and n == 0:
                            eng.wait_ge(su_pe, 1)
                    def step(f, name):
                        if name in ("vs", "vw"):
                            after(eng, a_vec, f"{'vt' if name == 'vs' else 'vu'}{g}", n)
                        if name == "vu":
                            after(eng, a_vec, f"vs{g}", n)
                        f().then_inc(*a_vec.step(f"{name}{g}"))
                    powers(step, p, 2 * g, 2, Vr, Vi, Vt)

            def a_center(n, p):
                after(eng, a_pe, "mean", n)
                after(eng, a_pe, "kvr2", n - 1)
                x = cur(xw[:, p]).rearrange("p (c b) t -> p c b t", c=CT)
                m = win1(bank[S_ST][:, 0:TOK]).unsqueeze(1).broadcast_to([P, CT, NB, NT])
                eng.tensor_tensor(xn[:].rearrange("p c (b t) -> p c b t", t=NT), x, m, ALU.subtract).then_inc(*a_vec.step("xc"))

            def a_norm(n, p):
                after(eng, a_act, "rstd", n)
                eng.tensor_tensor(xn[:], xn[:], both(rs1), ALU.mult).then_inc(*a_vec.step("xn"))
                after(eng, a_vec, "xn", n)
                for h in range(CT):
                    eng.tensor_scalar(xn[:, h], xn[:, h], col("g1", h), col("b1", h), ALU.mult,
                                      ALU.add).then_inc(*a_vec.step(f"xg{h}"))

            def a_mix(n, p):
                after(eng, a_act, "rp1", n)
                for j, (name, w, tm) in enumerate((("k", kw, "tmk"), ("v", vw, "tmv"), ("r", rw, "tmr"))):
                    after(eng, a_pe, f"kvr{j}", n)
                    for h in range(CT):
                        dst = cur(half(w[:], h))
                        eng.scalar_tensor_tensor(dst, win1(bank[S_A][:, h * TOK:(h + 1) * TOK]), col(tm, h), dst,
                                                 ALU.mult, ALU.add).then_inc(*a_vec.step(f"{name}{h}"))

            def flat(w):
                return w.rearrange("p l t -> p (l t)")

            def a_wkv(n, p):
                after(eng, a_vec, "x1", n - 1)
                eng.tensor_copy(kw[:, :, 0], mw[:, :, NT]).then_inc(*a_vec.step("mc"))
                after(eng, a_vec, "mc", n)
                eng.tensor_tensor_scan(flat(mw[:]), flat(wdec[:]), flat(kw[:]), 0.0, ALU.add, ALU.max).then_inc(*a_vec.step("m"))
                after(eng, a_vec, "m", n)
                for h in range(CT):
                    eng.scalar_tensor_tensor(cur(half(e1[:, 0], h)), prv(half(mw[:], h)), col("w", h), cur(half(mw[:], h)),
                                             ALU.add, ALU.subtract).then_inc(*a_vec.step(f"d1{h}"))
                after(eng, a_pe, "var", n)
                eng.tensor_tensor(cur(e2[:, 0]), cur(kw[:]), cur(mw[:]), ALU.subtract).then_inc(*a_vec.step("d2"))
                eng.tensor_copy(e2[:, 0, :, 0], sw[:, :, NT]).then_inc(*a_vec.step("sc"))
                after(eng, a_act, "d2", n)
                after(eng, a_vec, "sc", n)
                eng.tensor_tensor_scan(flat(sw[:]), flat(e1[:, 0]), flat(e2[:, 0]), 0.0, ALU.mult, ALU.add).then_inc(*a_vec.step("s"))
                after(eng, a_act, "lns", n)
                eng.tensor_tensor(t3[:], t3[:], mw[:], ALU.add).then_inc(*a_vec.step("bb"))
                after(eng, a_vec, "bb", n)
                for i, (name, s) in enumerate((("dl", lambda h: col("w", h)), ("gm", lambda h: negu[:, h:h + 1]))):
                    for h in range(CT):
                        eng.scalar_tensor_tensor(cur(half(e1[:, i], h)), prv(half(t3[:], h)), s(h), cur(half(kw[:], h)),
                                                 ALU.add, ALU.subtract).then_inc(*a_vec.step(f"{name}{h}"))
                after(eng, a_vec, "gm1", n)
                eng.tensor_scalar(cur(e2[:]), cur(e1[:]), 0.0, None, ALU.max).then_inc(*a_vec.step("mn"))
                after(eng, a_vec, "mn", n)
                eng.tensor_scalar(cur(e1[:]), cur(e1[:]), 0.0, None, ALU.min).then_inc(*a_vec.step("mx"))
                after(eng, a_act, "ef2", n)
                eng.tensor_tensor(cur(e2[:, 0]), cur(e2[:, 0]), cur(vw[:]), ALU.mult).then_inc(*a_vec.step("ev"))
                eng.tensor_copy(e2[:, 0, :, 0], aw[:, :, NT]).then_inc(*a_vec.step("ac"))
                after(eng, a_vec, "ac", n)
                eng.tensor_tensor_scan(flat(aw[:]), flat(e1[:, 0]), flat(e2[:, 0]), 0.0, ALU.mult, ALU.add).then_inc(*a_vec.step("aa"))
                eng.scalar_tensor_tensor(cur(t3[:]), cur(e1[:, 1]), WKV_EPS, cur(e2[:, 1]), ALU.add, ALU.add).then_inc(*a_vec.step("den"))
                after(eng, a_vec, "den", n)
                eng.tensor_tensor(cur(e1[:, 1]), cur(e1[:, 1]), prv(aw[:]), ALU.mult).then_inc(*a_vec.step("n1"))
                eng.tensor_tensor(cur(e2[:, 1]), cur(e2[:, 1]), cur(vw[:]), ALU.mult).then_inc(*a_vec.step("n2"))
                after(eng, a_vec, "n2", n)
                eng.tensor_tensor(cur(e1[:, 1]), cur(e1[:, 1]), cur(e2[:, 1]), ALU.add).then_inc(*a_vec.step("n3"))
                after(eng, a_act, "rden", n)
                after(eng, a_vec, "n3", n)
                eng.tensor_tensor(cur(e1[:, 1]), cur(e1[:, 1]), cur(t3[:]), ALU.mult).then_inc(*a_vec.step("y"))
                after(eng, a_act, "sig", n)
                after(eng, a_vec, "y", n)
                eng.tensor_tensor(cur(e1[:, 1]), cur(e1[:, 1]), cur(rw[:]), ALU.mult).then_inc(*a_vec.step("ry"))
                after(eng, a_vec, "ry", n)
                after(eng, b_pool, "xx", n - 2)
                after(eng, b_act, "rp1", n - 2)
                after(eng, a_vec, "x1s", n - 1)
                eng.tensor_tensor(cur(x1w[:, p]), cur(e1[:, 1]), cur(xw[:, p]), ALU.add).then_inc(*a_vec.step("x1"))
                eng.tensor_copy(x1w[:, p, :, 0], x1w[:, 1 - p, :, NT]).then_inc(*a_vec.step("x1s"))

            def b_center(n, p):
                after(eng, b_pe, "mean", n)
                after(eng, b_pe, "cm3", n - 1)
                x = cur(x1w[:, p]).rearrange("p (c b) t -> p c b t", c=CT)
                m = win1(bank[S_ST][:, 0:TOK]).unsqueeze(1).broadcast_to([P, CT, NB, NT])
                eng.tensor_tensor(xn2[:].rearrange("p c (b t) -> p c b t", t=NT), x, m, ALU.subtract).then_inc(*b_vec.step("xc"))

            def b_norm(n, p):
                after(eng, b_act, "rstd", n)
                eng.tensor_tensor(xn2[:], xn2[:], both(rsB), ALU.mult).then_inc(*b_vec.step("xn"))
                after(eng, b_vec, "xn", n)
                for h in range(CT):
                    eng.tensor_scalar(xn2[:, h], xn2[:, h], col("g2", h), col("b2", h), ALU.mult,
                                      ALU.add).then_inc(*b_vec.step(f"xg{h}"))
                after(eng, b_vec, "xg1", n)
                after(eng, b_act, "rp1", n)
                for h in range(CT):
                    eng.scalar_tensor_tensor(rr[:, h], xn2[:, h], col("cmr", h), rr[:, h], ALU.mult,
                                             ALU.add).then_inc(*b_vec.step(f"r{h}"))

            def b_relu(n, p, i):
                after(eng, b_pe, f"cm{i}", n)
                if i >= 2:
                    after(eng, b_pe, f"cp{i - 2}", n)
                for h in range(CT):
                    eng.scalar_tensor_tensor(kk[:, i % 2, h], bank[S_CM][:, h * TOK:(h + 1) * TOK], col("cmk", h), xpc[:, h],
                                             ALU.mult, ALU.add).then_inc(*b_vec.step(f"k{2 * i + h}"))
                after(eng, b_vec, f"k{2 * i + 1}", n)
                eng.scalar_tensor_tensor(kk[:, i % 2], kk[:, i % 2], 0.0, kk[:, i % 2], ALU.max,
                                         ALU.mult).then_inc(*b_vec.step(f"q{i}"))

            def b_res(n, p):
                after(eng, b_pe, "cp3", n)
                after(eng, b_act, "rr", n)
                eng.tensor_tensor(rr[:], bank[S_CP][:].rearrange("p (c n) -> p c n", c=CT), rr[:], ALU.mult).then_inc(*b_vec.step("rv"))
                after(eng, b_pool, "xx", n)
                after(eng, b_vec, "rv", n)
                eng.tensor_tensor(x2[:], x2[:], rr[:], ALU.add).then_inc(*b_vec.step("x2"))

            def b_norm3(n, p):
                after(eng, b_pe, "mean3", n)
                after(eng, b_pool, "sum3", n)
                eng.tensor_tensor(x2[:], x2[:], both(bank[S_ST][:, 0:TOK]), ALU.subtract).then_inc(*b_vec.step("xc3"))

            def b_out(n, p):
                after(eng, b_act, "rstd3", n)
                if not (isinstance(n, int) and n < 2):
                    eng.wait_ge(put_o[p], 8 * (n - p))
                eng.tensor_tensor(hres[:, p], x2[:], both(rsB), ALU.mult).then_inc(*b_vec.step("h"))

            def c_gate(n, p):
                after(eng, c_pe, "y", n - 1)
                for m in range(FT):
                    after(eng, c_act, f"s{m}", n)
                    eng.scalar_tensor_tensor(ha[:, m], bank[m % 4][:, TOK:2 * TOK], col("s2", m), sil[:, m % 2],
                                             ALU.mult, ALU.mult).then_inc(*c_vec.step(f"h{m}"))

            def c_res(n, p):
                after(eng, c_pe, "y", n)
                for h in range(CT):
                    eng.scalar_tensor_tensor(hres[:, p, h], bank[0][:, h * TOK:(h + 1) * TOK], col("s3", h), hres[:, p, h],
                                             ALU.mult, ALU.add).then_inc(*c_vec.step(f"y{h}"))

            def c_norm(n, p):
                after(eng, c_pe, "mean", n)
                after(eng, c_pool, "sum", n)
                eng.tensor_tensor(hres[:, p], hres[:, p], both(bank[S_ST][:, 0:TOK]), ALU.subtract).then_inc(*c_vec.step("xc"))
                after(eng, c_act, "rstd", n)
                eng.tensor_tensor(hres[:, p], hres[:, p], both(rs4[:]), ALU.mult).then_inc(*c_vec.step("o"))

            def stages(n, p):
                nonlocal k
                A, B, Cc = has("A", n), has("B", n), has("C", n)
                if isinstance(n, int) and n == CH:
                    after(eng, a_vec, "x1s", CH - 1)
                    did(eng.tensor_copy(x1w[:, 1, :, NT], x1_first[:]))
                    assert k == X1_FIXED
                if Cc:
                    c_gate(n - 2, p)
                if A:
                    a_powers(n, p)
                    a_center(n, p)
                    a_norm(n, p)
                    a_mix(n, p)
                    a_wkv(n, p)
                if B:
                    b_center(n - 1, 1 - p)
                    b_norm(n - 1, 1 - p)
                    for i in range(4):
                        b_relu(n - 1, 1 - p, i)
                    b_res(n - 1, 1 - p)
                if Cc:
                    c_res(n - 2, p)
                    c_norm(n - 2, p)
                if B:
                    b_norm3(n - 1, 1 - p)
                    b_out(n - 1, 1 - p)

            iterations(eng, stages)

        @block.tensor
        def _(eng):
            def mm(out_, w, x, start, stop, **kws):
                return eng.matmul(out_, w, x, start=start, stop=stop, **kws)

            eng.wait_ge(su_vec, V0_DONE)
            eng.wait_ge(su_pool, BD0_DONE)
            for h in range(CT):
                s = slice(h * P, (h + 1) * P)
                mm(bank[S_A][:, 64 * h:64 * h + 64], Vr[:, 0, s], bd[:, 0, 0], True, False)
                last = mm(bank[S_A][:, 64 * h:64 * h + 64], Vi[:, 0, s], bd[:, 0, 1], False, True)
            last.then_inc(su_pe, 1)
            eng.wait_ge(su_vec, HS0_DONE)
            mm(bank[S_ST][:, 0:NB], mean_w[:], hs1[:, 0:NB], True, True).then_inc(su_pe, 1)
            eng.wait_ge(su_vec, HQ0_DONE)
            mm(bank[S_ST][:, TOK:TOK + NB], mean_w[:], hs1[:, 0:NB], True, True).then_inc(su_pe, 1)
            eng.wait_ge(su_vec, XN0_DONE)
            eng.wait_ge(ld_tm, 16)
            for o in range(6):
                for c in range(CT):
                    last = mm(bank[S_A][:, o * NB:(o + 1) * NB], W_tm[:, c, o * P:(o + 1) * P], xn[:, c, 0:NB],
                              c == 0, c == CT - 1)
            last.then_inc(su_pe, 1)

            def a_tok(n, p):
                if isinstance(n, int) and n == 0:
                    eng.wait_ge(su_vec, A0_DONE)
                after(eng, a_pool, "bd3", n)
                after(eng, a_vec, "r1", n - 1)
                for g in range(2):
                    after(eng, a_vec, f"vw{g}", n)
                    for h in range(CT):
                        for q in range(2):
                            at = h * TOK + (2 * g + q) * 2 * NB
                            s = slice(h * P, (h + 1) * P)
                            mm(bank[S_A][:, at:at + 2 * NB], Vr[:, q, s], bd[:, 2 * g + q, 0], True, False)
                            last = mm(bank[S_A][:, at:at + 2 * NB], Vi[:, q, s], bd[:, 2 * g + q, 1], False, True)
                    last.then_inc(*a_pe.step(f"tok{g}"))

            def a_mean(n, p):
                after(eng, a_pool, "sum", n)
                if isinstance(n, int) and n < 2:
                    pass
                after(eng, b_act, "lnv3", n - 2)
                mm(bank[S_ST][:, 0:TOK], mean_w[:], hs1, True, True).then_inc(*a_pe.step("mean"))

            def a_var(n, p):
                after(eng, a_pool, "sum_sq", n)
                mm(bank[S_ST][:, TOK:2 * TOK], mean_w[:], hs1, True, True).then_inc(*a_pe.step("var"))

            def a_kvr(n, p, j):
                if j == 0:
                    after(eng, a_vec, "xg1", n)
                else:
                    after(eng, a_vec, ("k1", "v1")[j - 1], n)
                for h in range(CT):
                    o = CT * j + h
                    for c in range(CT):
                        last = mm(bank[S_A][:, h * TOK:(h + 1) * TOK], W_tm[:, c, o * P:(o + 1) * P], xn[:, c],
                                  c == 0, c == CT - 1)
                last.then_inc(*a_pe.step(f"kvr{j}"))

            def b_mean(n, p):
                after(eng, b_pool, "sum", n)
                if has("A", n + 1):
                    after(eng, a_act, "lnv", n + 1)
                if isinstance(n, int):
                    after(eng, b_act, "lnv3", n - 1)
                mm(bank[S_ST][:, 0:TOK], mean_w[:], hsB, True, True).then_inc(*b_pe.step("mean"))

            def b_var(n, p):
                after(eng, b_pool, "sum_sq", n)
                mm(bank[S_ST][:, TOK:2 * TOK], mean_w[:], hsB, True, True).then_inc(*b_pe.step("var"))

            def b_cm(n, p, i):
                if i == 0:
                    after(eng, b_vec, "xg1", n)
                    after(eng, b_vec, "k7", n - 1)
                else:
                    after(eng, b_vec, f"k{2 * i - 1}", n)
                for h in range(2):
                    o = 2 * i + h
                    for c in range(CT):
                        last = mm(bank[S_CM][:, h * TOK:(h + 1) * TOK], W_cm[:, c, o * P:(o + 1) * P], xn2[:, c],
                                  c == 0, c == CT - 1)
                last.then_inc(*b_pe.step(f"cm{i}"))

            def b_cp(n, p, i):
                after(eng, b_vec, f"q{i}", n)
                if i == 0:
                    after(eng, b_vec, "rv", n - 1)
                for j in range(2):
                    for h in range(CT):
                        first = i == 0 and j == 0
                        last = mm(bank[S_CP][:, h * TOK:(h + 1) * TOK], W_cp[:, 2 * i + j, h * P:(h + 1) * P],
                                  kk[:, i % 2, j], first and h == 0, i == 3 and j == 1, skip_group_check=True)
                last.then_inc(*b_pe.step(f"cp{i}"))

            def b_mean3(n, p):
                after(eng, b_pool, "sum3", n)
                if has("C", n + 1):
                    after(eng, c_act, "lnv", n - 1)
                mm(bank[S_ST][:, 0:TOK], mean_w[:], hsB, True, True).then_inc(*b_pe.step("mean3"))

            def b_var3(n, p):
                after(eng, b_pool, "sum_sq3", n)
                mm(bank[S_ST][:, TOK:2 * TOK], mean_w[:], hsB, True, True).then_inc(*b_pe.step("var3"))

            def c_w12(n, p):
                after(eng, b_vec, "h", n)
                for m in range(FT):
                    if m >= 4:
                        after(eng, c_vec, f"h{m - 4}", n)
                    elif m == 0:
                        after(eng, c_vec, "y1", n - 1)
                    else:
                        after(eng, c_act, f"g2{2 * m + 1}", n - 1)
                    for j, w in enumerate((W_1, W_2)):
                        for c in range(CT):
                            last = mm(bank[m % 4][:, j * TOK:(j + 1) * TOK], w[:, c, m * P:(m + 1) * P], hres[:, p, c],
                                      c == 0, c == CT - 1)
                    last.then_inc(*c_pe.step(f"w{m}"))

            def c_h(n, p, layer, i):
                w, src = (W_h1, ha) if layer == 1 else (W_h2, hb)
                if layer == 1:
                    after(eng, c_vec, f"h{4 + i}", n)
                else:
                    after(eng, c_act, f"g1{2 * i + 1}", n)
                for j in range(2):
                    o = 2 * i + j
                    for c in range(FT):
                        if i == 0 and j == 0:
                            if layer == 1:
                                after(eng, c_vec, f"h{c}", n)
                            else:
                                after(eng, c_act, f"g1{c}", n)
                        last = mm(bank[i][:, j * TOK:(j + 1) * TOK], w[:, c, o * P:(o + 1) * P], src[:, c],
                                  c == 0, c == FT - 1)
                last.then_inc(*c_pe.step(f"h{layer}{i}"))

            def c_y(n, p):
                after(eng, c_act, "g21", n)
                for h in range(CT):
                    for c in range(FT):
                        if h == 0:
                            after(eng, c_act, f"g2{c}", n)
                        last = mm(bank[0][:, h * TOK:(h + 1) * TOK], W_3[:, c, h * P:(h + 1) * P], ha[:, c],
                                  c == 0, c == FT - 1)
                last.then_inc(*c_pe.step("y"))

            def c_mean(n, p):
                after(eng, c_pool, "sum", n)
                if has("B", n + 2):
                    after(eng, b_act, "lnv", n + 1)
                else:
                    after(eng, b_act, "lnv3", n)
                mm(bank[S_ST][:, 0:TOK], mean_w[:], hs4[:], True, True).then_inc(*c_pe.step("mean"))

            def c_var(n, p):
                after(eng, c_pool, "sum_sq", n)
                mm(bank[S_ST][:, TOK:2 * TOK], mean_w[:], hs4[:], True, True).then_inc(*c_pe.step("var"))

            def stages(n, p):
                A, B, Cc = has("A", n), has("B", n), has("C", n)
                if isinstance(n, int) and n == 1:
                    eng.wait_ge(ld_cm, 32)
                if isinstance(n, int) and n == 1:
                    eng.wait_ge(ld_ff, 80)
                a, b, c = (n, p), (n - 1, 1 - p), (n - 2, p)
                if Cc:
                    c_w12(*c)
                if A:
                    a_tok(*a)
                    a_mean(*a)
                if Cc:
                    c_h(*c, 1, 0)
                    c_h(*c, 1, 1)
                if A:
                    a_var(*a)
                if Cc:
                    c_h(*c, 1, 2)
                    c_h(*c, 1, 3)
                if A:
                    a_kvr(*a, 0)
                    a_kvr(*a, 1)
                    a_kvr(*a, 2)
                if B:
                    b_mean(*b)
                if Cc:
                    c_h(*c, 2, 0)
                if B:
                    b_var(*b)
                if Cc:
                    c_h(*c, 2, 1)
                if B:
                    b_cm(*b, 0)
                if Cc:
                    c_h(*c, 2, 2)
                if B:
                    b_cm(*b, 1)
                    b_cp(*b, 0)
                if Cc:
                    c_h(*c, 2, 3)
                if B:
                    b_cm(*b, 2)
                    b_cp(*b, 1)
                if Cc:
                    c_y(*c)
                if B:
                    b_cm(*b, 3)
                    b_cp(*b, 2)
                    b_cp(*b, 3)
                if Cc:
                    c_mean(*c)
                    c_var(*c)
                if B:
                    b_mean3(*b)
                    b_var3(*b)

            iterations(eng, stages)


def ld_value(n, p):
    return 32 * ((n - p) // 2 + 1) + 16 * p if isinstance(n, int) else 16 * (n - p) + 32 + 16 * p


BM_DONE = 2
CB0_DONE = 6
BD0_DONE = 8
X0_DONE, SQ0_DONE, RS0_DONE, SG0_DONE = 1, 2, 4, 5
_Z = BM_DONE + 5 + 1 + 9 + 6 + 1 + 11 + 28
TG_DONE = [_Z + 21, _Z + 43, _Z + 64, _Z + 85]
V0_DONE = TG_DONE[3] + 3 + 9 + 6
HS0_DONE = V0_DONE + 1
XC0_DONE = HS0_DONE + 1
HQ0_DONE = XC0_DONE + 1
XN0_DONE = HQ0_DONE + 3
R0_DONE = XN0_DONE + 12
A0_DONE = R0_DONE + 4
X1_FIXED = A0_DONE + 1


def kernel(**inputs):
    import numpy as np
    import concourse.bacc as bacc
    from concourse.bass_utils import run_bass_kernel_spmd

    a = {k: np.asarray(v) for k, v in inputs.items()}

    def turned(v, axis):
        return np.roll(v, -1, axis=axis)

    def modes(v):
        v = turned(v, 0).reshape(QP, 2, NS, -1)
        return np.ascontiguousarray(v.transpose(1, 2, 0, 3).reshape(P, QP, -1))

    def tiles(w):
        return np.ascontiguousarray(w.reshape(-1, P, w.shape[1]).transpose(1, 0, 2))

    x = turned(a["x"], 1).reshape(NB, CH, QC, 2, NS, 2)
    c_in = np.ascontiguousarray(x.transpose(1, 3, 4, 2, 5, 0).reshape(CH, P, QC * 2 * NB))
    cols = {"w": "attn_time_decay", "u": "attn_time_first", "tmk": "attn_tmk", "tmv": "attn_tmv", "tmr": "attn_tmr",
            "g1": "attn_g1", "b1": "attn_b1", "g2": "attn_g2", "b2": "attn_b2", "cmk": "attn_cmk", "cmr": "attn_cmr",
            "s1": "ffn_w1_s", "s2": "ffn_w2_s", "sh1": "ffn_h1_s", "sh2": "ffn_h2_s", "s3": "ffn_w3_s"}
    par = np.ascontiguousarray(np.concatenate([a["L0_" + cols[k]].reshape(-1, P).T for k in COLS], axis=1))
    arrays = {
        "c_in": c_in,
        "log_dt": np.ascontiguousarray(turned(a["L0_tok_log_dt"], 0).reshape(QP, 2).T),
        "a_re": modes(a["L0_tok_inv_A_real"])[:, :, 0].copy(),
        "a_im": modes(a["L0_tok_A_imag"])[:, :, 0].copy(),
        "b_ri": modes(a["L0_tok_B_ri"]),
        "par": par,
        "w_tm": tiles(a["L0_attn_W_tm"]),
        "w_cm": tiles(a["L0_attn_W_cm"]),
        "w_cp": tiles(a["L0_attn_W_cp"]),
        "w1": tiles(a["L0_ffn_w1_w"].T),
        "w2": tiles(a["L0_ffn_w2_w"].T),
        "h1": tiles(a["L0_ffn_h1_w"].T),
        "h2": tiles(a["L0_ffn_h2_w"].T),
        "w3": tiles(a["L0_ffn_w3_w"].T),
    }
    nc = bacc.Bacc("TRN2", target_bir_lowering=False, num_devices=1)
    args = [nc.dram_tensor(k, v.shape, F32, kind="ExternalInput").ap() for k, v in arrays.items()]
    args.append(nc.dram_tensor("out", (CH, P, CT * TOK), F32, kind="ExternalOutput").ap())
    args.append(nc.dram_tensor("tpq", (CH, P, 2 * HX), F32, kind="Internal").ap())
    build(nc, *args)
    got = run_bass_kernel_spmd(nc, [arrays], core_ids=[0]).results[0]["out"]
    got = np.asarray(got).reshape(CH, P, CT, NB, NT).transpose(3, 0, 4, 2, 1).reshape(NB, T, C)
    return np.ascontiguousarray(np.roll(got, 1, axis=1))
```

```python
from contextlib import ExitStack

import concourse.bass as bass
from concourse import mybir

F32 = mybir.dt.float32
I32 = mybir.dt.int32
F32R = mybir.dt.float32r
ALU = mybir.AluOpType
ACT = mybir.ActivationFunctionType

P = 128
NB = 32
T = 256
C = 256
NS = 64
F = 1024
NT = 8
CH = T // NT
TOK = NB * NT
CT = C // P
FT = F // P
LN = CT * NB
W9 = NT + 1
QP = T // 2
QC = NT // 2
QG = 32
HX = QC * 2 * 16
R16 = 16
LN_EPS = 1e-5
WKV_EPS = 1e-8
NEG_INF = -1e38
LN_EXP = 6
SPLIT = 12
PIECE = 1024
NPIECE = 22
NLO = 88
LO_H1, LO_H2, LO_W3 = 16, 48, 80

COLS = {}
for _name, _n in (("w", CT), ("u", CT), ("tmk", CT), ("tmv", CT), ("tmr", CT), ("g1", CT), ("b1", CT),
                  ("g2", CT), ("b2", CT), ("cmk", CT), ("cmr", CT), ("s1", FT), ("s2", FT), ("sh1", FT),
                  ("sh2", FT), ("s3", CT)):
    COLS[_name] = (sum(n for _, n in COLS.values()), _n)
NCOL = sum(n for _, n in COLS.values())


class Line:

    def __init__(self, sem, steps):
        self.sem, self.steps, self.at = sem, steps, 0

    def step(self, name):
        assert self.steps[self.at] == name, (self.steps[self.at], name)
        self.at = (self.at + 1) % len(self.steps)
        return self.sem, 1

    def value(self, name, n):
        return len(self.steps) * n + self.steps.index(name) + 1


def after(eng, line, name, n):
    if not (isinstance(n, int) and n < 0):
        eng.wait_ge(line.sem, line.value(name, n))


def build(nc, c_in, log_dt, a_re, a_im, b_ri, par, w_tm, w_cs, w1, w2, h1, h2, w3, out, tpq, wlo):
    ctx = ExitStack()
    with ctx:
        def sb(name, shape, dt=F32, stack=ctx):
            return stack.enter_context(nc.sbuf_tensor(name, shape, dt))

        def sem(name):
            return ctx.enter_context(nc.semaphore(name))

        W_tm = sb("W_tm", [P, CT, 3 * C])
        W_1 = sb("W_1", [P, CT, F], F32R)
        W_2 = sb("W_2", [P, CT, F], F32R)
        W_h1 = sb("W_h1", [P, FT, F], F32R)
        W_h2 = sb("W_h2", [P, FT, F], F32R)
        W_3 = sb("W_3", [P, FT, C], F32R)
        wcs = sb("wcs", [P, 2, 2, 2 * C])
        prm = sb("prm", [P, NCOL])
        onem = sb("onem", [P, 5 * CT])
        negu = sb("negu", [P, CT])
        mean_w = sb("mean_w", [P, P])
        eps_c = sb("eps_c", [P, 2])
        wdec = sb("wdec", [P, LN, W9])
        bmode = sb("bmode", [P, QP, 2])
        x1_first = sb("x1_first", [P, LN])

        cin = sb("cin", [P, QC, 2, NB])
        pq = sb("pq", [P, 2, QC, 2, R16])
        cbt = sb("cbt", [P, 2, QC, 2, NB])
        bd = sb("bd", [P, QC, 2, 2 * NB])
        Vr = sb("Vr", [P, 2, C])
        Vi = sb("Vi", [P, 2, C])
        Vt = sb("Vt", [P, 2, C])
        xn = sb("xn", [P, CT, TOK])
        xw = sb("xw", [P, 2, LN, W9])
        x1w = sb("x1w", [P, 2, LN, W9])
        xn2 = sb("xn2", [P, CT, TOK])
        x2 = sb("x2", [P, CT, TOK])
        rr = sb("rr", [P, CT, TOK])
        xpc = sb("xpc", [P, CT, TOK])
        kk = sb("kk", [P, 2, 2, TOK])
        hres = sb("hres", [P, 2, CT, TOK])
        hx = sb("hx", [P, 2, CT, TOK], F32R)
        ha = sb("ha", [P, 3, 2, TOK], F32R)
        sil = sb("sil", [P, 2, TOK])
        gt = sb("gt", [P, 2, TOK])
        hs4 = sb("hs4", [P, TOK])
        rs4 = sb("rs4", [P, TOK])
        flag = sb("flag", [P, NPIECE + 2])
        flag_i = sb("flag_i", [P, 1], I32)
        lo_w = sb("lo_w", [P, C], F32R)
        staging = ExitStack()
        st = sb("st", [P, 2, PIECE], stack=staging)
        sl = sb("sl", [P, 2, PIECE], F32R, stack=staging)
        staging.close()
        hb = sb("hb", [P, 2, FT, TOK], F32R)

        setup = ExitStack()
        EX = sb("EX", [P, 2, QP], stack=setup)
        EN = sb("EN", [P, 2, QP], stack=setup)
        EQ = sb("EQ", [P, 2, QP], stack=setup)
        EI = sb("EI", [P, 2, QP], I32, stack=setup)
        aim = sb("aim", [P, QP], stack=setup)
        Z = sb("Z", [P, 2, QP, 2, 4], stack=setup)
        zt = sb("zt", [P, 2, 2 * QG, 8], stack=setup)
        tg = sb("tg", [P, 2, QG, 2, R16], stack=setup)
        setup.close()
        kw = sb("kw", [P, LN, W9])
        vw = sb("vw", [P, LN, W9])
        rw = sb("rw", [P, LN, W9])
        mw = sb("mw", [P, LN, W9])
        sw = sb("sw", [P, LN, W9])
        aw = sb("aw", [P, LN, W9])
        e1 = sb("e1", [P, 2, LN, W9])
        e2 = sb("e2", [P, 2, LN, W9])
        t3 = sb("t3", [P, LN, W9])

        bank = [ctx.enter_context(nc.psum_tensor(f"bank{i}", [P, 512], F32)) for i in range(8)]
        S_ST, S_CP, S_A, S_G = 4, 5, 6, 7
        S_CM = S_A

        def col(name, k=0):
            at = COLS[name][0] + k
            return prm[:, at:at + 1]

        def one_minus(name, k):
            at = CT * ("tmk", "tmv", "tmr", "cmk", "cmr").index(name) + k
            return onem[:, at:at + 1]

        def cur(w):
            return w[..., 1:W9]

        def prv(w):
            return w[..., 0:NT]

        def half(w, h):
            return w[:, h * NB:(h + 1) * NB, :]

        def win(flat):
            return flat.rearrange("p c (b t) -> p (c b) t", t=NT)

        def win1(flat):
            return flat.rearrange("p (b t) -> p b t", t=NT)

        def both(ap):
            return ap.unsqueeze(1).broadcast_to([P, CT, TOK])

        def grid(v, n=2):
            return v[:, 0:n].rearrange("p q (a b) -> p q a b", b=R16)

        def power(q0, ri, s, n=2):
            v = pq[:, ri, q0:q0 + n, s]
            return (v.unsqueeze(3) if s else v.unsqueeze(2)).broadcast_to([P, n, R16, R16])

        def split_to(u, part):
            return hb[:, part, u - 8] if 8 <= u < 16 else ha[:, u % 8 % 3, part]

        def gt_free(eng, n, u):
            if u >= 2:
                after(eng, c_pool, f"l{u - 2}", n)
            else:
                after(eng, c_pool, "sum_sq", n - 1)

        lnA = t3[:].rearrange("p l t -> p (l t)")
        hs1, rs1 = lnA[:, 0:TOK], lnA[:, TOK:2 * TOK]
        sq1 = e2[:, 1].rearrange("p l t -> p (l t)")[:, 0:CT * TOK].rearrange("p (c n) -> p c n", c=CT)
        sqB = kk[:, 0]
        hsB, rsB = kk[:, 1, 0], kk[:, 1, 1]

        ld_w = sem("ld_w")
        ld_tm = sem("ld_tm")
        ld_a = sem("ld_a")
        ld_s = [sem("ld_s0"), sem("ld_s1")]
        ld_p = [sem("ld_p0"), sem("ld_p1")]
        put_l = [sem("put_l0"), sem("put_l1")]
        w_hi = sem("w_hi")
        w_lo = sem("w_lo")
        w_nz = sem("w_nz")
        fl_sum = sem("fl_sum")
        fl_set = sem("fl_set")
        lo_in = sem("lo_in")
        lo_used = sem("lo_used")
        put_t = sem("put_t")
        put_o = [sem("put_o0"), sem("put_o1")]
        su_vec = sem("su_vec")
        su_pool = sem("su_pool")
        su_act = sem("su_act")
        su_pe = sem("su_pe")

        g_pool = Line(sem("g_pool"), ["cb_re", "cb_im", "bd0", "bd1", "bd2", "bd3", "vt0", "vu0", "vt1", "vu1"])
        g_vec = Line(sem("g_vec"), [f"{s}{g}" for g in range(2) for s in ("vr", "vs", "vi", "vw")])
        a_pool = Line(sem("a_pool"), ["sum", "sum_sq"])
        a_pe = Line(sem("a_pe"), ["tok0", "tok1", "mean", "var", "kvr0", "kvr1", "kvr2"])
        a_act = Line(sem("a_act"), ["x_slot", "x", "sq", "kp0", "kp1", "vp0", "vp1", "rp0", "rp1", "lnv", "rstd",
                                    "sig", "d1", "d2", "lns", "ef1", "ef2", "lnd", "rden"])
        a_vec = Line(sem("a_vec"), ["xc", "xn", "xg0", "xg1", "k0", "k1", "v0", "v1", "r0", "r1",
                                    "mc", "m", "d10", "d11", "d2", "sc", "s", "bb", "dl0", "dl1", "gm0", "gm1",
                                    "mn", "mx", "ev", "ac", "aa", "den", "n1", "n2", "n3", "y", "ry", "x1", "x1s"])
        b_pool = Line(sem("b_pool"), ["sum", "sum_sq", "xx", "sum3", "sum_sq3"])
        b_pe = Line(sem("b_pe"), ["mean", "var", "cm0", "cm1", "cp0", "cm2", "cp1", "cm3", "cp2", "cp3",
                                  "mean3", "var3"])
        b_act = Line(sem("b_act"), ["sq", "kp0", "kp1", "rp0", "rp1", "lnv", "rstd", "rr", "sq3", "lnv3", "rstd3"])
        b_vec = Line(sem("b_vec"), ["xc", "xn", "xg0", "xg1", "r0", "r1"]
                     + [s for i in range(4) for s in (f"k{2*i}", f"k{2*i+1}", f"q{i}")]
                     + ["rv", "x2", "xc3", "h", "hi", "lo"])
        c_pool = Line(sem("c_pool"), [f"l{u}" for u in range(24)] + ["sum", "sum_sq"])
        c_pe = Line(sem("c_pe"), ["w0"] + [s for m in range(7) for s in (f"w{m+1}", f"k{m}")] + ["k7"]
                    + ["h20", "h21", "y0", "y1", "h22", "y2", "y3", "h23", "y4", "y5", "y6", "y7", "mean", "var"])
        c_act = Line(sem("c_act"), [f"s{m}" for m in range(8)] + [f"g1{m}" for m in range(8)]
                     + [f"g2{m}" for m in range(8)] + ["sq", "lnv", "rstd"])
        c_vec = Line(sem("c_vec"), [s for m in range(8) for s in (f"g{m}", f"i{m}")] + [f"i{u}" for u in range(8, 24)]
                     + ["y0", "y1", "xc", "o"])

        block = ctx.enter_context(nc.Block())


        def iterations(eng, stages):
            for n in range(4):
                stages(n, n % 2)
            with eng.Fori(4, CH - 3, 2) as n:
                stages(n, 0)
                stages(n + 1, 1)
            for n in range(CH - 2, CH + 2):
                stages(n, n % 2)

        def has(stage, n):
            lag = "ABC".index(stage)
            return not isinstance(n, int) or 0 <= n - lag < CH

        def chunk(dram, n):
            return dram[bass.ds(n, 1)].rearrange("o p x -> (o p) x")

        pieces = []
        for j, (w, W) in enumerate(((w1, W_1), (w2, W_2))):
            for c in range(CT):
                pieces.append((w[:, c], W[:, c],
                               wlo[c:LO_H1:2, :, j * P:(j + 1) * P].rearrange("m p x -> p m x"), P))
        for c in range(FT):
            pieces.append((h1[:, c], W_h1[:, c],
                           wlo[LO_H1 + 4 * c:LO_H1 + 4 * c + 4].rearrange("m p x -> p m x"), C))
        for c in range(FT):
            pieces.append((h2[:, c], W_h2[:, c], wlo[LO_H2 + c:LO_W3:FT].rearrange("m p x -> p m x"), C))
        for j in range(2):
            s = slice(4 * j, 4 * j + 4)
            pieces.append((w3[:, s].rearrange("p k x -> p (k x)"), W_3[:, s].rearrange("p k x -> p (k x)"),
                           wlo[LO_W3 + 4 * j:LO_W3 + 4 * j + 4].rearrange("m p x -> p m x"), C))
        assert len(pieces) == NPIECE

        def pieces_of(n):
            half = NPIECE // 2
            return range(half * n, half * n + half) if isinstance(n, int) and n < 2 else ()

        def low_blocks(step):
            if step[0] == "w":
                return [2 * int(step[1]) + c for c in range(CT)]
            if step[0] == "k":
                return [LO_H1 + 4 * int(step[1]) + i for i in range(4)]
            if step[0] == "h":
                return [LO_H2 + 8 * int(step[2]) + c for c in range(FT)]
            return [LO_W3 + int(step[1])]

        low_at, low_list = {}, []
        for step in c_pe.steps[:-2]:
            low_at[step] = len(low_list)
            low_list += low_blocks(step)
        assert sorted(low_list) == list(range(NLO))

        @block.sync
        def _(eng):
            eng.dma_start(prm[:], par).then_inc(ld_w, 16)
            eng.dma_start(EX[0:NS, 0, :], log_dt[0:1, :].broadcast_to([NS, QP])).then_inc(ld_w, 16)
            eng.dma_start(EX[NS:P, 0, :], log_dt[1:2, :].broadcast_to([NS, QP])).then_inc(ld_w, 16)
            eng.dma_start(EX[:, 1, :], a_re).then_inc(ld_w, 16)
            eng.dma_start(aim[:], a_im).then_inc(ld_w, 16)
            eng.dma_start(bmode[:], b_ri).then_inc(ld_w, 16)
            eng.dma_start(cin[:].rearrange("p q r b -> p (q r b)"), c_in[CH - 1]).then_inc(ld_a, 16)
            eng.dma_start(W_tm[:], w_tm).then_inc(ld_tm, 16)
            for i, g in enumerate((3, 0, 1, 2)):
                eng.wait_ge(su_vec, TG_DONE[i])
                for ri in range(2):
                    eng.dma_start(tpq[8 * g:8 * g + 8, :, ri * HX:(ri + 1) * HX].rearrange("n p x -> p n x"),
                                  tg[:, ri].rearrange("p (n q) s r -> p n (q s r)", n=8)).then_inc(put_t, 16)
            eng.wait_ge(put_t, 128)

            def load_a(n):
                after(eng, g_pool, "vu1", n - 1)
                after(eng, g_vec, "vw1", n - 1)
                eng.dma_start(cin[:].rearrange("p q r b -> p (q r b)"), chunk(c_in, n)).then_inc(ld_a, 16)
                eng.dma_start(pq[:].rearrange("p r q s l -> p (r q s l)"), chunk(tpq, n)).then_inc(ld_a, 16)

            def load_s(n, i):
                if i >= 2:
                    after(eng, b_pe, f"cp{i - 2}", n)
                else:
                    after(eng, b_pe, f"cp{i + 2}", n - 1)
                eng.dma_start(wcs[:, i % 2].rearrange("p m x -> p (m x)"), w_cs[i]).then_inc(ld_s[i % 2], 16)

            def load_piece(i):
                if i >= 2:
                    eng.wait_ge(w_lo, i - 1)
                eng.dma_start(st[:, i % 2], pieces[i][0]).then_inc(ld_p[i % 2], 16)

            def store_piece(i):
                eng.wait_ge(w_lo, i + 1)
                dst, wid = pieces[i][2:]
                eng.dma_start(dst, sl[:, i % 2].bitcast(F32).rearrange("p (m x) -> p m x", x=wid)).then_inc(put_l[i % 2], 16)

            def send_low(n, flag_reg, steps):
                with eng.If(flag_reg):
                    for step in steps:
                        for j, b in enumerate(low_blocks(step)):
                            pos = low_at[step] + j
                            if not (isinstance(n, int) and NLO * n + pos == 0):
                                eng.wait_ge(lo_used, NLO * n + pos)
                            eng.dma_start(lo_w[:].bitcast(F32), wlo[b]).then_inc(lo_in, 16)

            eng.wait_ge(su_vec, V0_DONE)
            eng.wait_ge(su_pool, CB0_DONE)
            load_a(0)
            flag_reg = None

            def stages(n, p):
                nonlocal flag_reg
                if has("A", n) and (not isinstance(n, int) or n + 1 < CH):
                    load_a(n + 1)
                if has("B", n):
                    load_s(n - 1, 0)
                    load_s(n - 1, 1)
                if isinstance(n, int) and n == 2:
                    for q in range(2):
                        eng.wait_ge(put_l[q], 8 * NPIECE)
                    eng.wait_ge(fl_set, 1)
                    flag_reg = eng.value_load(flag_i[0:1, 0:1], min_val=0, max_val=1)
                if has("C", n):
                    send_low(n - 2, flag_reg, c_pe.steps[:c_pe.steps.index("h21")])
                if has("B", n):
                    load_s(n - 1, 2)
                if has("C", n):
                    send_low(n - 2, flag_reg, ["h21"])
                if has("B", n):
                    load_s(n - 1, 3)
                if has("C", n):
                    send_low(n - 2, flag_reg, c_pe.steps[c_pe.steps.index("y0"):-2])
                    after(eng, c_vec, "o", n - 2)
                    eng.dma_start(chunk(out, n - 2), hres[:, p].rearrange("p c n -> p (c n)")).then_inc(put_o[p], 16)
                for i in pieces_of(n):
                    load_piece(i)
                    if i >= 1:
                        store_piece(i - 1)
                    if i == NPIECE - 1:
                        store_piece(i)

            iterations(eng, stages)
            for p in range(2):
                eng.wait_ge(put_o[p], 8 * CH)

        @block.gpsimd
        def _(eng):
            k = 0

            def did(ins):
                nonlocal k
                k += 1
                ins.then_inc(su_pool, 1)

            did(eng.memset(mean_w[:], 1.0 / C))
            did(eng.memset(eps_c[:, 0:1], LN_EPS))
            did(eng.memset(eps_c[:, 1:2], WKV_EPS))
            did(eng.memset(bd[:], 0.0))
            eng.wait_ge(su_vec, BM_DONE)
            eng.wait_ge(ld_a, 16)
            q = QP - 1
            qc = QC - 1
            did(eng.tensor_tensor(cbt[:, 0, 0], cin[:, qc], bmode[:, q, 0:1].unsqueeze(2).broadcast_to([P, 2, NB]), ALU.mult))
            did(eng.tensor_tensor(cbt[:, 1, 0], cin[:, qc], bmode[:, q, 1:2].unsqueeze(2).broadcast_to([P, 2, NB]), ALU.mult))
            assert k == CB0_DONE
            eng.wait_ge(su_pool, k)
            s = slice(NS, P)
            did(eng.tensor_tensor(bd[s, 0, 0, NB:], cbt[s, 0, 0, 0], cbt[s, 1, 0, 1], ALU.add))
            did(eng.tensor_tensor(bd[s, 0, 1, NB:], cbt[s, 1, 0, 0], cbt[s, 0, 0, 1], ALU.subtract))
            assert k == BD0_DONE

            def g_modes(n):
                bre = bmode[:, bass.ds(QC * n, QC), 0:1]
                bim = bmode[:, bass.ds(QC * n, QC), 1:2]
                eng.wait_ge(ld_a, 16 + 32 * (n + 1))
                if isinstance(n, int) and n == 0:
                    eng.wait_ge(su_pool, BD0_DONE)
                after(eng, g_pool, "bd3", n - 1)
                eng.tensor_tensor(cbt[:, 0], cin[:], bre.unsqueeze(3).broadcast_to([P, QC, 2, NB]),
                                  ALU.mult).then_inc(*g_pool.step("cb_re"))
                eng.tensor_tensor(cbt[:, 1], cin[:], bim.unsqueeze(3).broadcast_to([P, QC, 2, NB]),
                                  ALU.mult).then_inc(*g_pool.step("cb_im"))
                after(eng, g_pool, "cb_im", n)
                after(eng, a_pe, "tok1", n - 1)
                if isinstance(n, int) and n == 0:
                    eng.wait_ge(su_pe, 1)
                for t in range(2):
                    s = slice(t * NS, (t + 1) * NS)
                    eng.tensor_tensor(bd[s, :, 0, t * NB:(t + 1) * NB], cbt[s, 0, :, 0], cbt[s, 1, :, 1],
                                      ALU.add).then_inc(*g_pool.step(f"bd{2 * t}"))
                    eng.tensor_tensor(bd[s, :, 1, t * NB:(t + 1) * NB], cbt[s, 1, :, 0], cbt[s, 0, :, 1],
                                      ALU.subtract).then_inc(*g_pool.step(f"bd{2 * t + 1}"))
                after(eng, g_pool, "bd3", n)

            def g_powers(n, g):
                if g == 0:
                    after(eng, g_vec, "vw1", n - 1)
                    if isinstance(n, int) and n == 0:
                        eng.wait_ge(su_vec, V0_DONE)
                else:
                    after(eng, g_vec, "vw0", n)
                eng.tensor_tensor(grid(Vt), power(2 * g, 1, 1), power(2 * g, 1, 0), ALU.mult).then_inc(*g_pool.step(f"vt{g}"))
                after(eng, g_vec, f"vs{g}", n)
                eng.tensor_tensor(grid(Vt), power(2 * g, 1, 1), power(2 * g, 0, 0), ALU.mult).then_inc(*g_pool.step(f"vu{g}"))

            def a_sum(n, p):
                after(eng, a_act, "x", n)
                after(eng, a_vec, "y", n - 1)
                if isinstance(n, int) and n == 0:
                    eng.wait_ge(su_vec, A0_DONE)
                eng.tensor_tensor(win1(hs1), cur(half(xw[:, p], 0)), cur(half(xw[:, p], 1)),
                                  ALU.add).then_inc(*a_pool.step("sum"))

            def a_sum_sq(n, p):
                after(eng, a_act, "sq", n)
                after(eng, a_pe, "mean", n)
                eng.tensor_tensor(hs1, sq1[:, 0], sq1[:, 1], ALU.add).then_inc(*a_pool.step("sum_sq"))

            def b_sum(n, p):
                after(eng, a_vec, "x1s", n)
                if isinstance(n, int) and n == CH - 1:
                    eng.wait_ge(su_vec, X1_FIXED)
                after(eng, b_vec, "h", n - 1)
                eng.tensor_tensor(win1(hsB), cur(half(x1w[:, p], 0)), cur(half(x1w[:, p], 1)),
                                  ALU.add).then_inc(*b_pool.step("sum"))

            def b_sum_sq(n, p):
                after(eng, b_act, "sq", n)
                after(eng, b_pe, "mean", n)
                eng.tensor_tensor(hsB, sqB[:, 0], sqB[:, 1], ALU.add).then_inc(*b_pool.step("sum_sq"))

            def b_xx(n, p):
                after(eng, b_vec, "lo", n - 1)
                eng.tensor_tensor(win(x2[:]), cur(xw[:, p]), cur(x1w[:, p]), ALU.add).then_inc(*b_pool.step("xx"))

            def b_sum3(n, p):
                after(eng, b_vec, "x2", n)
                after(eng, b_pe, "cp3", n)
                eng.tensor_tensor(hsB, x2[:, 0], x2[:, 1], ALU.add).then_inc(*b_pool.step("sum3"))

            def b_sum_sq3(n, p):
                after(eng, b_act, "sq3", n)
                after(eng, b_pe, "mean3", n)
                eng.tensor_tensor(hsB, sqB[:, 0], sqB[:, 1], ALU.add).then_inc(*b_pool.step("sum_sq3"))

            def c_low(n, u):
                after(eng, c_vec, f"i{u}", n)
                eng.tensor_tensor(split_to(u, 1), gt[:, u % 2], split_to(u, 0), ALU.subtract).then_inc(*c_pool.step(f"l{u}"))

            def c_sum(n, p):
                after(eng, c_vec, "y1", n)
                after(eng, c_pe, "var", n - 1)
                eng.tensor_tensor(hs4[:], hres[:, p, 0], hres[:, p, 1], ALU.add).then_inc(*c_pool.step("sum"))

            def c_sum_sq(n, p):
                after(eng, c_act, "sq", n)
                after(eng, c_pe, "mean", n)
                eng.tensor_tensor(hs4[:], gt[:, 0], gt[:, 1], ALU.add).then_inc(*c_pool.step("sum_sq"))

            def low_piece(i):
                eng.wait_ge(w_hi, i + 1)
                if i >= 2:
                    eng.wait_ge(put_l[i % 2], 16 * (i // 2))
                    eng.wait_ge(w_nz, i - 1)
                eng.tensor_tensor(sl[:, i % 2], st[:, i % 2], pieces[i][1], ALU.subtract).then_inc(w_lo, 1)

            g_modes(0)
            g_powers(0, 0)

            def stages(n, p):
                A, B, Cc = has("A", n), has("B", n), has("C", n)
                more = A and (not isinstance(n, int) or n + 1 < CH)
                a, b, c = (n, p), (n - 1, 1 - p), (n - 2, p)
                if B:
                    b_sum(*b)
                if Cc:
                    c_low(n - 2, 0)
                    c_low(n - 2, 1)
                if A:
                    g_powers(n, 1)
                if B:
                    b_sum_sq(*b)
                if Cc:
                    c_low(n - 2, 2)
                    c_low(n - 2, 3)
                if A:
                    a_sum(*a)
                if Cc:
                    c_low(n - 2, 4)
                    c_low(n - 2, 5)
                if A:
                    a_sum_sq(*a)
                if Cc:
                    c_low(n - 2, 6)
                    c_low(n - 2, 7)
                if more:
                    g_modes(n + 1)
                if Cc:
                    for u in range(8, 16):
                        c_low(n - 2, u)
                if B:
                    b_xx(*b)
                if Cc:
                    for u in range(16, 20):
                        c_low(n - 2, u)
                if more:
                    g_powers(n + 1, 0)
                if Cc:
                    for u in range(20, 24):
                        c_low(n - 2, u)
                if B:
                    b_sum3(*b)
                    b_sum_sq3(*b)
                if Cc:
                    c_sum(*c)
                    c_sum_sq(*c)
                for i in pieces_of(n):
                    low_piece(i)

            iterations(eng, stages)

        @block.scalar
        def _(eng):
            k = 0

            def did(ins):
                nonlocal k
                k += 1
                ins.then_inc(su_act, 1)

            def ln_exp():
                eng.add_instruction(mybir.InstLoadActFuncSet(
                    name=nc.get_next_instruction_name(), act_func_set_id=LN_EXP,
                    engine=mybir.EngineType.Activation, ins=[], outs=[]))

            xw0 = xw[:, 1, :, NT]
            eng.wait_ge(su_pe, 1)
            did(eng.activation(xw0.rearrange("p (c b) -> p c b", c=CT),
                               bank[S_A][:, 0:2 * 2 * NB].rearrange("p (c t b) -> p c t b", c=2, t=2)[:, :, 1, :], ACT.Copy))
            assert k == X0_DONE
            eng.wait_ge(su_vec, XC0_DONE)
            did(eng.activation(sq1[:, :, 0:NB], xn[:, :, 0:NB], ACT.Square))
            assert k == SQ0_DONE
            eng.wait_ge(su_pe, 3)
            eng.wait_ge(su_pool, BD0_DONE)
            ln_exp()
            did(eng.activation(rs1[:, 0:NB], bank[S_ST][:, TOK:TOK + NB], ACT.Ln, bias=eps_c[:, 0:1]))
            eng.wait_ge(su_act, k)
            did(eng.activation(rs1[:, 0:NB], rs1[:, 0:NB], ACT.Exp, scale=-0.5))
            assert k == RS0_DONE
            eng.wait_ge(su_vec, R0_DONE)
            did(eng.activation(rw[:, :, NT], rw[:, :, NT], ACT.Sigmoid))
            assert k == SG0_DONE

            def rstd(line, lnv, rst, n, dst):
                eng.activation(dst, bank[S_ST][:, TOK:2 * TOK], ACT.Ln, bias=eps_c[:, 0:1]).then_inc(*line.step(lnv))
                after(eng, line, lnv, n)
                eng.activation(dst, dst, ACT.Exp, scale=-0.5).then_inc(*line.step(rst))

            def a_x(n, p):
                after(eng, a_act, "rp1", n - 1)
                if isinstance(n, int) and n == 0:
                    eng.wait_ge(su_act, X0_DONE)
                eng.activation(xw[:, p, :, 0], xw[:, 1 - p, :, NT], ACT.Copy).then_inc(*a_act.step("x_slot"))
                after(eng, a_pe, "tok1", n)
                after(eng, b_pool, "xx", n - 2)
                src = bank[S_A][:].rearrange("p (c t b) -> p c t b", c=CT, b=NB)
                dst = cur(xw[:, p]).rearrange("p (c b) t -> p c t b", c=CT)
                eng.activation(dst, src, ACT.Copy).then_inc(*a_act.step("x"))

            def a_sq(n, p):
                after(eng, a_vec, "xc", n)
                eng.activation(sq1, xn[:], ACT.Square).then_inc(*a_act.step("sq"))

            def a_prev(n, p):
                after(eng, a_act, "x", n)
                after(eng, a_vec, "ry", n - 1)
                if isinstance(n, int) and n == 0:
                    eng.wait_ge(su_vec, A0_DONE)
                for name, w, tm in (("kp", kw, "tmk"), ("vp", vw, "tmv"), ("rp", rw, "tmr")):
                    for h in range(CT):
                        eng.activation(cur(half(w[:], h)), prv(half(xw[:, p], h)), ACT.Copy,
                                       scale=one_minus(tm, h)).then_inc(*a_act.step(f"{name}{h}"))

            def a_rstd(n, p):
                ln_exp()
                after(eng, a_pe, "var", n)
                rstd(a_act, "lnv", "rstd", n, rs1)

            def a_exp(n, p):
                ln_exp()
                after(eng, a_vec, "d11", n)
                eng.activation(cur(e1[:, 0]), cur(e1[:, 0]), ACT.Exp).then_inc(*a_act.step("d1"))
                after(eng, a_vec, "d2", n)
                eng.activation(cur(e2[:, 0]), cur(e2[:, 0]), ACT.Exp).then_inc(*a_act.step("d2"))
                after(eng, a_vec, "s", n)
                eng.activation(t3[:], sw[:], ACT.Ln, bias=eps_c[:, 1:2]).then_inc(*a_act.step("lns"))
                after(eng, a_vec, "mx", n)
                eng.activation(cur(e1[:]), cur(e1[:]), ACT.Exp).then_inc(*a_act.step("ef1"))
                eng.activation(cur(e2[:]), cur(e2[:]), ACT.Exp, scale=-1.0).then_inc(*a_act.step("ef2"))

            def a_den(n, p):
                ln_exp()
                after(eng, a_vec, "den", n)
                eng.activation(cur(t3[:]), cur(t3[:]), ACT.Ln).then_inc(*a_act.step("lnd"))
                after(eng, a_act, "lnd", n)
                eng.activation(cur(t3[:]), cur(t3[:]), ACT.Exp, scale=-1.0).then_inc(*a_act.step("rden"))

            def a_sig(n, p):
                after(eng, a_vec, "r1", n)
                eng.activation(cur(rw[:]), cur(rw[:]), ACT.Sigmoid).then_inc(*a_act.step("sig"))

            def b_sq(n, p):
                after(eng, b_vec, "xc", n)
                eng.activation(sqB, xn2[:], ACT.Square).then_inc(*b_act.step("sq"))

            def b_prev(n, p):
                after(eng, b_vec, "x2", n - 1)
                for h in range(CT):
                    eng.activation(win1(xpc[:, h]), prv(half(x1w[:, p], h)), ACT.Copy,
                                   scale=one_minus("cmk", h)).then_inc(*b_act.step(f"kp{h}"))
                for h in range(CT):
                    eng.activation(win1(rr[:, h]), prv(half(x1w[:, p], h)), ACT.Copy,
                                   scale=one_minus("cmr", h)).then_inc(*b_act.step(f"rp{h}"))

            def b_rstd(n, p):
                ln_exp()
                after(eng, b_pe, "var", n)
                rstd(b_act, "lnv", "rstd", n, rsB)

            def b_sig(n, p):
                after(eng, b_vec, "r1", n)
                eng.activation(rr[:], rr[:], ACT.Sigmoid).then_inc(*b_act.step("rr"))

            def b_norm3(n, p):
                after(eng, b_vec, "xc3", n)
                eng.activation(sqB, x2[:], ACT.Square).then_inc(*b_act.step("sq3"))
                ln_exp()
                after(eng, b_pe, "var3", n)
                rstd(b_act, "lnv3", "rstd3", n, rsB)

            def c_silu(n, m):
                after(eng, c_pe, f"w{m}", n)
                if m >= 2:
                    after(eng, c_vec, f"g{m - 2}", n)
                else:
                    after(eng, c_vec, f"g{m + 6}", n - 1)
                eng.activation(sil[:, m % 2], bank[S_G][:, 0:TOK], ACT.Silu,
                               scale=col("s1", m)).then_inc(*c_act.step(f"s{m}"))

            def c_gelu(n, layer, m):
                u = 8 * layer + m
                after(eng, c_pe, "k7" if layer == 1 else f"h2{m // 2}", n)
                gt_free(eng, n, u)
                eng.activation(gt[:, u % 2], bank[m // 2][:, (m % 2) * TOK:(m % 2 + 1) * TOK], ACT.Gelu,
                               scale=col("sh1" if layer == 1 else "sh2", m)).then_inc(*c_act.step(f"g{layer}{m}"))

            def c_norm(n, p):
                after(eng, c_vec, "xc", n)
                eng.activation(gt[:], hres[:, p], ACT.Square).then_inc(*c_act.step("sq"))
                ln_exp()
                after(eng, c_pe, "var", n)
                rstd(c_act, "lnv", "rstd", n, rs4[:])

            def stages(n, p):
                A, B, Cc = has("A", n), has("B", n), has("C", n)
                a, b, c = (n, p), (n - 1, 1 - p), (n - 2, p)
                if Cc:
                    c_silu(n - 2, 0)
                if B:
                    b_sq(*b)
                if Cc:
                    c_silu(n - 2, 1)
                if B:
                    b_prev(*b)
                if Cc:
                    c_silu(n - 2, 2)
                if A:
                    a_x(*a)
                if Cc:
                    c_silu(n - 2, 3)
                if B:
                    b_rstd(*b)
                if Cc:
                    c_silu(n - 2, 4)
                if A:
                    a_sq(*a)
                if Cc:
                    c_silu(n - 2, 5)
                if A:
                    a_prev(*a)
                if Cc:
                    c_silu(n - 2, 6)
                if A:
                    a_rstd(*a)
                if Cc:
                    c_silu(n - 2, 7)
                    for m in range(8):
                        c_gelu(n - 2, 1, m)
                if A:
                    a_sig(*a)
                if B:
                    b_sig(*b)
                if A:
                    a_exp(*a)
                if Cc:
                    for m in range(4):
                        c_gelu(n - 2, 2, m)
                if A:
                    a_den(*a)
                if Cc:
                    for m in range(4, 8):
                        c_gelu(n - 2, 2, m)
                if B:
                    b_norm3(*b)
                if Cc:
                    c_norm(*c)
                for i in pieces_of(n):
                    eng.wait_ge(ld_p[i % 2], 16 * (i // 2 + 1))
                    eng.activation(pieces[i][1], st[:, i % 2], ACT.Copy).then_inc(w_hi, 1)

            iterations(eng, stages)

        @block.vector
        def _(eng):
            k = 0

            def did(ins, then=None):
                nonlocal k
                k += 1
                ins.then_inc(su_vec, 1)
                eng.wait_ge(su_vec, k)

            eng.wait_ge(ld_w, 96)
            did(eng.tensor_scalar(bmode[:, :, 0], bmode[:, :, 0], 2.0, None, ALU.mult))
            did(eng.tensor_scalar(bmode[:, :, 1], bmode[:, :, 1], -2.0, None, ALU.mult))
            assert k == BM_DONE, k
            for i, name in enumerate(("tmk", "tmv", "tmr", "cmk", "cmr")):
                a = COLS[name][0]
                did(eng.tensor_scalar(onem[:, CT * i:CT * i + CT], prm[:, a:a + CT], -1.0, 1.0, ALU.mult, ALU.add))
            a = COLS["u"][0]
            did(eng.tensor_scalar(negu[:], prm[:, a:a + CT], -1.0, None, ALU.mult))
            magic = 12582912.0
            did(eng.tensor_scalar(EN[:], EX[:], 1.4426950408889634, magic, ALU.mult, ALU.add))
            did(eng.tensor_scalar(EN[:], EN[:], magic, None, ALU.subtract))
            did(eng.tensor_scalar(EN[:], EN[:], -126.0, 127.0, ALU.max, ALU.min))
            did(eng.scalar_tensor_tensor(EX[:], EN[:], -0.693359375, EX[:], ALU.mult, ALU.add))
            did(eng.scalar_tensor_tensor(EX[:], EN[:], 2.12194440054690583e-4, EX[:], ALU.mult, ALU.add))
            did(eng.tensor_scalar(EN[:], EN[:], 127.0, None, ALU.add))
            did(eng.tensor_copy(EI[:], EN[:]))
            did(eng.tensor_scalar(EI[:], EI[:], 23, None, ALU.logical_shift_left))
            did(eng.tensor_scalar(EQ[:], EX[:], 1.0 / 5040, None, ALU.mult))
            for c in (720, 120, 24, 6, 2, 1):
                did(eng.scalar_tensor_tensor(EQ[:], EQ[:], 1.0 / c, EX[:], ALU.add, ALU.mult))
            did(eng.scalar_tensor_tensor(EX[:], EQ[:], 1.0, EI[:].bitcast(F32), ALU.add, ALU.mult))
            dt, a, b = EX[:, 0], EX[:, 1], aim[:]
            did(eng.scalar_tensor_tensor(a, a, -0.5, dt, ALU.mult, ALU.mult))
            did(eng.scalar_tensor_tensor(b, b, 0.5, dt, ALU.mult, ALU.mult))
            b2, den, num = EQ[:, 0], EQ[:, 1], EN[:, 0]
            did(eng.tensor_tensor(b2, b, b, ALU.mult))
            did(eng.tensor_scalar(EN[:, 1], a, -1.0, 1.0, ALU.mult, ALU.add))
            did(eng.tensor_tensor(den, EN[:, 1], EN[:, 1], ALU.mult))
            did(eng.tensor_tensor(den, den, b2, ALU.add))
            did(eng.scalar_tensor_tensor(num, a, 1.0, EN[:, 1], ALU.add, ALU.mult))
            did(eng.tensor_tensor(num, num, b2, ALU.subtract))
            did(eng.reciprocal(EN[:, 1], den))
            did(eng.tensor_tensor(Z[:, 0, :, 0, 0], num, EN[:, 1], ALU.mult))
            did(eng.scalar_tensor_tensor(Z[:, 1, :, 0, 0], b, 2.0, EN[:, 1], ALU.mult, ALU.mult))
            for j in range(7):
                r0, i0 = Z[:, 0, :, j // 4, j % 4], Z[:, 1, :, j // 4, j % 4]
                r1, i1 = Z[:, 0, :, (j + 1) // 4, (j + 1) % 4], Z[:, 1, :, (j + 1) // 4, (j + 1) % 4]
                did(eng.tensor_tensor(r1, r0, r0, ALU.mult))
                did(eng.tensor_tensor(num, i0, i0, ALU.mult))
                did(eng.tensor_tensor(r1, r1, num, ALU.subtract))
                did(eng.scalar_tensor_tensor(i1, r0, 2.0, i0, ALU.mult, ALU.mult))
            for i, g in enumerate((3, 0, 1, 2)):
                if i:
                    eng.wait_ge(put_t, 32 * i)
                t = tg[:].rearrange("p r q s l -> p r (q s) l")
                zg = Z[:, :, g * QG:(g + 1) * QG].rearrange("p r q s j -> p r (q s) j")
                did(eng.memset(t[:, 0, :, 0], 1.0))
                did(eng.memset(t[:, 1, :, 0], 0.0))
                did(eng.tensor_copy(t[:, :, :, 1], zg[:, :, :, 0]))
                for j in range(1, 4):
                    n = 1 << j
                    re, im = t[:, 0, :, 0:n], t[:, 1, :, 0:n]
                    zr = zg[:, 0, :, j:j + 1].broadcast_to([P, 2 * QG, n])
                    zi = zg[:, 1, :, j:j + 1].broadcast_to([P, 2 * QG, n])
                    did(eng.tensor_tensor(t[:, 0, :, n:2 * n], re, zr, ALU.mult))
                    did(eng.tensor_tensor(zt[:, 0, :, 0:n], im, zi, ALU.mult))
                    did(eng.tensor_tensor(t[:, 0, :, n:2 * n], t[:, 0, :, n:2 * n], zt[:, 0, :, 0:n], ALU.subtract))
                    did(eng.tensor_tensor(t[:, 1, :, n:2 * n], re, zi, ALU.mult))
                    did(eng.tensor_tensor(zt[:, 1, :, 0:n], im, zr, ALU.mult))
                    did(eng.tensor_tensor(t[:, 1, :, n:2 * n], t[:, 1, :, n:2 * n], zt[:, 1, :, 0:n], ALU.add))
                assert k == TG_DONE[i], (i, k)
                if i == 0:
                    did(eng.tensor_copy(pq[:, :, QC - 1], tg[:, :, QG - 1]))
            eng.wait_ge(put_t, 128)
            did(eng.memset(wdec[:, :, 0], NEG_INF))
            for h in range(CT):
                did(eng.tensor_copy(half(wdec[:], h)[:, :, 1:W9], col("w", h).unsqueeze(2).broadcast_to([P, NB, NT])))
            for w in (e1, e2, kw, vw, rw, mw, sw, aw, t3):
                did(eng.memset(w[:], 0.0))
            did(eng.tensor_tensor(grid(Vr, 1), power(QC - 1, 0, 1, 1), power(QC - 1, 0, 0, 1), ALU.mult))
            did(eng.tensor_tensor(grid(Vt, 1), power(QC - 1, 1, 1, 1), power(QC - 1, 1, 0, 1), ALU.mult))
            did(eng.tensor_tensor(Vr[:, 0], Vr[:, 0], Vt[:, 0], ALU.subtract))
            did(eng.tensor_tensor(grid(Vi, 1), power(QC - 1, 0, 1, 1), power(QC - 1, 1, 0, 1), ALU.mult))
            did(eng.tensor_tensor(grid(Vt, 1), power(QC - 1, 1, 1, 1), power(QC - 1, 0, 0, 1), ALU.mult))
            did(eng.tensor_tensor(Vi[:, 0], Vi[:, 0], Vt[:, 0], ALU.add))
            assert k == V0_DONE, k
            x0 = xw[:, 1, :, NT].rearrange("p (c b) -> p c b", c=CT)
            eng.wait_ge(su_act, X0_DONE)
            did(eng.tensor_tensor(hs1[:, 0:NB], x0[:, 0], x0[:, 1], ALU.add))
            assert k == HS0_DONE, k
            eng.wait_ge(su_pe, 2)
            n0 = xn[:, :, 0:NB]
            did(eng.tensor_tensor(n0, x0, bank[S_ST][:, 0:NB].unsqueeze(1).broadcast_to([P, CT, NB]), ALU.subtract))
            assert k == XC0_DONE, k
            eng.wait_ge(su_act, SQ0_DONE)
            did(eng.tensor_tensor(hs1[:, 0:NB], sq1[:, 0, 0:NB], sq1[:, 1, 0:NB], ALU.add))
            assert k == HQ0_DONE, k
            eng.wait_ge(su_act, RS0_DONE)
            did(eng.tensor_tensor(n0, n0, rs1[:, 0:NB].unsqueeze(1).broadcast_to([P, CT, NB]), ALU.mult))
            for h in range(CT):
                did(eng.tensor_scalar(n0[:, h], n0[:, h], col("g1", h), col("b1", h), ALU.mult, ALU.add))
            assert k == XN0_DONE, k
            eng.wait_ge(su_pe, 4)
            for j, (w, tm) in enumerate(((mw, "tmk"), (aw, "tmv"), (rw, "tmr"))):
                for h in range(CT):
                    dst = half(w[:], h)[:, :, NT]
                    did(eng.tensor_scalar(dst, x0[:, h], one_minus(tm, h), None, ALU.mult))
                    at = (2 * j + h) * NB
                    did(eng.scalar_tensor_tensor(dst, bank[S_A][:, at:at + NB], col(tm, h), dst, ALU.mult, ALU.add))
            assert k == R0_DONE, k
            did(eng.memset(sw[:, :, NT], 1.0))
            eng.wait_ge(su_act, SG0_DONE)
            did(eng.scalar_tensor_tensor(x1_first[:], aw[:, :, NT], 1.0 / (1.0 + WKV_EPS), rw[:, :, NT], ALU.mult, ALU.mult))
            did(eng.tensor_tensor(x1_first[:], x1_first[:], xw[:, 1, :, NT], ALU.add))
            did(eng.tensor_copy(x1w[:, 1, :, NT], x1_first[:]))
            assert k == A0_DONE, k

            def g_powers(n, g):
                if g == 0:
                    eng.wait_ge(ld_a, 16 + 32 * (n + 1))
                    after(eng, a_pe, "tok1", n - 1)
                    if isinstance(n, int) and n == 0:
                        eng.wait_ge(su_pe, 1)
                else:
                    after(eng, a_pe, "tok0", n)
                eng.tensor_tensor(grid(Vr), power(2 * g, 0, 1), power(2 * g, 0, 0), ALU.mult).then_inc(*g_vec.step(f"vr{g}"))
                after(eng, g_pool, f"vt{g}", n)
                after(eng, g_vec, f"vr{g}", n)
                eng.tensor_tensor(Vr[:], Vr[:], Vt[:], ALU.subtract).then_inc(*g_vec.step(f"vs{g}"))
                eng.tensor_tensor(grid(Vi), power(2 * g, 0, 1), power(2 * g, 1, 0), ALU.mult).then_inc(*g_vec.step(f"vi{g}"))
                after(eng, g_pool, f"vu{g}", n)
                after(eng, g_vec, f"vi{g}", n)
                eng.tensor_tensor(Vi[:], Vi[:], Vt[:], ALU.add).then_inc(*g_vec.step(f"vw{g}"))

            def a_center(n, p):
                after(eng, a_pe, "mean", n)
                after(eng, a_pe, "kvr2", n - 1)
                x = cur(xw[:, p]).rearrange("p (c b) t -> p c b t", c=CT)
                m = win1(bank[S_ST][:, 0:TOK]).unsqueeze(1).broadcast_to([P, CT, NB, NT])
                eng.tensor_tensor(xn[:].rearrange("p c (b t) -> p c b t", t=NT), x, m, ALU.subtract).then_inc(*a_vec.step("xc"))

            def a_norm(n, p):
                after(eng, a_act, "rstd", n)
                eng.tensor_tensor(xn[:], xn[:], both(rs1), ALU.mult).then_inc(*a_vec.step("xn"))
                after(eng, a_vec, "xn", n)
                for h in range(CT):
                    eng.tensor_scalar(xn[:, h], xn[:, h], col("g1", h), col("b1", h), ALU.mult,
                                      ALU.add).then_inc(*a_vec.step(f"xg{h}"))

            def a_mix(n, j):
                name, w, tm = (("k", kw, "tmk"), ("v", vw, "tmv"), ("r", rw, "tmr"))[j]
                after(eng, a_act, "rp1", n)
                after(eng, a_pe, f"kvr{j}", n)
                for h in range(CT):
                    dst = cur(half(w[:], h))
                    eng.scalar_tensor_tensor(dst, win1(bank[S_A][:, h * TOK:(h + 1) * TOK]), col(tm, h), dst,
                                             ALU.mult, ALU.add).then_inc(*a_vec.step(f"{name}{h}"))

            def flat(w):
                return w.rearrange("p l t -> p (l t)")

            def wkv_max(n, p):
                after(eng, a_vec, "x1", n - 1)
                eng.tensor_copy(kw[:, :, 0], mw[:, :, NT]).then_inc(*a_vec.step("mc"))
                after(eng, a_vec, "mc", n)
                eng.tensor_tensor_scan(flat(mw[:]), flat(wdec[:]), flat(kw[:]), 0.0, ALU.add, ALU.max).then_inc(*a_vec.step("m"))
                after(eng, a_vec, "m", n)
                for h in range(CT):
                    eng.scalar_tensor_tensor(cur(half(e1[:, 0], h)), prv(half(mw[:], h)), col("w", h), cur(half(mw[:], h)),
                                             ALU.add, ALU.subtract).then_inc(*a_vec.step(f"d1{h}"))
                after(eng, a_pe, "var", n)
                eng.tensor_tensor(cur(e2[:, 0]), cur(kw[:]), cur(mw[:]), ALU.subtract).then_inc(*a_vec.step("d2"))
                eng.tensor_copy(e2[:, 0, :, 0], sw[:, :, NT]).then_inc(*a_vec.step("sc"))

            def wkv_sum(n, p):
                after(eng, a_act, "d2", n)
                after(eng, a_vec, "sc", n)
                eng.tensor_tensor_scan(flat(sw[:]), flat(e1[:, 0]), flat(e2[:, 0]), 0.0, ALU.mult, ALU.add).then_inc(*a_vec.step("s"))

            def wkv_bb(n, p):
                after(eng, a_act, "lns", n)
                eng.tensor_tensor(t3[:], t3[:], mw[:], ALU.add).then_inc(*a_vec.step("bb"))
                after(eng, a_vec, "bb", n)
                for i, (name, s) in enumerate((("dl", lambda h: col("w", h)), ("gm", lambda h: negu[:, h:h + 1]))):
                    for h in range(CT):
                        eng.scalar_tensor_tensor(cur(half(e1[:, i], h)), prv(half(t3[:], h)), s(h), cur(half(kw[:], h)),
                                                 ALU.add, ALU.subtract).then_inc(*a_vec.step(f"{name}{h}"))
                after(eng, a_vec, "gm1", n)
                eng.tensor_scalar(cur(e2[:]), cur(e1[:]), 0.0, None, ALU.max).then_inc(*a_vec.step("mn"))
                after(eng, a_vec, "mn", n)
                eng.tensor_scalar(cur(e1[:]), cur(e1[:]), 0.0, None, ALU.min).then_inc(*a_vec.step("mx"))

            def wkv_aa(n, p):
                after(eng, a_act, "ef2", n)
                eng.tensor_tensor(cur(e2[:, 0]), cur(e2[:, 0]), cur(vw[:]), ALU.mult).then_inc(*a_vec.step("ev"))
                eng.tensor_copy(e2[:, 0, :, 0], aw[:, :, NT]).then_inc(*a_vec.step("ac"))
                after(eng, a_vec, "ac", n)
                eng.tensor_tensor_scan(flat(aw[:]), flat(e1[:, 0]), flat(e2[:, 0]), 0.0, ALU.mult, ALU.add).then_inc(*a_vec.step("aa"))
                eng.scalar_tensor_tensor(cur(t3[:]), cur(e1[:, 1]), WKV_EPS, cur(e2[:, 1]), ALU.add, ALU.add).then_inc(*a_vec.step("den"))

            def wkv_num(n, p):
                after(eng, a_vec, "den", n)
                eng.tensor_tensor(cur(e1[:, 1]), cur(e1[:, 1]), prv(aw[:]), ALU.mult).then_inc(*a_vec.step("n1"))
                eng.tensor_tensor(cur(e2[:, 1]), cur(e2[:, 1]), cur(vw[:]), ALU.mult).then_inc(*a_vec.step("n2"))
                after(eng, a_vec, "n2", n)
                eng.tensor_tensor(cur(e1[:, 1]), cur(e1[:, 1]), cur(e2[:, 1]), ALU.add).then_inc(*a_vec.step("n3"))

            def wkv_out(n, p):
                after(eng, a_act, "rden", n)
                after(eng, a_vec, "n3", n)
                eng.tensor_tensor(cur(e1[:, 1]), cur(e1[:, 1]), cur(t3[:]), ALU.mult).then_inc(*a_vec.step("y"))
                after(eng, a_act, "sig", n)
                after(eng, a_vec, "y", n)
                eng.tensor_tensor(cur(e1[:, 1]), cur(e1[:, 1]), cur(rw[:]), ALU.mult).then_inc(*a_vec.step("ry"))
                after(eng, a_vec, "ry", n)
                after(eng, b_pool, "xx", n - 2)
                after(eng, b_act, "rp1", n - 2)
                after(eng, a_vec, "x1s", n - 1)
                eng.tensor_tensor(cur(x1w[:, p]), cur(e1[:, 1]), cur(xw[:, p]), ALU.add).then_inc(*a_vec.step("x1"))
                eng.tensor_copy(x1w[:, p, :, 0], x1w[:, 1 - p, :, NT]).then_inc(*a_vec.step("x1s"))

            def b_center(n, p):
                after(eng, b_pe, "mean", n)
                after(eng, b_pe, "cm3", n - 1)
                x = cur(x1w[:, p]).rearrange("p (c b) t -> p c b t", c=CT)
                m = win1(bank[S_ST][:, 0:TOK]).unsqueeze(1).broadcast_to([P, CT, NB, NT])
                eng.tensor_tensor(xn2[:].rearrange("p c (b t) -> p c b t", t=NT), x, m, ALU.subtract).then_inc(*b_vec.step("xc"))

            def b_norm(n, p):
                after(eng, b_act, "rstd", n)
                eng.tensor_tensor(xn2[:], xn2[:], both(rsB), ALU.mult).then_inc(*b_vec.step("xn"))
                after(eng, b_vec, "xn", n)
                for h in range(CT):
                    eng.tensor_scalar(xn2[:, h], xn2[:, h], col("g2", h), col("b2", h), ALU.mult,
                                      ALU.add).then_inc(*b_vec.step(f"xg{h}"))
                after(eng, b_vec, "xg1", n)
                after(eng, b_act, "rp1", n)
                for h in range(CT):
                    eng.scalar_tensor_tensor(rr[:, h], xn2[:, h], col("cmr", h), rr[:, h], ALU.mult,
                                             ALU.add).then_inc(*b_vec.step(f"r{h}"))

            def b_relu(n, i):
                after(eng, b_pe, f"cm{i}", n)
                if i >= 2:
                    after(eng, b_pe, f"cp{i - 2}", n)
                for h in range(CT):
                    eng.scalar_tensor_tensor(kk[:, i % 2, h], bank[S_CM][:, h * TOK:(h + 1) * TOK], col("cmk", h), xpc[:, h],
                                             ALU.mult, ALU.add).then_inc(*b_vec.step(f"k{2 * i + h}"))
                after(eng, b_vec, f"k{2 * i + 1}", n)
                eng.scalar_tensor_tensor(kk[:, i % 2], kk[:, i % 2], 0.0, kk[:, i % 2], ALU.max,
                                         ALU.mult).then_inc(*b_vec.step(f"q{i}"))

            def b_res(n, p):
                after(eng, b_pe, "cp3", n)
                after(eng, b_act, "rr", n)
                eng.tensor_tensor(rr[:], bank[S_CP][:].rearrange("p (c n) -> p c n", c=CT), rr[:], ALU.mult).then_inc(*b_vec.step("rv"))
                after(eng, b_pool, "xx", n)
                after(eng, b_vec, "rv", n)
                eng.tensor_tensor(x2[:], x2[:], rr[:], ALU.add).then_inc(*b_vec.step("x2"))

            def b_center3(n, p):
                after(eng, b_pe, "mean3", n)
                after(eng, b_pool, "sum3", n)
                eng.tensor_tensor(x2[:], x2[:], both(bank[S_ST][:, 0:TOK]), ALU.subtract).then_inc(*b_vec.step("xc3"))

            def b_out(n, p):
                after(eng, b_act, "rstd3", n)
                if not (isinstance(n, int) and n < 2):
                    eng.wait_ge(put_o[p], 8 * (n - p))
                eng.tensor_tensor(hres[:, p], x2[:], both(rsB), ALU.mult).then_inc(*b_vec.step("h"))
                after(eng, b_vec, "h", n)
                after(eng, c_pe, "w7", n - 1)
                eng.tensor_copy(hx[:, 0], hres[:, p]).then_inc(*b_vec.step("hi"))
                after(eng, b_vec, "hi", n)
                eng.tensor_tensor(hx[:, 1], hres[:, p], hx[:, 0], ALU.subtract).then_inc(*b_vec.step("lo"))

            def c_gate(n, m):
                after(eng, c_act, f"s{m}", n)
                gt_free(eng, n, m)
                eng.scalar_tensor_tensor(gt[:, m % 2], bank[S_G][:, TOK:2 * TOK], col("s2", m), sil[:, m % 2],
                                         ALU.mult, ALU.mult).then_inc(*c_vec.step(f"g{m}"))
                after(eng, c_vec, f"g{m}", n)
                c_high(n, m)

            def c_high(n, u):
                m = u % 8
                if 8 <= u < 16:
                    after(eng, c_act, f"g1{m}", n)
                    after(eng, c_pe, "h23", n - 1)
                elif u >= 16:
                    after(eng, c_act, f"g2{m}", n)
                    after(eng, c_pe, f"y{m - 3}" if m >= 3 else "k7", n)
                elif m >= 3:
                    after(eng, c_pe, f"k{m - 3}", n)
                else:
                    after(eng, c_pe, "y7", n - 1)
                eng.tensor_copy(split_to(u, 0), gt[:, u % 2]).then_inc(*c_vec.step(f"i{u}"))

            def c_res(n, p):
                after(eng, c_pe, "y7", n)
                for h in range(CT):
                    eng.scalar_tensor_tensor(hres[:, p, h], bank[S_G][:, h * TOK:(h + 1) * TOK], col("s3", h), hres[:, p, h],
                                             ALU.mult, ALU.add).then_inc(*c_vec.step(f"y{h}"))

            def c_center(n, p):
                after(eng, c_pe, "mean", n)
                after(eng, c_pool, "sum", n)
                eng.tensor_tensor(hres[:, p], hres[:, p], both(bank[S_ST][:, 0:TOK]), ALU.subtract).then_inc(*c_vec.step("xc"))

            def c_out(n, p):
                after(eng, c_act, "rstd", n)
                eng.tensor_tensor(hres[:, p], hres[:, p], both(rs4[:]), ALU.mult).then_inc(*c_vec.step("o"))

            def nonzero(i):
                eng.wait_ge(w_lo, i + 1)
                eng.tensor_reduce(flag[:, i:i + 1], sl[:, i % 2].bitcast(F32), mybir.AxisListType.X, ALU.max,
                                  apply_absolute_value=True).then_inc(w_nz, 1)

            def set_flag():
                eng.wait_ge(w_nz, NPIECE)
                eng.tensor_reduce(flag[:, NPIECE:NPIECE + 1], flag[:, 0:NPIECE], mybir.AxisListType.X,
                                  ALU.max).then_inc(w_nz, 1)
                eng.wait_ge(w_nz, NPIECE + 1)
                eng.tensor_scalar(flag[:, NPIECE:NPIECE + 1], flag[:, NPIECE:NPIECE + 1], 0.0, None,
                                  ALU.not_equal).then_inc(w_nz, 1)
                eng.wait_ge(fl_sum, 1)
                eng.tensor_scalar(flag[:, NPIECE + 1:], bank[S_G][:, 0:1], 0.0, None, ALU.not_equal).then_inc(w_nz, 1)
                eng.wait_ge(w_nz, NPIECE + 3)
                eng.tensor_copy(flag_i[:], flag[:, NPIECE + 1:]).then_inc(fl_set, 1)

            g_powers(0, 0)

            def stages(n, p):
                nonlocal k
                A, B, Cc = has("A", n), has("B", n), has("C", n)
                more = A and (not isinstance(n, int) or n + 1 < CH)
                a, b, c = (n, p), (n - 1, 1 - p), (n - 2, p)
                if isinstance(n, int) and n == CH:
                    after(eng, a_vec, "x1s", CH - 1)
                    did(eng.tensor_copy(x1w[:, 1, :, NT], x1_first[:]))
                    assert k == X1_FIXED
                if Cc:
                    c_gate(n - 2, 0)
                if B:
                    b_center(*b)
                if Cc:
                    c_gate(n - 2, 1)
                if A:
                    g_powers(n, 1)
                if Cc:
                    c_gate(n - 2, 2)
                    c_gate(n - 2, 3)
                if B:
                    b_norm(*b)
                if Cc:
                    c_gate(n - 2, 4)
                if A:
                    a_center(*a)
                if Cc:
                    c_gate(n - 2, 5)
                    c_gate(n - 2, 6)
                if A:
                    a_norm(*a)
                if Cc:
                    c_gate(n - 2, 7)
                if A:
                    a_mix(n, 0)
                if Cc:
                    for u in range(8, 12):
                        c_high(n - 2, u)
                if A:
                    a_mix(n, 1)
                if Cc:
                    for u in range(12, 16):
                        c_high(n - 2, u)
                if A:
                    a_mix(n, 2)
                    wkv_max(*a)
                if B:
                    b_relu(n - 1, 0)
                if A:
                    wkv_sum(*a)
                if B:
                    b_relu(n - 1, 1)
                if A:
                    wkv_bb(*a)
                if Cc:
                    c_high(n - 2, 16)
                    c_high(n - 2, 17)
                if B:
                    b_relu(n - 1, 2)
                if A:
                    wkv_aa(*a)
                if Cc:
                    c_high(n - 2, 18)
                    c_high(n - 2, 19)
                if A:
                    wkv_num(*a)
                if B:
                    b_relu(n - 1, 3)
                if Cc:
                    c_high(n - 2, 20)
                    c_high(n - 2, 21)
                if more:
                    g_powers(n + 1, 0)
                if A:
                    wkv_out(*a)
                if B:
                    b_res(*b)
                if Cc:
                    c_high(n - 2, 22)
                    c_high(n - 2, 23)
                if B:
                    b_center3(*b)
                if Cc:
                    c_res(*c)
                if B:
                    b_out(*b)
                if Cc:
                    c_center(*c)
                    c_out(*c)
                for i in pieces_of(n):
                    nonzero(i)
                if isinstance(n, int) and n == 1:
                    set_flag()

            iterations(eng, stages)

        @block.tensor
        def _(eng):
            def mm(out_, w, x, start, stop, **kws):
                return eng.matmul(out_, w, x, start=start, stop=stop, **kws)

            eng.wait_ge(su_vec, V0_DONE)
            eng.wait_ge(su_pool, BD0_DONE)
            for h in range(CT):
                s = slice(h * P, (h + 1) * P)
                mm(bank[S_A][:, 64 * h:64 * h + 64], Vr[:, 0, s], bd[:, 0, 0], True, False)
                last = mm(bank[S_A][:, 64 * h:64 * h + 64], Vi[:, 0, s], bd[:, 0, 1], False, True)
            last.then_inc(su_pe, 1)
            eng.wait_ge(su_vec, HS0_DONE)
            mm(bank[S_ST][:, 0:NB], mean_w[:], hs1[:, 0:NB], True, True).then_inc(su_pe, 1)
            eng.wait_ge(su_vec, HQ0_DONE)
            mm(bank[S_ST][:, TOK:TOK + NB], mean_w[:], hs1[:, 0:NB], True, True).then_inc(su_pe, 1)
            eng.wait_ge(su_vec, XN0_DONE)
            eng.wait_ge(ld_tm, 16)
            for o in range(6):
                for c in range(CT):
                    last = mm(bank[S_A][:, o * NB:(o + 1) * NB], W_tm[:, c, o * P:(o + 1) * P], xn[:, c, 0:NB],
                              c == 0, c == CT - 1)
            last.then_inc(su_pe, 1)

            def a_tok(n, g):
                if g == 0:
                    if isinstance(n, int) and n == 0:
                        eng.wait_ge(su_vec, A0_DONE)
                    after(eng, g_pool, "bd3", n)
                    after(eng, a_vec, "r1", n - 1)
                    after(eng, b_vec, "k7", n - 2)
                after(eng, g_vec, f"vw{g}", n)
                for h in range(CT):
                    for q in range(2):
                        at = h * TOK + (2 * g + q) * 2 * NB
                        s = slice(h * P, (h + 1) * P)
                        mm(bank[S_A][:, at:at + 2 * NB], Vr[:, q, s], bd[:, 2 * g + q, 0], True, False)
                        last = mm(bank[S_A][:, at:at + 2 * NB], Vi[:, q, s], bd[:, 2 * g + q, 1], False, True)
                last.then_inc(*a_pe.step(f"tok{g}"))

            def b_mean(n, p):
                after(eng, b_pool, "sum", n)
                if has("C", n + 1):
                    after(eng, c_act, "lnv", n - 2)
                after(eng, b_act, "lnv3", n - 1)
                if isinstance(n, int) and n == 0:
                    after(eng, a_act, "lnv", 0)
                mm(bank[S_ST][:, 0:TOK], mean_w[:], hsB, True, True).then_inc(*b_pe.step("mean"))

            def b_var(n, p):
                after(eng, b_pool, "sum_sq", n)
                mm(bank[S_ST][:, TOK:2 * TOK], mean_w[:], hsB, True, True).then_inc(*b_pe.step("var"))

            def a_mean(n, p):
                after(eng, a_pool, "sum", n)
                after(eng, b_act, "lnv", n - 1)
                mm(bank[S_ST][:, 0:TOK], mean_w[:], hs1, True, True).then_inc(*a_pe.step("mean"))

            def a_var(n, p):
                after(eng, a_pool, "sum_sq", n)
                mm(bank[S_ST][:, TOK:2 * TOK], mean_w[:], hs1, True, True).then_inc(*a_pe.step("var"))

            def b_mean3(n, p):
                after(eng, b_pool, "sum3", n)
                if has("A", n + 1):
                    after(eng, a_act, "lnv", n + 1)
                mm(bank[S_ST][:, 0:TOK], mean_w[:], hsB, True, True).then_inc(*b_pe.step("mean3"))

            def b_var3(n, p):
                after(eng, b_pool, "sum_sq3", n)
                mm(bank[S_ST][:, TOK:2 * TOK], mean_w[:], hsB, True, True).then_inc(*b_pe.step("var3"))

            def c_mean(n, p):
                after(eng, c_pool, "sum", n)
                if has("B", n + 2):
                    after(eng, b_act, "lnv3", n + 1)
                else:
                    after(eng, b_act, "lnv3", n)
                mm(bank[S_ST][:, 0:TOK], mean_w[:], hs4[:], True, True).then_inc(*c_pe.step("mean"))

            def c_var(n, p):
                after(eng, c_pool, "sum_sq", n)
                mm(bank[S_ST][:, TOK:2 * TOK], mean_w[:], hs4[:], True, True).then_inc(*c_pe.step("var"))

            def a_kvr(n, p, j):
                if j == 0:
                    after(eng, a_vec, "xg1", n)
                else:
                    after(eng, a_vec, ("k1", "v1")[j - 1], n)
                for h in range(CT):
                    o = CT * j + h
                    for c in range(CT):
                        last = mm(bank[S_A][:, h * TOK:(h + 1) * TOK], W_tm[:, c, o * P:(o + 1) * P], xn[:, c],
                                  c == 0, c == CT - 1)
                last.then_inc(*a_pe.step(f"kvr{j}"))

            def b_cm(n, i):
                if i == 0:
                    after(eng, b_vec, "xg1", n)
                    if has("A", n + 1):
                        after(eng, a_vec, "r1", n + 1)
                    after(eng, b_vec, "k7", n - 1)
                else:
                    after(eng, b_vec, f"k{2 * i - 1}", n)
                eng.wait_ge(ld_s[i % 2], 32 * n + 16 * (i // 2 + 1))
                for h in range(2):
                    for c in range(CT):
                        last = mm(bank[S_CM][:, h * TOK:(h + 1) * TOK], wcs[:, i % 2, h, c * P:(c + 1) * P], xn2[:, c],
                                  c == 0, c == CT - 1)
                last.then_inc(*b_pe.step(f"cm{i}"))

            def b_cp(n, i):
                after(eng, b_vec, f"q{i}", n)
                if i == 0:
                    after(eng, b_vec, "rv", n - 1)
                for j in range(2):
                    for h in range(CT):
                        first = i == 0 and j == 0
                        last = mm(bank[S_CP][:, h * TOK:(h + 1) * TOK], wcs[:, i % 2, j, C + h * P:C + (h + 1) * P],
                                  kk[:, i % 2, j], first and h == 0, i == 3 and j == 1, skip_group_check=True)
                last.then_inc(*b_pe.step(f"cp{i}"))

            def low(n, step, j, todo):
                pos = low_at[step] + j
                eng.wait_ge(lo_in, 16 * (NLO * n + pos + 1))
                for i, (o, w, x) in enumerate(todo):
                    last = mm(o, w, x, False, False, skip_group_check=True)
                last.then_inc(lo_used, 1)

            def c_w(n, m):
                if m == 0:
                    after(eng, b_vec, "lo", n)
                    after(eng, c_vec, "y1", n - 1)
                else:
                    after(eng, c_vec, f"g{m - 1}", n)
                todo = [(bank[S_G][:, j * TOK:(j + 1) * TOK], w[:, c, m * P:(m + 1) * P], hx[:, part, c])
                        for j, w in enumerate((W_1, W_2)) for c in range(CT) for part in range(2)]
                for i, (o, w, x) in enumerate(todo[:-1]):
                    mm(o, w, x, i == 0, False, skip_group_check=True)
                with eng.If(flag_reg):
                    for c in range(CT):
                        low(n, f"w{m}", c, [(bank[S_G][:, j * TOK:(j + 1) * TOK], lo_w[:, j * P:(j + 1) * P], hx[:, 0, c])
                                            for j in range(2)])
                mm(*todo[-1], False, True, skip_group_check=True).then_inc(*c_pe.step(f"w{m}"))

            def c_k(n, m):
                after(eng, c_pool, f"l{m}", n)
                if m == 0:
                    after(eng, c_act, "g27", n - 1)
                todo = [(bank[o // 2][:, (o % 2) * TOK:(o % 2 + 1) * TOK], W_h1[:, m, o * P:(o + 1) * P], ha[:, m % 3, part],
                         m == 0 and o % 2 == 0 and part == 0)
                        for o in range(FT) for part in range(2)]
                for o, w, x, start in todo[:-1]:
                    mm(o, w, x, start, m == 7, skip_group_check=True)
                with eng.If(flag_reg):
                    for i in range(4):
                        low(n, f"k{m}", i, [(bank[i][:, j * TOK:(j + 1) * TOK], lo_w[:, j * P:(j + 1) * P], ha[:, m % 3, 0])
                                            for j in range(2)])
                o, w, x, _ = todo[-1]
                mm(o, w, x, False, m == 7, skip_group_check=True).then_inc(*c_pe.step(f"k{m}"))

            def c_h(n, i):
                after(eng, c_act, f"g1{2 * i + 1}", n)
                todo = [(bank[i][:, j * TOK:(j + 1) * TOK], W_h2[:, c, (2 * i + j) * P:(2 * i + j + 1) * P], hb[:, part, c], c)
                        for j in range(2) for c in range(FT) for part in range(2)]
                for q, (o, w, x, c) in enumerate(todo[:-1]):
                    if i == 0 and q < 2 * FT and q % 2 == 0:
                        after(eng, c_pool, f"l{8 + c}", n)
                    mm(o, w, x, q == 0, False, skip_group_check=True)
                with eng.If(flag_reg):
                    for c in range(FT):
                        low(n, f"h2{i}", c, [(bank[i][:, j * TOK:(j + 1) * TOK], lo_w[:, j * P:(j + 1) * P], hb[:, 0, c])
                                             for j in range(2)])
                o, w, x, _ = todo[-1]
                mm(o, w, x, False, True, skip_group_check=True).then_inc(*c_pe.step(f"h2{i}"))

            def c_y(n, m):
                after(eng, c_pool, f"l{16 + m}", n)
                todo = [(bank[S_G][:, h * TOK:(h + 1) * TOK], W_3[:, m, h * P:(h + 1) * P], ha[:, m % 3, part])
                        for h in range(CT) for part in range(2)]
                if m == 0:
                    after(eng, c_vec, "g7", n)
                for i, (o, w, x) in enumerate(todo[:-1]):
                    mm(o, w, x, m == 0 and i == 0, m == 7, skip_group_check=True)
                with eng.If(flag_reg):
                    low(n, f"y{m}", 0, [(bank[S_G][:, h * TOK:(h + 1) * TOK], lo_w[:, h * P:(h + 1) * P], ha[:, m % 3, 0])
                                        for h in range(CT)])
                mm(*todo[-1], False, m == 7, skip_group_check=True).then_inc(*c_pe.step(f"y{m}"))

            flag_reg = None

            def stages(n, p):
                nonlocal flag_reg
                A, B, Cc = has("A", n), has("B", n), has("C", n)
                a, b, c = (n, p), (n - 1, 1 - p), (n - 2, p)
                if isinstance(n, int) and n == 2:
                    eng.wait_ge(w_nz, NPIECE + 2)
                    mm(bank[S_G][:, 0:1], mean_w[:], flag[:, NPIECE:NPIECE + 1], True, True).then_inc(fl_sum, 1)
                    eng.wait_ge(fl_set, 1)
                    flag_reg = eng.value_load(flag_i[0:1, 0:1], min_val=0, max_val=1)
                if A:
                    a_tok(n, 0)
                if Cc:
                    c_w(n - 2, 0)
                if B:
                    b_mean(*b)
                if Cc:
                    c_w(n - 2, 1)
                    c_k(n - 2, 0)
                    c_w(n - 2, 2)
                if A:
                    a_tok(n, 1)
                if Cc:
                    c_k(n - 2, 1)
                if B:
                    b_var(*b)
                if Cc:
                    c_w(n - 2, 3)
                    c_k(n - 2, 2)
                if A:
                    a_mean(*a)
                if Cc:
                    c_w(n - 2, 4)
                    c_k(n - 2, 3)
                    c_w(n - 2, 5)
                    c_k(n - 2, 4)
                if A:
                    a_var(*a)
                if Cc:
                    c_w(n - 2, 6)
                    c_k(n - 2, 5)
                    c_w(n - 2, 7)
                    c_k(n - 2, 6)
                if A:
                    a_kvr(*a, 0)
                if Cc:
                    c_k(n - 2, 7)
                if A:
                    a_kvr(*a, 1)
                    a_kvr(*a, 2)
                if B:
                    b_cm(n - 1, 0)
                if Cc:
                    c_h(n - 2, 0)
                if B:
                    b_cm(n - 1, 1)
                    b_cp(n - 1, 0)
                if Cc:
                    c_h(n - 2, 1)
                if B:
                    b_cm(n - 1, 2)
                    b_cp(n - 1, 1)
                if Cc:
                    c_y(n - 2, 0)
                    c_y(n - 2, 1)
                    c_h(n - 2, 2)
                if B:
                    b_cm(n - 1, 3)
                    b_cp(n - 1, 2)
                if Cc:
                    c_y(n - 2, 2)
                    c_y(n - 2, 3)
                    c_h(n - 2, 3)
                if B:
                    b_cp(n - 1, 3)
                if Cc:
                    c_y(n - 2, 4)
                    c_y(n - 2, 5)
                if B:
                    b_mean3(*b)
                if Cc:
                    c_y(n - 2, 6)
                    c_y(n - 2, 7)
                if B:
                    b_var3(*b)
                if Cc:
                    c_mean(*c)
                    c_var(*c)

            iterations(eng, stages)


BM_DONE = 2
CB0_DONE = 6
BD0_DONE = 8
X0_DONE, SQ0_DONE, RS0_DONE, SG0_DONE = 1, 2, 4, 5
_Z = BM_DONE + 5 + 1 + 9 + 6 + 1 + 11 + 28
TG_DONE = [_Z + 21, _Z + 43, _Z + 64, _Z + 85]
V0_DONE = TG_DONE[3] + 3 + 9 + 6
HS0_DONE = V0_DONE + 1
XC0_DONE = HS0_DONE + 1
HQ0_DONE = XC0_DONE + 1
XN0_DONE = HQ0_DONE + 3
R0_DONE = XN0_DONE + 12
A0_DONE = R0_DONE + 4
X1_FIXED = A0_DONE + 1


def kernel(**inputs):
    import numpy as np
    import concourse.bacc as bacc
    from concourse.bass_utils import run_bass_kernel_spmd

    a = {k: np.asarray(v) for k, v in inputs.items()}

    def turned(v, axis):
        return np.roll(v, -1, axis=axis)

    def modes(v):
        v = turned(v, 0).reshape(QP, 2, NS, -1)
        return np.ascontiguousarray(v.transpose(1, 2, 0, 3).reshape(P, QP, -1))

    def tiles(w):
        return np.ascontiguousarray(w.reshape(-1, P, w.shape[1]).transpose(1, 0, 2))

    x = turned(a["x"], 1).reshape(NB, CH, QC, 2, NS, 2)
    c_in = np.ascontiguousarray(x.transpose(1, 3, 4, 2, 5, 0).reshape(CH, P, QC * 2 * NB))
    cols = {"w": "attn_time_decay", "u": "attn_time_first", "tmk": "attn_tmk", "tmv": "attn_tmv", "tmr": "attn_tmr",
            "g1": "attn_g1", "b1": "attn_b1", "g2": "attn_g2", "b2": "attn_b2", "cmk": "attn_cmk", "cmr": "attn_cmr",
            "s1": "ffn_w1_s", "s2": "ffn_w2_s", "sh1": "ffn_h1_s", "sh2": "ffn_h2_s", "s3": "ffn_w3_s"}
    cm = a["L0_attn_W_cm"].reshape(CT, P, FT, P).transpose(2, 1, 0, 3).reshape(FT, P, C)
    cp = a["L0_attn_W_cp"].reshape(FT, P, C)
    w_cs = np.ascontiguousarray(np.concatenate([cm, cp], axis=2).reshape(4, 2, P, 2 * C).transpose(0, 2, 1, 3)
                                .reshape(4, P, 4 * C))
    par = np.ascontiguousarray(np.concatenate([a["L0_" + cols[k]].reshape(-1, P).T for k in COLS], axis=1))
    arrays = {
        "c_in": c_in,
        "log_dt": np.ascontiguousarray(turned(a["L0_tok_log_dt"], 0).reshape(QP, 2).T),
        "a_re": modes(a["L0_tok_inv_A_real"])[:, :, 0].copy(),
        "a_im": modes(a["L0_tok_A_imag"])[:, :, 0].copy(),
        "b_ri": modes(a["L0_tok_B_ri"]),
        "par": par,
        "w_tm": tiles(a["L0_attn_W_tm"]),
        "w_cs": w_cs,
        "w1": tiles(a["L0_ffn_w1_w"].T),
        "w2": tiles(a["L0_ffn_w2_w"].T),
        "h1": tiles(a["L0_ffn_h1_w"].T),
        "h2": tiles(a["L0_ffn_h2_w"].T),
        "w3": tiles(a["L0_ffn_w3_w"].T),
    }
    nc = bacc.Bacc("TRN2", target_bir_lowering=False, num_devices=1)
    args = [nc.dram_tensor(k, v.shape, F32, kind="ExternalInput").ap() for k, v in arrays.items()]
    args.append(nc.dram_tensor("out", (CH, P, CT * TOK), F32, kind="ExternalOutput").ap())
    args.append(nc.dram_tensor("tpq", (CH, P, 2 * HX), F32, kind="Internal").ap())
    args.append(nc.dram_tensor("wlo", (NLO, P, C), F32, kind="Internal").ap())
    build(nc, *args)
    got = run_bass_kernel_spmd(nc, [arrays], core_ids=[0]).results[0]["out"]
    got = np.asarray(got).reshape(CH, P, CT, NB, NT).transpose(3, 0, 4, 2, 1).reshape(NB, T, C)
    return np.ascontiguousarray(np.roll(got, 1, axis=1))
```

```python
from contextlib import ExitStack

import concourse.bass as bass
from concourse import mybir

F32 = mybir.dt.float32
I32 = mybir.dt.int32
F32R = mybir.dt.float32r
ALU = mybir.AluOpType
ACT = mybir.ActivationFunctionType

P = 128
NB = 32
T = 256
C = 256
NS = 64
F = 1024
NT = 8
CH = T // NT
TOK = NB * NT
CT = C // P
FT = F // P
LN = CT * NB
W9 = NT + 1
QP = T // 2
QC = NT // 2
QG = 32
HX = QC * 2 * 16
R16 = 16
LN_EPS = 1e-5
WKV_EPS = 1e-8
NEG_INF = -1e38
SIGMOID, LN_EXP, GELU, SILU = 2, 6, 10, 18
PIECE = 1024
NPIECE = 22
RING = 4
NLO = 88
LO_H1, LO_H2, LO_W3 = 16, 48, 80

COLS = {}
for _name, _n in (("w", CT), ("u", CT), ("tmk", CT), ("tmv", CT), ("tmr", CT), ("g1", CT), ("b1", CT),
                  ("g2", CT), ("b2", CT), ("cmk", CT), ("cmr", CT), ("s1", FT), ("s2", FT), ("sh1", FT),
                  ("sh2", FT), ("s3", CT)):
    COLS[_name] = (sum(n for _, n in COLS.values()), _n)
NCOL = sum(n for _, n in COLS.values())


class Line:

    def __init__(self, sem, steps):
        self.sem, self.steps, self.at = sem, steps, 0

    def step(self, name):
        assert self.steps[self.at] == name, (self.steps[self.at], name)
        self.at = (self.at + 1) % len(self.steps)
        return self.sem, 1

    def value(self, name, n):
        return len(self.steps) * n + self.steps.index(name) + 1


def after(eng, line, name, n):
    if not (isinstance(n, int) and n < 0):
        eng.wait_ge(line.sem, line.value(name, n))


def build(nc, c_in, log_dt, a_re, a_im, b_ri, par, w_tm, w_cs, w1, w2, h1, h2, w3, out, tpq, wlo):
    ctx = ExitStack()
    with ctx:
        def sb(name, shape, dt=F32, stack=ctx):
            return stack.enter_context(nc.sbuf_tensor(name, shape, dt))

        def sem(name):
            return ctx.enter_context(nc.semaphore(name))

        W_tm = sb("W_tm", [P, CT, 3 * C])
        W_1 = sb("W_1", [P, CT, F], F32R)
        W_2 = sb("W_2", [P, CT, F], F32R)
        W_h1 = sb("W_h1", [P, FT, F], F32R)
        W_h2 = sb("W_h2", [P, FT, F], F32R)
        W_3 = sb("W_3", [P, FT, C], F32R)
        wcs = sb("wcs", [P, 2, 2, 2 * C])
        prm = sb("prm", [P, NCOL])
        onem = sb("onem", [P, 5 * CT])
        negu = sb("negu", [P, CT])
        mean_w = sb("mean_w", [P, P])
        eps_c = sb("eps_c", [P, 2])
        wdec = sb("wdec", [P, LN, W9])
        bmode = sb("bmode", [P, QP, 2])
        x1_first = sb("x1_first", [P, LN])

        cin = sb("cin", [P, QC, 2, NB])
        pq = sb("pq", [P, 2, QC, 2, R16])
        cbt = sb("cbt", [P, 2, QC, 2, NB])
        bd = sb("bd", [P, QC, 2, 2 * NB])
        Vr = sb("Vr", [P, QC, C])
        Vi = sb("Vi", [P, QC, C])
        Vt = sb("Vt", [P, 2, C])
        xn = sb("xn", [P, CT, TOK])
        xw = sb("xw", [P, 2, LN, W9])
        x1w = sb("x1w", [P, 2, LN, W9])
        staging_b = ExitStack()
        tg_b = sb("tg_b", [P, 2, QG, 2, R16], stack=staging_b)
        staging_b.close()
        xn2 = sb("xn2", [P, CT, TOK])
        x2 = sb("x2", [P, CT, TOK])
        rr = sb("rr", [P, CT, TOK])
        xpc = sb("xpc", [P, CT, TOK])
        kk = sb("kk", [P, 2, 2, TOK])
        hres = sb("hres", [P, 2, CT, TOK])
        hx = sb("hx", [P, 2, CT, TOK], F32R)
        ha = sb("ha", [P, 3, 2, TOK], F32R)
        sil = sb("sil", [P, 2, TOK])
        gt = sb("gt", [P, 2, TOK])
        hs4 = sb("hs4", [P, TOK])
        rs4 = sb("rs4", [P, TOK])
        flag = sb("flag", [P, NPIECE + 2])
        flag_i = sb("flag_i", [P, 1], I32)
        lo_w = sb("lo_w", [P, C], F32R)
        staging = ExitStack()
        st = sb("st", [P, RING, PIECE], stack=staging)
        staging.close()
        hb = sb("hb", [P, 2, FT, TOK], F32R)

        setup = ExitStack()
        EX = sb("EX", [P, 2, QP], stack=setup)
        EN = sb("EN", [P, 2, QP], stack=setup)
        EQ = sb("EQ", [P, 2, QP], stack=setup)
        EI = sb("EI", [P, 2, QP], I32, stack=setup)
        aim = sb("aim", [P, QP], stack=setup)
        Z = sb("Z", [P, 2, QP, 2, 4], stack=setup)
        zt = sb("zt", [P, 2, 2 * QG, 8], stack=setup)
        tgs = [tg_b, sb("tg", [P, 2, QG, 2, R16], stack=setup)]
        setup.close()
        kw = sb("kw", [P, LN, W9])
        vw = sb("vw", [P, LN, W9])
        rw = sb("rw", [P, LN, W9])
        mw = sb("mw", [P, LN, W9])
        sw = sb("sw", [P, LN, W9])
        aw = sb("aw", [P, LN, W9])
        e1 = sb("e1", [P, 2, LN, W9])
        e2 = sb("e2", [P, 2, LN, W9])
        t3 = sb("t3", [P, LN, W9])

        bank = [ctx.enter_context(nc.psum_tensor(f"bank{i}", [P, 512], F32)) for i in range(8)]
        S_ST, S_CP, S_A, S_G = 4, 5, 6, 7
        GATE = (S_CP, S_G)

        def col(name, k=0):
            at = COLS[name][0] + k
            return prm[:, at:at + 1]

        def one_minus(name, k):
            at = CT * ("tmk", "tmv", "tmr", "cmk", "cmr").index(name) + k
            return onem[:, at:at + 1]

        def cur(w):
            return w[..., 1:W9]

        def prv(w):
            return w[..., 0:NT]

        def half(w, h):
            return w[:, h * NB:(h + 1) * NB, :]

        def win(flat):
            return flat.rearrange("p c (b t) -> p (c b) t", t=NT)

        def win1(flat):
            return flat.rearrange("p (b t) -> p b t", t=NT)

        def both(ap):
            return ap.unsqueeze(1).broadcast_to([P, CT, TOK])

        def grid(v):
            return v.rearrange("p q (a b) -> p q a b", b=R16)

        def power(q0, ri, s, n=2):
            v = pq[:, ri, q0:q0 + n, s]
            return (v.unsqueeze(3) if s else v.unsqueeze(2)).broadcast_to([P, n, R16, R16])

        def split_to(u, part):
            return hb[:, part, u - 8] if 8 <= u < 16 else ha[:, u % 8 % 3, part]

        def gt_free(eng, n, u):
            if u >= 2:
                after(eng, c_pool, f"l{u - 2}", n)
            else:
                after(eng, c_pool, f"l{22 + u}", n - 1)

        lnA = t3[:].rearrange("p l t -> p (l t)")
        hs1, rs1 = lnA[:, 0:TOK], lnA[:, TOK:2 * TOK]
        sq1 = e2[:, 1].rearrange("p l t -> p (l t)")[:, 0:CT * TOK].rearrange("p (c n) -> p c n", c=CT)
        junk = hx[:].rearrange("p h c n -> p (h c n)")
        sqB = kk[:, 0]
        sq4 = Vt[:]
        hsB, rsB = kk[:, 1, 0], kk[:, 1, 1]

        ld_w = sem("ld_w")
        ld_tm = sem("ld_tm")
        ld_a = sem("ld_a")
        ld_s = [sem("ld_s0"), sem("ld_s1")]
        ld_p = [sem(f"ld_p{i}") for i in range(RING)]
        put_l = [sem(f"put_l{i}") for i in range(RING)]
        w_hi = sem("w_hi")
        w_lo = sem("w_lo")
        w_nz = sem("w_nz")
        fl_sum = sem("fl_sum")
        fl_set = sem("fl_set")
        lo_in = sem("lo_in")
        lo_used = sem("lo_used")
        put_t = [sem("put_t0"), sem("put_t1")]
        put_o = [sem("put_o0"), sem("put_o1")]
        su_vec = sem("su_vec")
        su_pool = sem("su_pool")
        su_act = sem("su_act")
        su_pe = sem("su_pe")

        g_pool = Line(sem("g_pool"), ["cb_re", "cb_im", "bd0", "bd1", "bd2", "bd3", "vt0", "vu0", "vt1", "vu1"])
        g_vec = Line(sem("g_vec"), [f"{s}{g}" for g in range(2) for s in ("vr", "vs", "vi", "vw")])
        a_pool = Line(sem("a_pool"), ["sum", "sum_sq", "d2"])
        a_pe = Line(sem("a_pe"), ["tok0", "tok1", "mean", "var", "kvr0", "kvr1", "kvr2"])
        a_act = Line(sem("a_act"), ["x_slot", "x", "sq", "lnv", "rstd", "kp0", "kp1", "vp0", "vp1", "rp0", "rp1",
                                    "sig", "d1", "d2", "lns", "ef1", "ef2"])
        a_vec = Line(sem("a_vec"), ["xc", "nt", "nv", "ny", "xn", "xg0", "xg1", "k0", "k1", "v0", "v1", "r0", "r1",
                                    "mc", "m", "d10", "d11", "sc", "s", "bb", "dl0", "dl1", "gm0", "gm1",
                                    "mn", "mx", "ev", "ac", "aa", "den", "n1", "n2", "n3", "rec0", "rec1", "y", "ry", "x1", "x1s"])
        b_pool = Line(sem("b_pool"), ["sum", "sum_sq", "xx", "sum3", "sum_sq3"])
        b_pe = Line(sem("b_pe"), ["mean", "var", "cm0", "cm1", "cp0", "cm2", "cp1", "cm3", "cp2", "cp3",
                                  "mean3", "var3"])
        b_act = Line(sem("b_act"), ["kp0", "kp1", "rp0", "rp1", "sq", "lnv", "rstd", "rr", "sq3", "lnv3", "rstd3"])
        b_vec = Line(sem("b_vec"), ["xc", "nt", "nv", "ny", "xn", "xg0", "xg1", "r0", "r1"]
                     + [s for i in range(4) for s in (f"k{2*i}", f"k{2*i+1}", f"q{i}")]
                     + ["rv", "x2", "xc3", "nt3", "nv3", "ny3", "h", "hi", "lo"])
        c_pool = Line(sem("c_pool"), [f"l{u}" for u in range(24)])
        c_pe = Line(sem("c_pe"), ["w0", "w1"] + [s for m in range(2, 8) for s in (f"w{m}", f"k{m-2}")] + ["k6", "k7"]
                    + ["h20", "h21", "h22", "y0", "y1", "y2", "h23"] + [f"y{m}" for m in range(3, 8)])
        c_act = Line(sem("c_act"), [f"s{m}" for m in range(8)] + [f"g1{m}" for m in range(8)]
                     + [f"g2{m}" for m in range(8)])
        c_vec = Line(sem("c_vec"), [s for m in range(8) for s in (f"g{m}", f"i{m}")] + [f"i{u}" for u in range(8, 24)]
                     + ["y0", "y1"])
        d_pool = Line(sem("d_pool"), ["sum", "sum_sq"])
        d_pe = Line(sem("d_pe"), ["mean", "var"])
        d_act = Line(sem("d_act"), ["sq", "lnv", "rstd"])
        d_vec = Line(sem("d_vec"), ["xc", "nt", "nv", "ny", "o"])

        block = ctx.enter_context(nc.Block())


        def iterations(eng, stages):
            for n in range(4):
                stages(n, n % 2)
            with eng.Fori(4, CH - 3, 2) as n:
                stages(n, 0)
                stages(n + 1, 1)
            for n in range(CH - 2, CH + 3):
                stages(n, n % 2)

        def has(stage, n):
            lag = "ABCD".index(stage)
            return not isinstance(n, int) or 0 <= n - lag < CH

        def more(n):
            return not isinstance(n, int) or n + 1 < CH

        def chunk(dram, n):
            return dram[bass.ds(n, 1)].rearrange("o p x -> (o p) x")

        pieces = []
        for j, (w, W) in enumerate(((w1, W_1), (w2, W_2))):
            for c in range(CT):
                pieces.append((w[:, c], W[:, c],
                               wlo[c:LO_H1:2, :, j * P:(j + 1) * P].rearrange("m p x -> p m x"), P))
        for c in range(FT):
            pieces.append((h1[:, c], W_h1[:, c],
                           wlo[LO_H1 + 4 * c:LO_H1 + 4 * c + 4].rearrange("m p x -> p m x"), C))
        for c in range(FT):
            pieces.append((h2[:, c], W_h2[:, c], wlo[LO_H2 + c:LO_W3:FT].rearrange("m p x -> p m x"), C))
        for j in range(2):
            s = slice(4 * j, 4 * j + 4)
            pieces.append((w3[:, s].rearrange("p k x -> p (k x)"), W_3[:, s].rearrange("p k x -> p (k x)"),
                           wlo[LO_W3 + 4 * j:LO_W3 + 4 * j + 4].rearrange("m p x -> p m x"), C))
        assert len(pieces) == NPIECE

        def slot_value(q):
            return 16 * len(range(q, NPIECE, RING))

        def low_blocks(step):
            if step[0] == "w":
                return [2 * int(step[1]) + c for c in range(CT)]
            if step[0] == "k":
                return [LO_H1 + 4 * int(step[1]) + i for i in range(4)]
            if step[0] == "h":
                return [LO_H2 + 8 * int(step[2]) + c for c in range(FT)]
            return [LO_W3 + int(step[1])]

        low_at, low_list = {}, []
        for step in c_pe.steps:
            low_at[step] = len(low_list)
            low_list += low_blocks(step)
        assert sorted(low_list) == list(range(NLO))

        @block.sync
        def _(eng):
            eng.dma_start(prm[:], par).then_inc(ld_w, 16)
            eng.dma_start(EX[0:NS, 0, :], log_dt[0:1, :].broadcast_to([NS, QP])).then_inc(ld_w, 16)
            eng.dma_start(EX[NS:P, 0, :], log_dt[1:2, :].broadcast_to([NS, QP])).then_inc(ld_w, 16)
            eng.dma_start(EX[:, 1, :], a_re).then_inc(ld_w, 16)
            eng.dma_start(aim[:], a_im).then_inc(ld_w, 16)
            eng.dma_start(bmode[:], b_ri).then_inc(ld_w, 16)
            eng.dma_start(cin[:].rearrange("p q r b -> p (q r b)"), c_in[CH - 1]).then_inc(ld_a, 16)
            eng.dma_start(W_tm[:], w_tm).then_inc(ld_tm, 16)
            for i, g in enumerate((3, 0, 1, 2)):
                eng.wait_ge(su_vec, TG_DONE[i])
                for ri in range(2):
                    eng.dma_start(tpq[8 * g:8 * g + 8, :, ri * HX:(ri + 1) * HX].rearrange("n p x -> p n x"),
                                  tgs[i % 2][:, ri].rearrange("p (n q) s r -> p n (q s r)", n=8)).then_inc(put_t[i % 2], 16)
            for q in range(2):
                eng.wait_ge(put_t[q], 64)

            def load_a(n):
                after(eng, g_pool, "vu1", n - 1)
                after(eng, g_vec, "vw1", n - 1)
                eng.dma_start(cin[:].rearrange("p q r b -> p (q r b)"), chunk(c_in, n)).then_inc(ld_a, 16)
                eng.dma_start(pq[:].rearrange("p r q s l -> p (r q s l)"), chunk(tpq, n)).then_inc(ld_a, 16)

            def load_s(n, i):
                if i >= 2:
                    after(eng, b_pe, f"cp{i - 2}", n)
                else:
                    after(eng, b_pe, f"cp{i + 2}", n - 1)
                eng.dma_start(wcs[:, i % 2].rearrange("p m x -> p (m x)"), w_cs[i]).then_inc(ld_s[i % 2], 16)

            def all_low():
                def store(i):
                    eng.wait_ge(w_lo, NPIECE + i + 1)
                    dst, wid = pieces[i][2:]
                    eng.dma_start(dst, st[:, i % RING].rearrange("p (m x) -> p m x", x=wid)).then_inc(put_l[i % RING], 16)

                with eng.If(flag_reg):
                    for i in range(NPIECE):
                        if i >= RING:
                            eng.wait_ge(put_l[i % RING], 16 * (i // RING))
                        eng.dma_start(st[:, i % RING], pieces[i][0]).then_inc(ld_p[i % RING], 16)
                        if i:
                            store(i - 1)
                    store(NPIECE - 1)
                    for q in range(RING):
                        eng.wait_ge(put_l[q], slot_value(q))

            def send_low(n, flag_reg, steps):
                with eng.If(flag_reg):
                    for step in steps:
                        for j, b in enumerate(low_blocks(step)):
                            pos = low_at[step] + j
                            if not (isinstance(n, int) and NLO * n + pos == 0):
                                eng.wait_ge(lo_used, NLO * n + pos)
                            eng.dma_start(lo_w[:].bitcast(F32), wlo[b]).then_inc(lo_in, 16)

            eng.wait_ge(su_vec, V0_DONE)
            eng.wait_ge(su_pool, CB0_DONE)
            load_a(0)
            flag_reg = None

            def stages(n, p):
                nonlocal flag_reg
                if has("A", n) and more(n):
                    load_a(n + 1)
                if has("B", n):
                    load_s(n - 1, 0)
                    load_s(n - 1, 1)
                if isinstance(n, int) and n == 2:
                    eng.wait_ge(fl_set, 1)
                    flag_reg = eng.value_load(flag_i[0:1, 0:1], min_val=0, max_val=1)
                    all_low()
                if has("C", n):
                    send_low(n - 2, flag_reg, c_pe.steps[:c_pe.steps.index("h21")])
                if has("B", n):
                    load_s(n - 1, 2)
                if has("C", n):
                    send_low(n - 2, flag_reg, ["h21"])
                if has("B", n):
                    load_s(n - 1, 3)
                if has("D", n):
                    after(eng, d_vec, "o", n - 3)
                    eng.dma_start(chunk(out, n - 3), hres[:, 1 - p].rearrange("p c n -> p (c n)")).then_inc(put_o[1 - p], 16)
                if has("C", n):
                    send_low(n - 2, flag_reg, c_pe.steps[c_pe.steps.index("h22"):])

            iterations(eng, stages)
            for p in range(2):
                eng.wait_ge(put_o[p], 8 * CH)

        @block.gpsimd
        def _(eng):
            k = 0

            def did(ins):
                nonlocal k
                k += 1
                ins.then_inc(su_pool, 1)

            did(eng.memset(mean_w[:], 1.0 / C))
            did(eng.memset(eps_c[:, 0:1], LN_EPS))
            did(eng.memset(eps_c[:, 1:2], WKV_EPS))
            did(eng.memset(bd[:], 0.0))
            eng.wait_ge(su_vec, BM_DONE)
            eng.wait_ge(ld_a, 16)
            q = QP - 1
            qc = QC - 1
            did(eng.tensor_tensor(cbt[:, 0, 0], cin[:, qc], bmode[:, q, 0:1].unsqueeze(2).broadcast_to([P, 2, NB]), ALU.mult))
            did(eng.tensor_tensor(cbt[:, 1, 0], cin[:, qc], bmode[:, q, 1:2].unsqueeze(2).broadcast_to([P, 2, NB]), ALU.mult))
            assert k == CB0_DONE
            for i in range(NPIECE):
                eng.wait_ge(w_hi, i + 1)
                eng.tensor_tensor(st[:, i % RING], st[:, i % RING], pieces[i][1], ALU.subtract).then_inc(w_lo, 1)
            eng.wait_ge(w_lo, NPIECE)
            eng.wait_ge(su_pool, k)
            s = slice(NS, P)
            did(eng.tensor_tensor(bd[s, 0, 0, NB:], cbt[s, 0, 0, 0], cbt[s, 1, 0, 1], ALU.add))
            did(eng.tensor_tensor(bd[s, 0, 1, NB:], cbt[s, 1, 0, 0], cbt[s, 0, 0, 1], ALU.subtract))
            assert k == BD0_DONE

            def g_products(n):
                bre = bmode[:, bass.ds(QC * n, QC), 0:1]
                bim = bmode[:, bass.ds(QC * n, QC), 1:2]
                if isinstance(n, int) and n == 0:
                    eng.wait_ge(su_pool, BD0_DONE)
                after(eng, g_pool, "bd3", n - 1)
                eng.tensor_tensor(cbt[:, 0], cin[:], bre.unsqueeze(3).broadcast_to([P, QC, 2, NB]),
                                  ALU.mult).then_inc(*g_pool.step("cb_re"))
                eng.tensor_tensor(cbt[:, 1], cin[:], bim.unsqueeze(3).broadcast_to([P, QC, 2, NB]),
                                  ALU.mult).then_inc(*g_pool.step("cb_im"))

            def g_modes(n):
                after(eng, g_pool, "cb_im", n)
                after(eng, a_pe, "tok1", n - 1)
                if isinstance(n, int) and n == 0:
                    eng.wait_ge(su_pe, 1)
                for t in range(2):
                    s = slice(t * NS, (t + 1) * NS)
                    eng.tensor_tensor(bd[s, :, 0, t * NB:(t + 1) * NB], cbt[s, 0, :, 0], cbt[s, 1, :, 1],
                                      ALU.add).then_inc(*g_pool.step(f"bd{2 * t}"))
                    eng.tensor_tensor(bd[s, :, 1, t * NB:(t + 1) * NB], cbt[s, 1, :, 0], cbt[s, 0, :, 1],
                                      ALU.subtract).then_inc(*g_pool.step(f"bd{2 * t + 1}"))
                after(eng, g_pool, "bd3", n)

            def wait_a(n):
                eng.wait_ge(ld_a, 16 + 32 * (n + 1))

            def g_re(n, g):
                after(eng, g_vec, f"vw{1 - g}", n - 1 + g)
                if g == 0:
                    after(eng, d_pool, "sum_sq", n - 4)
                if isinstance(n, int) and n == 0:
                    eng.wait_ge(su_vec, V0_DONE)
                eng.tensor_tensor(grid(Vt[:]), power(2 * g, 1, 1), power(2 * g, 1, 0), ALU.mult).then_inc(*g_pool.step(f"vt{g}"))

            def g_im(n, g):
                after(eng, g_vec, f"vs{g}", n)
                eng.tensor_tensor(grid(Vt[:]), power(2 * g, 1, 1), power(2 * g, 0, 0), ALU.mult).then_inc(*g_pool.step(f"vu{g}"))

            def a_sum(n, p):
                after(eng, a_act, "x", n)
                after(eng, a_vec, "y", n - 1)
                if isinstance(n, int) and n == 0:
                    eng.wait_ge(su_vec, A0_DONE)
                eng.tensor_tensor(win1(hs1), cur(half(xw[:, p], 0)), cur(half(xw[:, p], 1)),
                                  ALU.add).then_inc(*a_pool.step("sum"))

            def a_sum_sq(n, p):
                after(eng, a_act, "sq", n)
                after(eng, a_pe, "mean", n)
                eng.tensor_tensor(hs1, sq1[:, 0], sq1[:, 1], ALU.add).then_inc(*a_pool.step("sum_sq"))

            def a_d2(n, p):
                after(eng, a_vec, "m", n)
                eng.tensor_tensor(cur(e2[:, 0]), cur(kw[:]), cur(mw[:]), ALU.subtract).then_inc(*a_pool.step("d2"))

            def b_sum(n, p):
                after(eng, a_vec, "x1s", n)
                if isinstance(n, int) and n == CH - 1:
                    eng.wait_ge(su_vec, X1_FIXED)
                after(eng, b_vec, "h", n - 1)
                eng.tensor_tensor(win1(hsB), cur(half(x1w[:, p], 0)), cur(half(x1w[:, p], 1)),
                                  ALU.add).then_inc(*b_pool.step("sum"))

            def b_sum_sq(n, p):
                after(eng, b_act, "sq", n)
                after(eng, b_pe, "mean", n)
                eng.tensor_tensor(hsB, sqB[:, 0], sqB[:, 1], ALU.add).then_inc(*b_pool.step("sum_sq"))

            def b_xx(n, p):
                after(eng, b_vec, "lo", n - 1)
                eng.tensor_tensor(win(x2[:]), cur(xw[:, p]), cur(x1w[:, p]), ALU.add).then_inc(*b_pool.step("xx"))

            def b_sum3(n, p):
                after(eng, b_vec, "x2", n)
                after(eng, b_pe, "cp3", n)
                eng.tensor_tensor(hsB, x2[:, 0], x2[:, 1], ALU.add).then_inc(*b_pool.step("sum3"))

            def b_sum_sq3(n, p):
                after(eng, b_act, "sq3", n)
                after(eng, b_pe, "mean3", n)
                eng.tensor_tensor(hsB, sqB[:, 0], sqB[:, 1], ALU.add).then_inc(*b_pool.step("sum_sq3"))

            def c_low(n, u):
                after(eng, c_vec, f"i{u}", n)
                eng.tensor_tensor(split_to(u, 1), gt[:, u % 2], split_to(u, 0), ALU.subtract).then_inc(*c_pool.step(f"l{u}"))

            def d_sum(n, p):
                after(eng, c_vec, "y1", n)
                after(eng, d_vec, "nv", n - 1)
                eng.tensor_tensor(hs4[:], hres[:, p, 0], hres[:, p, 1], ALU.add).then_inc(*d_pool.step("sum"))

            def d_sum_sq(n, p):
                after(eng, d_act, "sq", n)
                after(eng, d_pe, "mean", n)
                eng.tensor_tensor(hs4[:], sq4[:, 0], sq4[:, 1], ALU.add).then_inc(*d_pool.step("sum_sq"))

            wait_a(0)
            g_products(0)
            g_modes(0)
            g_re(0, 0)
            g_im(0, 0)
            g_re(0, 1)
            g_im(0, 1)

            def lows(n, a, b):
                if has("C", n):
                    for u in range(a, b):
                        c_low(n - 2, u)

            def stages(n, p):
                A, B, D = has("A", n), has("B", n), has("D", n)
                a, b, d = (n, p), (n - 1, 1 - p), (n - 3, 1 - p)
                if isinstance(n, int) and n == 2:
                    eng.wait_ge(fl_set, 1)
                    with eng.If(eng.value_load(flag_i[0:1, 0:1], min_val=0, max_val=1)):
                        for i in range(NPIECE):
                            eng.wait_ge(ld_p[i % RING], slot_value(i % RING) + 16 * (i // RING + 1))
                            eng.tensor_tensor(st[:, i % RING], st[:, i % RING], pieces[i][1], ALU.subtract).then_inc(w_lo, 1)
                if A:
                    a_sum(*a)
                lows(n, 0, 1)
                if B:
                    b_sum(*b)
                if D:
                    d_sum(*d)
                lows(n, 1, 2)
                if B:
                    b_sum_sq(*b)
                lows(n, 2, 3)
                if D:
                    d_sum_sq(*d)
                lows(n, 3, 4)
                if A and more(n):
                    wait_a(n + 1)
                    g_products(n + 1)
                    g_modes(n + 1)
                lows(n, 4, 6)
                if A:
                    a_sum_sq(*a)
                lows(n, 6, 8)
                if A and more(n):
                    g_re(n + 1, 0)
                    g_im(n + 1, 0)
                lows(n, 8, 16)
                if A:
                    a_d2(*a)
                if B:
                    b_xx(*b)
                if A and more(n):
                    g_re(n + 1, 1)
                    g_im(n + 1, 1)
                lows(n, 16, 18)
                if B:
                    b_sum3(*b)
                lows(n, 18, 19)
                if B:
                    b_sum_sq3(*b)
                lows(n, 19, 24)

            iterations(eng, stages)

        @block.scalar
        def _(eng):
            k = 0

            def did(ins):
                nonlocal k
                k += 1
                ins.then_inc(su_act, 1)

            def tables(which):
                eng.add_instruction(mybir.InstLoadActFuncSet(
                    name=nc.get_next_instruction_name(), act_func_set_id=which,
                    engine=mybir.EngineType.Activation, ins=[], outs=[]))

            def load_piece(i):
                if i >= RING:
                    eng.wait_ge(w_nz, i - RING + 1)
                eng.dma_start(st[:, i % RING], pieces[i][0]).then_inc(ld_p[i % RING], 16)

            def any_low(i):
                eng.wait_ge(w_lo, i + 1)
                if i:
                    eng.wait_ge(w_nz, i)
                eng.activation(junk, st[:, i % RING], ACT.Abs, accum_out=flag[:, i:i + 1]).then_inc(w_nz, 1)

            for i in range(RING - 2):
                load_piece(i)
            for i in range(NPIECE):
                if i + RING - 2 < NPIECE:
                    load_piece(i + RING - 2)
                eng.wait_ge(ld_p[i % RING], 16 * (i // RING + 1))
                eng.activation(pieces[i][1], st[:, i % RING], ACT.Copy).then_inc(w_hi, 1)
                if i >= 1:
                    any_low(i - 1)
            any_low(NPIECE - 1)

            xw0 = xw[:, 1, :, NT]
            eng.wait_ge(su_pe, 1)
            did(eng.activation(xw0.rearrange("p (c b) -> p c b", c=CT),
                               bank[S_A][:, 0:2 * 2 * NB].rearrange("p (c t b) -> p c t b", c=2, t=2)[:, :, 1, :], ACT.Copy))
            assert k == X0_DONE
            eng.wait_ge(su_vec, XC0_DONE)
            did(eng.activation(sq1[:, :, 0:NB], xn[:, :, 0:NB], ACT.Square))
            assert k == SQ0_DONE
            eng.wait_ge(su_pe, 3)
            eng.wait_ge(su_pool, BD0_DONE)
            tables(LN_EXP)
            did(eng.activation(rs1[:, 0:NB], bank[S_ST][:, TOK:TOK + NB], ACT.Ln, bias=eps_c[:, 0:1]))
            eng.wait_ge(su_act, k)
            did(eng.activation(rs1[:, 0:NB], rs1[:, 0:NB], ACT.Exp, scale=-0.5))
            assert k == RS0_DONE
            eng.wait_ge(su_vec, R0_DONE)
            did(eng.activation(rw[:, :, NT], rw[:, :, NT], ACT.Sigmoid))
            assert k == SG0_DONE

            def rstd(line, lnv, rst, n, dst, stat=S_ST):
                eng.activation(dst, bank[stat][:, TOK:2 * TOK], ACT.Ln, bias=eps_c[:, 0:1]).then_inc(*line.step(lnv))
                after(eng, line, lnv, n)
                eng.activation(dst, dst, ACT.Exp, scale=-0.5).then_inc(*line.step(rst))

            def a_x(n, p):
                after(eng, a_act, "rp1", n - 1)
                if isinstance(n, int) and n == 0:
                    eng.wait_ge(su_act, X0_DONE)
                eng.activation(xw[:, p, :, 0], xw[:, 1 - p, :, NT], ACT.Copy).then_inc(*a_act.step("x_slot"))
                after(eng, a_pe, "tok1", n)
                after(eng, b_pool, "xx", n - 2)
                src = bank[S_A][:].rearrange("p (c t b) -> p c t b", c=CT, b=NB)
                dst = cur(xw[:, p]).rearrange("p (c b) t -> p c t b", c=CT)
                eng.activation(dst, src, ACT.Copy).then_inc(*a_act.step("x"))

            def a_sq(n, p):
                after(eng, a_vec, "xc", n)
                eng.activation(sq1, xn[:], ACT.Square).then_inc(*a_act.step("sq"))

            def a_prev(n, p):
                after(eng, a_act, "x", n)
                after(eng, a_vec, "ry", n - 1)
                if isinstance(n, int) and n == 0:
                    eng.wait_ge(su_vec, A0_DONE)
                for name, w, tm in (("kp", kw, "tmk"), ("vp", vw, "tmv"), ("rp", rw, "tmr")):
                    for h in range(CT):
                        eng.activation(cur(half(w[:], h)), prv(half(xw[:, p], h)), ACT.Copy,
                                       scale=one_minus(tm, h)).then_inc(*a_act.step(f"{name}{h}"))

            def a_rstd(n, p):
                tables(LN_EXP)
                after(eng, a_pe, "var", n)
                rstd(a_act, "lnv", "rstd", n, rs1)

            def a_exp(n, p):
                after(eng, a_vec, "d11", n)
                eng.activation(cur(e1[:, 0]), cur(e1[:, 0]), ACT.Exp).then_inc(*a_act.step("d1"))
                after(eng, a_pool, "d2", n)
                eng.activation(cur(e2[:, 0]), cur(e2[:, 0]), ACT.Exp).then_inc(*a_act.step("d2"))
                after(eng, a_vec, "s", n)
                eng.activation(t3[:], sw[:], ACT.Ln, bias=eps_c[:, 1:2]).then_inc(*a_act.step("lns"))
                after(eng, a_vec, "mx", n)
                eng.activation(cur(e1[:]), cur(e1[:]), ACT.Exp).then_inc(*a_act.step("ef1"))
                eng.activation(cur(e2[:]), cur(e2[:]), ACT.Exp, scale=-1.0).then_inc(*a_act.step("ef2"))

            def a_sig(n, p):
                after(eng, a_vec, "r1", n)
                eng.activation(cur(rw[:]), cur(rw[:]), ACT.Sigmoid).then_inc(*a_act.step("sig"))

            def b_sq(n, p):
                after(eng, b_vec, "xc", n)
                eng.activation(sqB, xn2[:], ACT.Square).then_inc(*b_act.step("sq"))

            def b_prev(n, p):
                after(eng, a_vec, "x1s", n)
                after(eng, b_vec, "x2", n - 1)
                for h in range(CT):
                    eng.activation(win1(xpc[:, h]), prv(half(x1w[:, p], h)), ACT.Copy,
                                   scale=one_minus("cmk", h)).then_inc(*b_act.step(f"kp{h}"))
                for h in range(CT):
                    eng.activation(win1(rr[:, h]), prv(half(x1w[:, p], h)), ACT.Copy,
                                   scale=one_minus("cmr", h)).then_inc(*b_act.step(f"rp{h}"))

            def b_rstd(n, p):
                after(eng, b_pe, "var", n)
                rstd(b_act, "lnv", "rstd", n, rsB)

            def b_sig(n, p):
                after(eng, b_vec, "r1", n)
                eng.activation(rr[:], rr[:], ACT.Sigmoid).then_inc(*b_act.step("rr"))

            def b_sq3(n, p):
                after(eng, b_vec, "xc3", n)
                eng.activation(sqB, x2[:], ACT.Square).then_inc(*b_act.step("sq3"))

            def b_rstd3(n, p):
                tables(LN_EXP)
                after(eng, b_pe, "var3", n)
                rstd(b_act, "lnv3", "rstd3", n, rsB)

            def c_silu(n, m):
                after(eng, c_pe, f"w{m}", n)
                if m >= 2:
                    after(eng, c_vec, f"g{m - 2}", n)
                else:
                    after(eng, c_vec, f"g{m + 6}", n - 1)
                eng.activation(sil[:, m % 2], bank[GATE[m % 2]][:, 0:TOK], ACT.Silu,
                               scale=col("s1", m)).then_inc(*c_act.step(f"s{m}"))

            def c_gelu(n, layer, m):
                u = 8 * layer + m
                after(eng, c_pe, "k7" if layer == 1 else f"h2{m // 2}", n)
                gt_free(eng, n, u)
                eng.activation(gt[:, u % 2], bank[m // 2][:, (m % 2) * TOK:(m % 2 + 1) * TOK], ACT.Gelu,
                               scale=col("sh1" if layer == 1 else "sh2", m)).then_inc(*c_act.step(f"g{layer}{m}"))

            def d_sq(n, p):
                after(eng, d_vec, "xc", n)
                if has("A", n + 3):
                    after(eng, g_vec, "vw1", n + 3)
                eng.activation(sq4, hres[:, p], ACT.Square).then_inc(*d_act.step("sq"))

            def d_rstd(n, p):
                after(eng, d_pe, "var", n)
                rstd(d_act, "lnv", "rstd", n, rs4[:], S_A)

            def stages(n, p):
                A, B, Cc, D = has("A", n), has("B", n), has("C", n), has("D", n)
                a, b, d = (n, p), (n - 1, 1 - p), (n - 3, 1 - p)

                def silu(*tiles):
                    if Cc:
                        for m in tiles:
                            c_silu(n - 2, m)

                if A:
                    a_x(*a)
                if Cc:
                    tables(SILU)
                silu(0, 1, 2)
                if B:
                    b_prev(*b)
                    b_sq(*b)
                if D:
                    d_sq(*d)
                silu(3, 4)
                if B or D:
                    tables(LN_EXP)
                if B:
                    b_rstd(*b)
                if D:
                    d_rstd(*d)
                if Cc:
                    tables(SILU)
                silu(5)
                if A:
                    a_sq(*a)
                silu(6, 7)
                if A:
                    a_rstd(*a)
                    a_prev(*a)
                if Cc:
                    tables(GELU)
                    for m in range(8):
                        c_gelu(n - 2, 1, m)
                if A or B:
                    tables(SIGMOID)
                if A:
                    a_sig(*a)
                if B:
                    b_sig(*b)
                if A:
                    tables(LN_EXP)
                    a_exp(*a)
                if Cc:
                    tables(GELU)
                    for m in range(4):
                        c_gelu(n - 2, 2, m)
                if B:
                    b_sq3(*b)
                if Cc:
                    for m in range(4, 6):
                        c_gelu(n - 2, 2, m)
                if B:
                    b_rstd3(*b)
                if Cc:
                    tables(GELU)
                    for m in range(6, 8):
                        c_gelu(n - 2, 2, m)

            iterations(eng, stages)

        @block.vector
        def _(eng):
            k = 0

            def going(ins):
                nonlocal k
                k += 1
                ins.then_inc(su_vec, 1)

            def did(ins):
                going(ins)
                eng.wait_ge(su_vec, k)

            eng.wait_ge(ld_w, 96)
            did(eng.tensor_scalar(bmode[:, :, 0], bmode[:, :, 0], 2.0, None, ALU.mult))
            did(eng.tensor_scalar(bmode[:, :, 1], bmode[:, :, 1], -2.0, None, ALU.mult))
            assert k == BM_DONE, k
            for i, name in enumerate(("tmk", "tmv", "tmr", "cmk", "cmr")):
                a = COLS[name][0]
                did(eng.tensor_scalar(onem[:, CT * i:CT * i + CT], prm[:, a:a + CT], -1.0, 1.0, ALU.mult, ALU.add))
            a = COLS["u"][0]
            did(eng.tensor_scalar(negu[:], prm[:, a:a + CT], -1.0, None, ALU.mult))
            magic = 12582912.0
            did(eng.tensor_scalar(EN[:], EX[:], 1.4426950408889634, magic, ALU.mult, ALU.add))
            did(eng.tensor_scalar(EN[:], EN[:], magic, None, ALU.subtract))
            did(eng.tensor_scalar(EN[:], EN[:], -126.0, 127.0, ALU.max, ALU.min))
            did(eng.scalar_tensor_tensor(EX[:], EN[:], -0.693359375, EX[:], ALU.mult, ALU.add))
            did(eng.scalar_tensor_tensor(EX[:], EN[:], 2.12194440054690583e-4, EX[:], ALU.mult, ALU.add))
            did(eng.tensor_scalar(EN[:], EN[:], 127.0, None, ALU.add))
            did(eng.tensor_copy(EI[:], EN[:]))
            did(eng.tensor_scalar(EI[:], EI[:], 23, None, ALU.logical_shift_left))
            did(eng.tensor_scalar(EQ[:], EX[:], 1.0 / 5040, None, ALU.mult))
            for c in (720, 120, 24, 6, 2, 1):
                did(eng.scalar_tensor_tensor(EQ[:], EQ[:], 1.0 / c, EX[:], ALU.add, ALU.mult))
            did(eng.scalar_tensor_tensor(EX[:], EQ[:], 1.0, EI[:].bitcast(F32), ALU.add, ALU.mult))
            dt, a, b = EX[:, 0], EX[:, 1], aim[:]
            did(eng.scalar_tensor_tensor(a, a, -0.5, dt, ALU.mult, ALU.mult))
            did(eng.scalar_tensor_tensor(b, b, 0.5, dt, ALU.mult, ALU.mult))
            b2, den, num = EQ[:, 0], EQ[:, 1], EN[:, 0]
            did(eng.tensor_tensor(b2, b, b, ALU.mult))
            did(eng.tensor_scalar(EN[:, 1], a, -1.0, 1.0, ALU.mult, ALU.add))
            did(eng.tensor_tensor(den, EN[:, 1], EN[:, 1], ALU.mult))
            did(eng.tensor_tensor(den, den, b2, ALU.add))
            did(eng.scalar_tensor_tensor(num, a, 1.0, EN[:, 1], ALU.add, ALU.mult))
            did(eng.tensor_tensor(num, num, b2, ALU.subtract))
            did(eng.reciprocal(EN[:, 1], den))
            did(eng.tensor_tensor(Z[:, 0, :, 0, 0], num, EN[:, 1], ALU.mult))
            did(eng.scalar_tensor_tensor(Z[:, 1, :, 0, 0], b, 2.0, EN[:, 1], ALU.mult, ALU.mult))
            for j in range(7):
                r0, i0 = Z[:, 0, :, j // 4, j % 4], Z[:, 1, :, j // 4, j % 4]
                r1, i1 = Z[:, 0, :, (j + 1) // 4, (j + 1) % 4], Z[:, 1, :, (j + 1) // 4, (j + 1) % 4]
                going(eng.tensor_tensor(r1, r0, r0, ALU.mult))
                going(eng.tensor_tensor(num, i0, i0, ALU.mult))
                did(eng.scalar_tensor_tensor(i1, r0, 2.0, i0, ALU.mult, ALU.mult))
                did(eng.tensor_tensor(r1, r1, num, ALU.subtract))
            for i, g in enumerate((3, 0, 1, 2)):
                tg = tgs[i % 2]
                if i >= 2:
                    eng.wait_ge(put_t[i % 2], 32)
                t = tg[:].rearrange("p r q s l -> p r (q s) l")
                zg = Z[:, :, g * QG:(g + 1) * QG].rearrange("p r q s j -> p r (q s) j")
                going(eng.memset(t[:, 0, :, 0], 1.0))
                going(eng.memset(t[:, 1, :, 0], 0.0))
                did(eng.tensor_copy(t[:, :, :, 1], zg[:, :, :, 0]))
                for j in range(1, 4):
                    n = 1 << j
                    re, im = t[:, 0, :, 0:n], t[:, 1, :, 0:n]
                    zr = zg[:, 0, :, j:j + 1].broadcast_to([P, 2 * QG, n])
                    zi = zg[:, 1, :, j:j + 1].broadcast_to([P, 2 * QG, n])
                    going(eng.tensor_tensor(t[:, 0, :, n:2 * n], re, zr, ALU.mult))
                    going(eng.tensor_tensor(zt[:, 0, :, 0:n], im, zi, ALU.mult))
                    going(eng.tensor_tensor(t[:, 1, :, n:2 * n], re, zi, ALU.mult))
                    did(eng.tensor_tensor(zt[:, 1, :, 0:n], im, zr, ALU.mult))
                    going(eng.tensor_tensor(t[:, 0, :, n:2 * n], t[:, 0, :, n:2 * n], zt[:, 0, :, 0:n], ALU.subtract))
                    did(eng.tensor_tensor(t[:, 1, :, n:2 * n], t[:, 1, :, n:2 * n], zt[:, 1, :, 0:n], ALU.add))
                assert k == TG_DONE[i], (i, k)
                if i == 0:
                    did(eng.tensor_copy(pq[:, :, QC - 1], tg[:, :, QG - 1]))
            for q in range(2):
                eng.wait_ge(put_t[q], 64)
            did(eng.memset(wdec[:, :, 0], NEG_INF))
            for h in range(CT):
                did(eng.tensor_copy(half(wdec[:], h)[:, :, 1:W9], col("w", h).unsqueeze(2).broadcast_to([P, NB, NT])))
            for w in (e1, e2, kw, vw, rw, mw, sw, aw, t3):
                going(eng.memset(w[:], 0.0))
            did(eng.tensor_tensor(grid(Vr[:, 0:1]), power(QC - 1, 0, 1, 1), power(QC - 1, 0, 0, 1), ALU.mult))
            did(eng.tensor_tensor(grid(Vt[:, 0:1]), power(QC - 1, 1, 1, 1), power(QC - 1, 1, 0, 1), ALU.mult))
            did(eng.tensor_tensor(Vr[:, 0], Vr[:, 0], Vt[:, 0], ALU.subtract))
            did(eng.tensor_tensor(grid(Vi[:, 0:1]), power(QC - 1, 0, 1, 1), power(QC - 1, 1, 0, 1), ALU.mult))
            did(eng.tensor_tensor(grid(Vt[:, 0:1]), power(QC - 1, 1, 1, 1), power(QC - 1, 0, 0, 1), ALU.mult))
            did(eng.tensor_tensor(Vi[:, 0], Vi[:, 0], Vt[:, 0], ALU.add))
            assert k == V0_DONE, k
            x0 = xw[:, 1, :, NT].rearrange("p (c b) -> p c b", c=CT)
            eng.wait_ge(su_act, X0_DONE)
            did(eng.tensor_tensor(hs1[:, 0:NB], x0[:, 0], x0[:, 1], ALU.add))
            assert k == HS0_DONE, k
            eng.wait_ge(su_pe, 2)
            n0 = xn[:, :, 0:NB]
            did(eng.tensor_tensor(n0, x0, bank[S_ST][:, 0:NB].unsqueeze(1).broadcast_to([P, CT, NB]), ALU.subtract))
            assert k == XC0_DONE, k
            eng.wait_ge(su_act, SQ0_DONE)
            did(eng.tensor_tensor(hs1[:, 0:NB], sq1[:, 0, 0:NB], sq1[:, 1, 0:NB], ALU.add))
            assert k == HQ0_DONE, k
            eng.wait_ge(su_act, RS0_DONE)
            did(eng.tensor_tensor(n0, n0, rs1[:, 0:NB].unsqueeze(1).broadcast_to([P, CT, NB]), ALU.mult))
            for h in range(CT):
                did(eng.tensor_scalar(n0[:, h], n0[:, h], col("g1", h), col("b1", h), ALU.mult, ALU.add))
            assert k == XN0_DONE, k
            eng.wait_ge(su_pe, 4)
            for j, (w, tm) in enumerate(((mw, "tmk"), (aw, "tmv"), (rw, "tmr"))):
                for h in range(CT):
                    dst = half(w[:], h)[:, :, NT]
                    did(eng.tensor_scalar(dst, x0[:, h], one_minus(tm, h), None, ALU.mult))
                    at = (2 * j + h) * NB
                    did(eng.scalar_tensor_tensor(dst, bank[S_A][:, at:at + NB], col(tm, h), dst, ALU.mult, ALU.add))
            assert k == R0_DONE, k
            did(eng.memset(sw[:, :, NT], 1.0))
            eng.wait_ge(su_act, SG0_DONE)
            did(eng.scalar_tensor_tensor(x1_first[:], aw[:, :, NT], 1.0 / (1.0 + WKV_EPS), rw[:, :, NT], ALU.mult, ALU.mult))
            did(eng.tensor_tensor(x1_first[:], x1_first[:], xw[:, 1, :, NT], ALU.add))
            did(eng.tensor_copy(x1w[:, 1, :, NT], x1_first[:]))
            assert k == A0_DONE, k

            def g_re(n, g):
                V = Vr[:, 2 * g:2 * g + 2]
                if g == 0:
                    eng.wait_ge(ld_a, 16 + 32 * (n + 1))
                    after(eng, a_pe, "tok1", n - 1)
                    if isinstance(n, int) and n == 0:
                        eng.wait_ge(su_pe, 1)
                eng.tensor_tensor(grid(V), power(2 * g, 0, 1), power(2 * g, 0, 0), ALU.mult).then_inc(*g_vec.step(f"vr{g}"))
                after(eng, g_pool, f"vt{g}", n)
                after(eng, g_vec, f"vr{g}", n)
                eng.tensor_tensor(V, V, Vt[:], ALU.subtract).then_inc(*g_vec.step(f"vs{g}"))

            def g_im(n, g):
                V = Vi[:, 2 * g:2 * g + 2]
                eng.tensor_tensor(grid(V), power(2 * g, 0, 1), power(2 * g, 1, 0), ALU.mult).then_inc(*g_vec.step(f"vi{g}"))
                after(eng, g_pool, f"vu{g}", n)
                after(eng, g_vec, f"vi{g}", n)
                eng.tensor_tensor(V, V, Vt[:], ALU.add).then_inc(*g_vec.step(f"vw{g}"))

            def newton(line, n, y, t, tag="", stat=S_ST):
                eng.tensor_tensor(t, y, y, ALU.mult).then_inc(*line.step("nt" + tag))
                after(eng, line, "nt" + tag, n)
                eng.scalar_tensor_tensor(t, bank[stat][:, TOK:2 * TOK], LN_EPS, t, ALU.add,
                                         ALU.mult).then_inc(*line.step("nv" + tag))
                after(eng, line, "nv" + tag, n)
                eng.scalar_tensor_tensor(y, t, -3.0, y, ALU.add, ALU.mult).then_inc(*line.step("ny" + tag))
                after(eng, line, "ny" + tag, n)

            def a_center(n, p):
                after(eng, a_pe, "mean", n)
                after(eng, a_pe, "kvr2", n - 1)
                x = cur(xw[:, p]).rearrange("p (c b) t -> p c b t", c=CT)
                m = win1(bank[S_ST][:, 0:TOK]).unsqueeze(1).broadcast_to([P, CT, NB, NT])
                eng.tensor_tensor(xn[:].rearrange("p c (b t) -> p c b t", t=NT), x, m, ALU.subtract).then_inc(*a_vec.step("xc"))

            def a_norm(n, p):
                after(eng, a_act, "rstd", n)
                newton(a_vec, n, rs1, hs1)
                eng.scalar_tensor_tensor(xn[:], xn[:], -0.5, both(rs1), ALU.mult, ALU.mult).then_inc(*a_vec.step("xn"))
                after(eng, a_vec, "xn", n)
                for h in range(CT):
                    eng.tensor_scalar(xn[:, h], xn[:, h], col("g1", h), col("b1", h), ALU.mult,
                                      ALU.add).then_inc(*a_vec.step(f"xg{h}"))

            def a_mix(n, j):
                name, w, tm = (("k", kw, "tmk"), ("v", vw, "tmv"), ("r", rw, "tmr"))[j]
                after(eng, a_act, "rp1", n)
                after(eng, a_pe, f"kvr{j}", n)
                for h in range(CT):
                    dst = cur(half(w[:], h))
                    eng.scalar_tensor_tensor(dst, win1(bank[GATE[j % 2]][:, h * TOK:(h + 1) * TOK]), col(tm, h), dst,
                                             ALU.mult, ALU.add).then_inc(*a_vec.step(f"{name}{h}"))

            def flat(w):
                return w.rearrange("p l t -> p (l t)")

            def wkv_max(n, p):
                after(eng, a_vec, "x1", n - 1)
                eng.tensor_copy(kw[:, :, 0], mw[:, :, NT]).then_inc(*a_vec.step("mc"))
                after(eng, a_vec, "mc", n)
                eng.tensor_tensor_scan(flat(mw[:]), flat(wdec[:]), flat(kw[:]), 0.0, ALU.add, ALU.max).then_inc(*a_vec.step("m"))
                after(eng, a_vec, "m", n)
                for h in range(CT):
                    eng.scalar_tensor_tensor(cur(half(e1[:, 0], h)), prv(half(mw[:], h)), col("w", h), cur(half(mw[:], h)),
                                             ALU.add, ALU.subtract).then_inc(*a_vec.step(f"d1{h}"))
                eng.tensor_copy(e2[:, 0, :, 0], sw[:, :, NT]).then_inc(*a_vec.step("sc"))

            def wkv_sum(n, p):
                after(eng, a_act, "d2", n)
                after(eng, a_vec, "sc", n)
                eng.tensor_tensor_scan(flat(sw[:]), flat(e1[:, 0]), flat(e2[:, 0]), 0.0, ALU.mult, ALU.add).then_inc(*a_vec.step("s"))

            def wkv_bb(n, p):
                after(eng, a_act, "lns", n)
                eng.tensor_tensor(t3[:], t3[:], mw[:], ALU.add).then_inc(*a_vec.step("bb"))
                after(eng, a_vec, "bb", n)
                for i, (name, s) in enumerate((("dl", lambda h: col("w", h)), ("gm", lambda h: negu[:, h:h + 1]))):
                    for h in range(CT):
                        eng.scalar_tensor_tensor(cur(half(e1[:, i], h)), prv(half(t3[:], h)), s(h), cur(half(kw[:], h)),
                                                 ALU.add, ALU.subtract).then_inc(*a_vec.step(f"{name}{h}"))
                after(eng, a_vec, "gm1", n)
                eng.tensor_scalar(cur(e2[:]), cur(e1[:]), 0.0, None, ALU.max).then_inc(*a_vec.step("mn"))
                after(eng, a_vec, "mn", n)
                eng.tensor_scalar(cur(e1[:]), cur(e1[:]), 0.0, None, ALU.min).then_inc(*a_vec.step("mx"))

            def wkv_aa(n, p):
                after(eng, a_act, "ef2", n)
                eng.tensor_tensor(cur(e2[:, 0]), cur(e2[:, 0]), cur(vw[:]), ALU.mult).then_inc(*a_vec.step("ev"))
                eng.tensor_copy(e2[:, 0, :, 0], aw[:, :, NT]).then_inc(*a_vec.step("ac"))
                after(eng, a_vec, "ac", n)
                eng.tensor_tensor_scan(flat(aw[:]), flat(e1[:, 0]), flat(e2[:, 0]), 0.0, ALU.mult, ALU.add).then_inc(*a_vec.step("aa"))
                eng.scalar_tensor_tensor(cur(t3[:]), cur(e1[:, 1]), WKV_EPS, cur(e2[:, 1]), ALU.add, ALU.add).then_inc(*a_vec.step("den"))

            def wkv_num1(n, p):
                after(eng, a_vec, "den", n)
                eng.tensor_tensor(cur(e1[:, 1]), cur(e1[:, 1]), prv(aw[:]), ALU.mult).then_inc(*a_vec.step("n1"))

            def wkv_num2(n, p):
                eng.tensor_tensor(cur(e2[:, 1]), cur(e2[:, 1]), cur(vw[:]), ALU.mult).then_inc(*a_vec.step("n2"))
                after(eng, a_vec, "n2", n)
                eng.tensor_tensor(cur(e1[:, 1]), cur(e1[:, 1]), cur(e2[:, 1]), ALU.add).then_inc(*a_vec.step("n3"))

            def wkv_rec(n, h):
                after(eng, a_vec, "den", n)
                w = cur(half(t3[:], h))
                eng.reciprocal(w, w).then_inc(*a_vec.step(f"rec{h}"))

            def wkv_out(n, p):
                after(eng, a_vec, "rec1", n)
                eng.tensor_tensor(cur(e1[:, 1]), cur(e1[:, 1]), cur(t3[:]), ALU.mult).then_inc(*a_vec.step("y"))

            def wkv_res(n, p):
                after(eng, a_act, "sig", n)
                after(eng, a_vec, "y", n)
                eng.tensor_tensor(cur(e1[:, 1]), cur(e1[:, 1]), cur(rw[:]), ALU.mult).then_inc(*a_vec.step("ry"))
                after(eng, a_vec, "ry", n)
                after(eng, b_pool, "xx", n - 2)
                after(eng, b_act, "rp1", n - 2)
                after(eng, a_vec, "x1s", n - 1)
                eng.tensor_tensor(cur(x1w[:, p]), cur(e1[:, 1]), cur(xw[:, p]), ALU.add).then_inc(*a_vec.step("x1"))
                eng.tensor_copy(x1w[:, p, :, 0], x1w[:, 1 - p, :, NT]).then_inc(*a_vec.step("x1s"))

            def b_center(n, p):
                after(eng, b_pe, "mean", n)
                after(eng, b_pe, "cm3", n - 1)
                x = cur(x1w[:, p]).rearrange("p (c b) t -> p c b t", c=CT)
                m = win1(bank[S_ST][:, 0:TOK]).unsqueeze(1).broadcast_to([P, CT, NB, NT])
                eng.tensor_tensor(xn2[:].rearrange("p c (b t) -> p c b t", t=NT), x, m, ALU.subtract).then_inc(*b_vec.step("xc"))

            def b_norm(n, p):
                after(eng, b_act, "rstd", n)
                newton(b_vec, n, rsB, hsB)
                eng.scalar_tensor_tensor(xn2[:], xn2[:], -0.5, both(rsB), ALU.mult, ALU.mult).then_inc(*b_vec.step("xn"))
                after(eng, b_vec, "xn", n)
                for h in range(CT):
                    eng.tensor_scalar(xn2[:, h], xn2[:, h], col("g2", h), col("b2", h), ALU.mult,
                                      ALU.add).then_inc(*b_vec.step(f"xg{h}"))
                after(eng, b_vec, "xg1", n)
                after(eng, b_act, "rp1", n)
                for h in range(CT):
                    eng.scalar_tensor_tensor(rr[:, h], xn2[:, h], col("cmr", h), rr[:, h], ALU.mult,
                                             ALU.add).then_inc(*b_vec.step(f"r{h}"))

            def b_relu(n, i):
                after(eng, b_pe, f"cm{i}", n)
                if i >= 2:
                    after(eng, b_pe, f"cp{i - 2}", n)
                for h in range(CT):
                    eng.scalar_tensor_tensor(kk[:, i % 2, h], bank[S_A][:, h * TOK:(h + 1) * TOK], col("cmk", h), xpc[:, h],
                                             ALU.mult, ALU.add).then_inc(*b_vec.step(f"k{2 * i + h}"))
                after(eng, b_vec, f"k{2 * i + 1}", n)
                eng.scalar_tensor_tensor(kk[:, i % 2], kk[:, i % 2], 0.0, kk[:, i % 2], ALU.max,
                                         ALU.mult).then_inc(*b_vec.step(f"q{i}"))

            def b_res(n, p):
                after(eng, b_pe, "cp3", n)
                after(eng, b_act, "rr", n)
                eng.tensor_tensor(rr[:], bank[S_CP][:].rearrange("p (c n) -> p c n", c=CT), rr[:], ALU.mult).then_inc(*b_vec.step("rv"))
                after(eng, b_pool, "xx", n)
                after(eng, b_vec, "rv", n)
                eng.tensor_tensor(x2[:], x2[:], rr[:], ALU.add).then_inc(*b_vec.step("x2"))

            def b_center3(n, p):
                after(eng, b_pe, "mean3", n)
                after(eng, b_pool, "sum3", n)
                eng.tensor_tensor(x2[:], x2[:], both(bank[S_ST][:, 0:TOK]), ALU.subtract).then_inc(*b_vec.step("xc3"))

            def b_out(n, p):
                after(eng, b_act, "rstd3", n)
                newton(b_vec, n, rsB, hsB, "3")
                if not (isinstance(n, int) and n < 2):
                    eng.wait_ge(put_o[p], 8 * (n - p))
                eng.scalar_tensor_tensor(hres[:, p], x2[:], -0.5, both(rsB), ALU.mult, ALU.mult).then_inc(*b_vec.step("h"))
                after(eng, b_vec, "h", n)
                after(eng, c_pe, "w7", n - 1)
                eng.tensor_copy(hx[:, 0], hres[:, p]).then_inc(*b_vec.step("hi"))
                after(eng, b_vec, "hi", n)
                eng.tensor_tensor(hx[:, 1], hres[:, p], hx[:, 0], ALU.subtract).then_inc(*b_vec.step("lo"))

            def c_gate(n, m):
                after(eng, c_act, f"s{m}", n)
                gt_free(eng, n, m)
                eng.scalar_tensor_tensor(gt[:, m % 2], bank[GATE[m % 2]][:, TOK:2 * TOK], col("s2", m), sil[:, m % 2],
                                         ALU.mult, ALU.mult).then_inc(*c_vec.step(f"g{m}"))
                after(eng, c_vec, f"g{m}", n)
                c_high(n, m)

            def c_high(n, u):
                m = u % 8
                if 8 <= u < 16:
                    after(eng, c_act, f"g1{m}", n)
                    after(eng, c_pe, "h23", n - 1)
                elif u >= 16:
                    after(eng, c_act, f"g2{m}", n)
                    after(eng, c_pe, f"y{m - 3}" if m >= 3 else "k7", n)
                elif m >= 3:
                    after(eng, c_pe, f"k{m - 3}", n)
                else:
                    after(eng, c_pe, "y7", n - 1)
                eng.tensor_copy(split_to(u, 0), gt[:, u % 2]).then_inc(*c_vec.step(f"i{u}"))

            def c_res(n, p):
                after(eng, c_pe, "y7", n)
                for h in range(CT):
                    eng.scalar_tensor_tensor(hres[:, p, h], bank[S_G][:, h * TOK:(h + 1) * TOK], col("s3", h), hres[:, p, h],
                                             ALU.mult, ALU.add).then_inc(*c_vec.step(f"y{h}"))

            def d_center(n, p):
                after(eng, d_pe, "mean", n)
                eng.tensor_tensor(hres[:, p], hres[:, p], both(bank[S_A][:, 0:TOK]), ALU.subtract).then_inc(*d_vec.step("xc"))

            def d_out(n, p):
                after(eng, d_act, "rstd", n)
                newton(d_vec, n, rs4[:], hs4[:], stat=S_A)
                eng.scalar_tensor_tensor(hres[:, p], hres[:, p], -0.5, both(rs4[:]), ALU.mult,
                                         ALU.mult).then_inc(*d_vec.step("o"))

            def set_flag():
                eng.wait_ge(w_nz, NPIECE)
                eng.tensor_reduce(flag[:, NPIECE:NPIECE + 1], flag[:, 0:NPIECE], mybir.AxisListType.X,
                                  ALU.max).then_inc(w_nz, 1)
                eng.wait_ge(w_nz, NPIECE + 1)
                eng.tensor_scalar(flag[:, NPIECE:NPIECE + 1], flag[:, NPIECE:NPIECE + 1], 0.0, None,
                                  ALU.not_equal).then_inc(w_nz, 1)
                eng.wait_ge(fl_sum, 1)
                eng.tensor_scalar(flag[:, NPIECE + 1:], bank[S_G][:, 0:1], 0.0, None, ALU.not_equal).then_inc(w_nz, 1)
                eng.wait_ge(w_nz, NPIECE + 3)
                eng.tensor_copy(flag_i[:], flag[:, NPIECE + 1:]).then_inc(fl_set, 1)

            for g in range(2):
                g_re(0, g)
                g_im(0, g)

            def stages(n, p):
                nonlocal k
                A, B, Cc, D = has("A", n), has("B", n), has("C", n), has("D", n)
                a, b, c, d = (n, p), (n - 1, 1 - p), (n - 2, p), (n - 3, 1 - p)

                def gates(*tiles):
                    if Cc:
                        for m in tiles:
                            c_gate(n - 2, m)

                def highs(*tiles):
                    if Cc:
                        for u in tiles:
                            c_high(n - 2, u)

                gates(0)
                if B:
                    wkv_res(*b)
                if isinstance(n, int) and n == CH:
                    after(eng, a_vec, "x1s", CH - 1)
                    did(eng.tensor_copy(x1w[:, 1, :, NT], x1_first[:]))
                    assert k == X1_FIXED
                gates(1, 2)
                if B:
                    b_center(*b)
                if D:
                    d_center(*d)
                gates(3, 4)
                if B:
                    b_norm(*b)
                gates(5)
                if A:
                    a_center(*a)
                gates(6)
                if D:
                    d_out(*d)
                gates(7)
                if A:
                    a_norm(*a)
                if B:
                    b_relu(n - 1, 0)
                if A and more(n):
                    g_re(n + 1, 0)
                if A:
                    a_mix(n, 0)
                highs(8, 9)
                if A and more(n):
                    g_im(n + 1, 0)
                if A:
                    a_mix(n, 1)
                highs(10, 11)
                if A:
                    a_mix(n, 2)
                highs(12, 13, 14, 15)
                if A:
                    wkv_max(*a)
                if B:
                    b_relu(n - 1, 1)
                if A and more(n):
                    g_re(n + 1, 1)
                if A:
                    wkv_sum(*a)
                if B:
                    b_relu(n - 1, 2)
                if A:
                    wkv_bb(*a)
                if B:
                    b_relu(n - 1, 3)
                if A:
                    wkv_aa(*a)
                highs(16, 17)
                if B:
                    b_res(*b)
                if A and more(n):
                    g_im(n + 1, 1)
                highs(18)
                if A:
                    wkv_num1(*a)
                if B:
                    b_center3(*b)
                if A:
                    wkv_num2(*a)
                highs(19)
                highs(20, 21)
                if A:
                    wkv_rec(n, 0)
                if B:
                    b_out(*b)
                highs(22, 23)
                if A:
                    wkv_rec(n, 1)
                if Cc:
                    c_res(*c)
                if A:
                    wkv_out(*a)
                if isinstance(n, int) and n == 1:
                    set_flag()

            iterations(eng, stages)

        @block.tensor
        def _(eng):
            def mm(out_, w, x, start, stop, **kws):
                return eng.matmul(out_, w, x, start=start, stop=stop, **kws)

            eng.wait_ge(su_vec, V0_DONE)
            eng.wait_ge(su_pool, BD0_DONE)
            for h in range(CT):
                s = slice(h * P, (h + 1) * P)
                mm(bank[S_A][:, 64 * h:64 * h + 64], Vr[:, 0, s], bd[:, 0, 0], True, False)
                last = mm(bank[S_A][:, 64 * h:64 * h + 64], Vi[:, 0, s], bd[:, 0, 1], False, True)
            last.then_inc(su_pe, 1)
            eng.wait_ge(su_vec, HS0_DONE)
            mm(bank[S_ST][:, 0:NB], mean_w[:], hs1[:, 0:NB], True, True).then_inc(su_pe, 1)
            eng.wait_ge(su_vec, HQ0_DONE)
            mm(bank[S_ST][:, TOK:TOK + NB], mean_w[:], hs1[:, 0:NB], True, True).then_inc(su_pe, 1)
            eng.wait_ge(su_vec, XN0_DONE)
            eng.wait_ge(ld_tm, 16)
            for o in range(6):
                for c in range(CT):
                    last = mm(bank[S_A][:, o * NB:(o + 1) * NB], W_tm[:, c, o * P:(o + 1) * P], xn[:, c, 0:NB],
                              c == 0, c == CT - 1)
            last.then_inc(su_pe, 1)

            def a_tok(n, g):
                if g == 0:
                    if isinstance(n, int) and n == 0:
                        eng.wait_ge(su_vec, A0_DONE)
                    after(eng, g_pool, "bd3", n)
                    after(eng, a_act, "x", n - 1)
                    after(eng, b_vec, "k7", n - 2)
                after(eng, g_vec, f"vw{g}", n)
                for h in range(CT):
                    for q in range(2):
                        at = h * TOK + (2 * g + q) * 2 * NB
                        s = slice(h * P, (h + 1) * P)
                        mm(bank[S_A][:, at:at + 2 * NB], Vr[:, 2 * g + q, s], bd[:, 2 * g + q, 0], True, False)
                        last = mm(bank[S_A][:, at:at + 2 * NB], Vi[:, 2 * g + q, s], bd[:, 2 * g + q, 1], False, True)
                last.then_inc(*a_pe.step(f"tok{g}"))

            def mean(x, stat=S_ST):
                return mm(bank[stat][:, 0:TOK], mean_w[:], x, True, True)

            def var(x, stat=S_ST):
                return mm(bank[stat][:, TOK:2 * TOK], mean_w[:], x, True, True)

            def b_mean(n, p):
                after(eng, b_pool, "sum", n)
                after(eng, b_vec, "nv3", n - 1)
                if isinstance(n, int) and n == 0:
                    after(eng, a_vec, "nv", 0)
                mean(hsB).then_inc(*b_pe.step("mean"))

            def b_var(n, p):
                after(eng, b_pool, "sum_sq", n)
                var(hsB).then_inc(*b_pe.step("var"))

            def a_mean(n, p):
                after(eng, a_pool, "sum", n)
                after(eng, b_vec, "nv", n - 1)
                mean(hs1).then_inc(*a_pe.step("mean"))

            def a_var(n, p):
                after(eng, a_pool, "sum_sq", n)
                var(hs1).then_inc(*a_pe.step("var"))

            def d_mean(n, p):
                after(eng, d_pool, "sum", n)
                if has("A", n + 3):
                    after(eng, a_act, "x", n + 3)
                if has("B", n + 2):
                    after(eng, b_vec, "k7", n + 1)
                mean(hs4[:], S_A).then_inc(*d_pe.step("mean"))

            def d_var(n, p):
                after(eng, d_pool, "sum_sq", n)
                var(hs4[:], S_A).then_inc(*d_pe.step("var"))

            def b_mean3(n, p):
                after(eng, b_pool, "sum3", n)
                if has("A", n + 1):
                    after(eng, a_vec, "nv", n + 1)
                else:
                    after(eng, b_vec, "nv", n)
                mean(hsB).then_inc(*b_pe.step("mean3"))

            def b_var3(n, p):
                after(eng, b_pool, "sum_sq3", n)
                var(hsB).then_inc(*b_pe.step("var3"))

            def a_kvr(n, p, j):
                if j == 0:
                    after(eng, a_vec, "xg1", n)
                if j < 2:
                    after(eng, c_vec, f"g{6 + j}", n - 2)
                    after(eng, a_vec, ("r1", "v1")[j], n - 1)
                else:
                    after(eng, a_vec, "k1", n)
                for h in range(CT):
                    o = CT * j + h
                    for c in range(CT):
                        last = mm(bank[GATE[j % 2]][:, h * TOK:(h + 1) * TOK], W_tm[:, c, o * P:(o + 1) * P], xn[:, c],
                                  c == 0, c == CT - 1)
                last.then_inc(*a_pe.step(f"kvr{j}"))

            def b_cm(n, i):
                if i == 0:
                    after(eng, b_vec, "xg1", n)
                    if has("A", n + 1):
                        after(eng, a_act, "x", n + 1)
                    after(eng, d_vec, "nv", n - 2)
                    after(eng, b_vec, "k7", n - 1)
                else:
                    after(eng, b_vec, f"k{2 * i - 1}", n)
                eng.wait_ge(ld_s[i % 2], 32 * n + 16 * (i // 2 + 1))
                for h in range(2):
                    for c in range(CT):
                        last = mm(bank[S_A][:, h * TOK:(h + 1) * TOK], wcs[:, i % 2, h, c * P:(c + 1) * P], xn2[:, c],
                                  c == 0, c == CT - 1)
                last.then_inc(*b_pe.step(f"cm{i}"))

            def b_cp(n, i):
                after(eng, b_vec, f"q{i}", n)
                if i == 0:
                    after(eng, b_vec, "rv", n - 1)
                    if has("A", n + 1):
                        after(eng, a_vec, "r1", n + 1)
                    else:
                        after(eng, c_vec, "g6", n - 1)
                for j in range(2):
                    for h in range(CT):
                        first = i == 0 and j == 0
                        last = mm(bank[S_CP][:, h * TOK:(h + 1) * TOK], wcs[:, i % 2, j, C + h * P:C + (h + 1) * P],
                                  kk[:, i % 2, j], first and h == 0, i == 3 and j == 1, skip_group_check=True)
                last.then_inc(*b_pe.step(f"cp{i}"))

            def low(n, step, j, todo):
                pos = low_at[step] + j
                eng.wait_ge(lo_in, 16 * (NLO * n + pos + 1))
                for o, w, x in todo:
                    last = mm(o, w, x, False, False, skip_group_check=True)
                last.then_inc(lo_used, 1)

            def c_w(n, m):
                if m == 0:
                    after(eng, b_vec, "lo", n)
                elif m == 1:
                    after(eng, c_vec, "y1", n - 1)
                else:
                    after(eng, c_vec, f"g{m - 2}", n)
                gate = bank[GATE[m % 2]]
                todo = [(gate[:, j * TOK:(j + 1) * TOK], w[:, c, m * P:(m + 1) * P], hx[:, part, c])
                        for j, w in enumerate((W_1, W_2)) for c in range(CT) for part in range(2)]
                for i, (o, w, x) in enumerate(todo[:-1]):
                    mm(o, w, x, i == 0, False, skip_group_check=True)
                with eng.If(flag_reg):
                    for c in range(CT):
                        low(n, f"w{m}", c, [(gate[:, j * TOK:(j + 1) * TOK], lo_w[:, j * P:(j + 1) * P], hx[:, part, c])
                                            for j in range(2) for part in range(2)])
                mm(*todo[-1], False, True, skip_group_check=True).then_inc(*c_pe.step(f"w{m}"))

            def c_k(n, m):
                after(eng, c_pool, f"l{m}", n)
                if m == 0:
                    after(eng, c_act, "g27", n - 1)
                todo = [(bank[o // 2][:, (o % 2) * TOK:(o % 2 + 1) * TOK], W_h1[:, m, o * P:(o + 1) * P], ha[:, m % 3, part],
                         m == 0 and o % 2 == 0 and part == 0)
                        for o in range(FT) for part in range(2)]
                for o, w, x, start in todo[:-1]:
                    mm(o, w, x, start, m == 7, skip_group_check=True)
                with eng.If(flag_reg):
                    for i in range(4):
                        low(n, f"k{m}", i, [(bank[i][:, j * TOK:(j + 1) * TOK], lo_w[:, j * P:(j + 1) * P], ha[:, m % 3, part])
                                            for j in range(2) for part in range(2)])
                o, w, x, _ = todo[-1]
                mm(o, w, x, False, m == 7, skip_group_check=True).then_inc(*c_pe.step(f"k{m}"))

            def c_h(n, i, between=None):
                after(eng, c_act, f"g1{2 * i + 1}", n)
                todo = [(bank[i][:, j * TOK:(j + 1) * TOK], W_h2[:, c, (2 * i + j) * P:(2 * i + j + 1) * P], hb[:, part, c], c)
                        for j in range(2) for c in range(FT) for part in range(2)]
                for q, (o, w, x, c) in enumerate(todo[:-1]):
                    if i == 0 and q < 2 * FT and q % 2 == 0:
                        after(eng, c_pool, f"l{8 + c}", n)
                    if q == 2 * FT and between:
                        between()
                    mm(o, w, x, q == 0, False, skip_group_check=True)
                with eng.If(flag_reg):
                    for c in range(FT):
                        low(n, f"h2{i}", c, [(bank[i][:, j * TOK:(j + 1) * TOK], lo_w[:, j * P:(j + 1) * P], hb[:, part, c])
                                             for j in range(2) for part in range(2)])
                o, w, x, _ = todo[-1]
                mm(o, w, x, False, True, skip_group_check=True).then_inc(*c_pe.step(f"h2{i}"))

            def c_y(n, m):
                after(eng, c_pool, f"l{16 + m}", n)
                todo = [(bank[S_G][:, h * TOK:(h + 1) * TOK], W_3[:, m, h * P:(h + 1) * P], ha[:, m % 3, part])
                        for h in range(CT) for part in range(2)]
                if m == 0:
                    if has("A", n + 2):
                        after(eng, a_vec, "v1", n + 2)
                    else:
                        after(eng, c_vec, "g7", n)
                for i, (o, w, x) in enumerate(todo[:-1]):
                    mm(o, w, x, m == 0 and i == 0, m == 7, skip_group_check=True)
                with eng.If(flag_reg):
                    low(n, f"y{m}", 0, [(bank[S_G][:, h * TOK:(h + 1) * TOK], lo_w[:, h * P:(h + 1) * P], ha[:, m % 3, part])
                                        for h in range(CT) for part in range(2)])
                mm(*todo[-1], False, m == 7, skip_group_check=True).then_inc(*c_pe.step(f"y{m}"))

            flag_reg = None

            def stages(n, p):
                nonlocal flag_reg
                A, B, Cc, D = has("A", n), has("B", n), has("C", n), has("D", n)
                a, b, d = (n, p), (n - 1, 1 - p), (n - 3, 1 - p)
                if isinstance(n, int) and n == 2:
                    after(eng, a_vec, "v1", 1)
                    eng.wait_ge(w_nz, NPIECE + 2)
                    mm(bank[S_G][:, 0:1], mean_w[:], flag[:, NPIECE:NPIECE + 1], True, True).then_inc(fl_sum, 1)
                    eng.wait_ge(fl_set, 1)
                    flag_reg = eng.value_load(flag_i[0:1, 0:1], min_val=0, max_val=1)
                def ffn(*steps):
                    if Cc:
                        for step in steps:
                            {"w": c_w, "k": c_k, "h": c_h, "y": c_y}[step[0]](n - 2, int(step[1]))

                ffn("w0", "w1", "w2", "k0")
                if B:
                    b_mean(*b)
                if D:
                    d_mean(*d)
                ffn("w3", "k1", "w4")
                if B:
                    b_var(*b)
                ffn("k2")
                if D:
                    d_var(*d)
                ffn("w5", "k3")
                if A:
                    a_mean(*a)
                ffn("w6", "k4", "w7", "k5")
                if A:
                    a_var(*a)
                ffn("k6")
                if B:
                    b_cm(n - 1, 0)
                ffn("k7")
                if A:
                    a_kvr(*a, 0)
                if A:
                    a_kvr(*a, 1)
                    a_kvr(*a, 2)
                if B:
                    b_cm(n - 1, 1)
                    b_cp(n - 1, 0)
                ffn("h0")
                if B:
                    b_cm(n - 1, 2)
                    b_cp(n - 1, 1)
                ffn("h1")
                if B:
                    b_cm(n - 1, 3)
                    b_cp(n - 1, 2)
                    b_cp(n - 1, 3)
                ffn("h2")
                if B:
                    b_mean3(*b)
                ffn("y0", "y1", "y2")
                if Cc:
                    c_h(n - 2, 3, (lambda: b_var3(*b)) if B else None)
                elif B:
                    b_var3(*b)
                ffn("y3", "y4", "y5")
                if A and more(n):
                    a_tok(n + 1, 0)
                    a_tok(n + 1, 1)
                ffn("y6", "y7")

            a_tok(0, 0)
            a_tok(0, 1)
            iterations(eng, stages)


BM_DONE = 2
CB0_DONE = 6
BD0_DONE = 8
X0_DONE, SQ0_DONE, RS0_DONE, SG0_DONE = 1, 2, 4, 5
_Z = BM_DONE + 5 + 1 + 9 + 6 + 1 + 11 + 28
TG_DONE = [_Z + 21, _Z + 43, _Z + 64, _Z + 85]
V0_DONE = TG_DONE[3] + 3 + 9 + 6
HS0_DONE = V0_DONE + 1
XC0_DONE = HS0_DONE + 1
HQ0_DONE = XC0_DONE + 1
XN0_DONE = HQ0_DONE + 3
R0_DONE = XN0_DONE + 12
A0_DONE = R0_DONE + 4
X1_FIXED = A0_DONE + 1


def kernel(**inputs):
    import numpy as np
    import concourse.bacc as bacc
    from concourse.bass_utils import run_bass_kernel_spmd

    a = {k: np.asarray(v) for k, v in inputs.items()}

    def turned(v, axis):
        return np.roll(v, -1, axis=axis)

    def modes(v):
        v = turned(v, 0).reshape(QP, 2, NS, -1)
        return np.ascontiguousarray(v.transpose(1, 2, 0, 3).reshape(P, QP, -1))

    def tiles(w):
        return np.ascontiguousarray(w.reshape(-1, P, w.shape[1]).transpose(1, 0, 2))

    x = turned(a["x"], 1).reshape(NB, CH, QC, 2, NS, 2)
    c_in = np.ascontiguousarray(x.transpose(1, 3, 4, 2, 5, 0).reshape(CH, P, QC * 2 * NB))
    cols = {"w": "attn_time_decay", "u": "attn_time_first", "tmk": "attn_tmk", "tmv": "attn_tmv", "tmr": "attn_tmr",
            "g1": "attn_g1", "b1": "attn_b1", "g2": "attn_g2", "b2": "attn_b2", "cmk": "attn_cmk", "cmr": "attn_cmr",
            "s1": "ffn_w1_s", "s2": "ffn_w2_s", "sh1": "ffn_h1_s", "sh2": "ffn_h2_s", "s3": "ffn_w3_s"}
    cm = a["L0_attn_W_cm"].reshape(CT, P, FT, P).transpose(2, 1, 0, 3).reshape(FT, P, C)
    cp = a["L0_attn_W_cp"].reshape(FT, P, C)
    w_cs = np.ascontiguousarray(np.concatenate([cm, cp], axis=2).reshape(4, 2, P, 2 * C).transpose(0, 2, 1, 3)
                                .reshape(4, P, 4 * C))
    par = np.ascontiguousarray(np.concatenate([a["L0_" + cols[k]].reshape(-1, P).T for k in COLS], axis=1))
    arrays = {
        "c_in": c_in,
        "log_dt": np.ascontiguousarray(turned(a["L0_tok_log_dt"], 0).reshape(QP, 2).T),
        "a_re": modes(a["L0_tok_inv_A_real"])[:, :, 0].copy(),
        "a_im": modes(a["L0_tok_A_imag"])[:, :, 0].copy(),
        "b_ri": modes(a["L0_tok_B_ri"]),
        "par": par,
        "w_tm": tiles(a["L0_attn_W_tm"]),
        "w_cs": w_cs,
        "w1": tiles(a["L0_ffn_w1_w"].T),
        "w2": tiles(a["L0_ffn_w2_w"].T),
        "h1": tiles(a["L0_ffn_h1_w"].T),
        "h2": tiles(a["L0_ffn_h2_w"].T),
        "w3": tiles(a["L0_ffn_w3_w"].T),
    }
    nc = bacc.Bacc("TRN2", target_bir_lowering=False, num_devices=1)
    args = [nc.dram_tensor(k, v.shape, F32, kind="ExternalInput").ap() for k, v in arrays.items()]
    args.append(nc.dram_tensor("out", (CH, P, CT * TOK), F32, kind="ExternalOutput").ap())
    args.append(nc.dram_tensor("tpq", (CH, P, 2 * HX), F32, kind="Internal").ap())
    args.append(nc.dram_tensor("wlo", (NLO, P, C), F32, kind="Internal").ap())
    build(nc, *args)
    got = run_bass_kernel_spmd(nc, [arrays], core_ids=[0]).results[0]["out"]
    got = np.asarray(got).reshape(CH, P, CT, NB, NT).transpose(3, 0, 4, 2, 1).reshape(NB, T, C)
    return np.ascontiguousarray(np.roll(got, 1, axis=1))
```
